# Optimizing a Trainium2 kernel written in Bass

```python
import numpy as np
import jax
import jax.numpy as jnp

def _softmax(x, axis=-1):
    return jax.nn.softmax(x, axis=axis)

def _gelu(x):
    return jax.nn.gelu(x, approximate=True)

def _silu(x):
    return jax.nn.silu(x)

def _sigmoid(x):
    return jax.nn.sigmoid(x)

def _layernorm(x, axis=-1, eps=1e-05):
    m = jnp.mean(x, axis=axis, keepdims=True)
    v = jnp.var(x, axis=axis, keepdims=True)
    return (x - m) / jnp.sqrt(v + eps)

def _scatter_add(tgt, idx, src, axis=0):
    return tgt.at[idx].add(src)

def _segment_sum(src, seg, n):
    return jax.ops.segment_sum(src, seg, n)
kernel_name = 'mk_prb_d2_jaxref_r4_4deb91'

def setup_inputs(seed: int=0):
    np.random.seed(seed)
    _w = jnp.asarray

    def _L0_attn_setup():
        import jax, jax.numpy as jnp
        import numpy as np
        B, T, C, H = (2, 512, 256, 16)
        key = jax.random.key(seed)
        ks = jax.random.split(key, 6)
        x = jax.random.normal(ks[0], (B, T, C), dtype=jnp.float32)
        wq = jax.random.normal(ks[1], (C, H * 3), dtype=jnp.float32) * C ** (-0.5)
        wk = jax.random.normal(ks[2], (C, H * 3), dtype=jnp.float32) * C ** (-0.5)
        wv = jax.random.normal(ks[3], (C, C), dtype=jnp.float32) * C ** (-0.5)
        wo = jax.random.normal(ks[4], (C, C), dtype=jnp.float32) * C ** (-0.5)
        dirs = jax.random.normal(ks[5], (H, 3), dtype=jnp.float32)
        head_dirs = dirs / jnp.linalg.norm(dirs, axis=1, keepdims=True)
        scale = jnp.full((1,), 1.0 / np.sqrt(3.0), dtype=jnp.float32)
        return {'x': x, 'wq': wq, 'wk': wk, 'wv': wv, 'wo': wo, 'head_dirs': head_dirs, 'scale': scale}
    _L0_attn_in = _L0_attn_setup()

    def _L0_ffn_setup():
        import jax, jax.numpy as jnp
        import numpy as np
        EPS_LN = 1e-05
        EPS_GATE = 1e-08

        def layer_norm(x, gamma, beta):
            mu = jnp.mean(x, axis=-1, keepdims=True)
            var = jnp.mean(jnp.square(x - mu), axis=-1, keepdims=True)
            return (x - mu) * jax.lax.rsqrt(var + EPS_LN) * gamma + beta
        key = jax.random.key(seed)
        ks = jax.random.split(key, 8)
        B, S, D, E, H = (4, 1024, 256, 4, 512)
        s_in = 1.0 / np.sqrt(D)
        s_h = 1.0 / np.sqrt(H)
        return {'h': jax.random.normal(ks[0], (B, S, D), dtype=jnp.float32), 'router_w': jax.random.uniform(ks[1], (E, D), jnp.float32, -s_in, s_in), 'rn_g': jnp.ones((D,), jnp.float32), 'rn_b': jnp.zeros((D,), jnp.float32), 'w1': jax.random.uniform(ks[2], (E, D, H), jnp.float32, -s_in, s_in), 'ln_g': jnp.ones((E, H), jnp.float32), 'ln_b': jnp.zeros((E, H), jnp.float32), 'w2': jax.random.uniform(ks[3], (E, H, D), jnp.float32, -s_h, s_h), 'on_g': jnp.ones((D,), jnp.float32), 'on_b': jnp.zeros((D,), jnp.float32)}
    _L0_ffn_in = _L0_ffn_setup()

    def _L1_attn_setup():
        import math
        import jax, jax.numpy as jnp
        import numpy as np
        N_EMBD = 256
        N_HEAD = 16
        B, T = (2, 512)

        def _heads(t):
            b, s, d = t.shape
            return t.reshape(b, s, N_HEAD, d // N_HEAD).transpose(0, 2, 1, 3)
        key = jax.random.key(seed)
        ks = jax.random.split(key, 7)
        D = N_EMBD
        s = 0.02
        return {'x': jax.random.normal(ks[0], (B, T, D), dtype=jnp.float32), 'w_attn': jax.random.normal(ks[1], (2 * D, D), dtype=jnp.float32) * s, 'b_attn': jnp.zeros((2 * D,), dtype=jnp.float32), 'w_k2': jax.random.normal(ks[2], (D, D), dtype=jnp.float32) * s, 'b_k2': jnp.zeros((D,), dtype=jnp.float32), 'w_proj': jax.random.normal(ks[3], (D, D), dtype=jnp.float32) * s, 'b_proj': jnp.zeros((D,), dtype=jnp.float32)}
    _L1_attn_in = _L1_attn_setup()

    def _L1_ffn_setup():
        import jax, jax.numpy as jnp
        import numpy as np
        TOP_K = 2
        NUM_EXPERTS = 8
        key = jax.random.key(seed)
        ks = jax.random.split(key, 8)
        h, d, ds, E = (256, 128, 256, NUM_EXPERTS)
        s = 1.0 / np.sqrt(h)
        return {'x': jax.random.normal(ks[0], (2, 512, h), jnp.float32), 'router': jax.random.normal(ks[1], (h, E), jnp.float32) * s, 'experts_gate': jax.random.normal(ks[2], (E, h, d), jnp.float32) * s, 'experts_up': jax.random.normal(ks[3], (E, h, d), jnp.float32) * s, 'experts_down': jax.random.normal(ks[4], (E, d, h), jnp.float32) * (1.0 / np.sqrt(d)), 'shared_gate': jax.random.normal(ks[5], (h, ds), jnp.float32) * s, 'shared_up': jax.random.normal(ks[6], (h, ds), jnp.float32) * s, 'shared_down': jax.random.normal(ks[7], (ds, h), jnp.float32) * (1.0 / np.sqrt(ds))}
    _L1_ffn_in = _L1_ffn_setup()
    _d = {'L0_attn_x': _L0_attn_in['x'], 'L0_attn_wq': _L0_attn_in['wq'], 'L0_attn_wk': _L0_attn_in['wk'], 'L0_attn_wv': _L0_attn_in['wv'], 'L0_attn_wo': _L0_attn_in['wo'], 'L0_attn_head_dirs': _L0_attn_in['head_dirs'], 'L0_attn_scale': _L0_attn_in['scale'], 'L0_ffn_router_w': _L0_ffn_in['router_w'], 'L0_ffn_rn_g': _L0_ffn_in['rn_g'], 'L0_ffn_rn_b': _L0_ffn_in['rn_b'], 'L0_ffn_w1': _L0_ffn_in['w1'], 'L0_ffn_ln_g': _L0_ffn_in['ln_g'], 'L0_ffn_ln_b': _L0_ffn_in['ln_b'], 'L0_ffn_w2': _L0_ffn_in['w2'], 'L0_ffn_on_g': _L0_ffn_in['on_g'], 'L0_ffn_on_b': _L0_ffn_in['on_b'], 'L1_attn_w_attn': _L1_attn_in['w_attn'], 'L1_attn_b_attn': _L1_attn_in['b_attn'], 'L1_attn_w_k2': _L1_attn_in['w_k2'], 'L1_attn_b_k2': _L1_attn_in['b_k2'], 'L1_attn_w_proj': _L1_attn_in['w_proj'], 'L1_attn_b_proj': _L1_attn_in['b_proj'], 'L1_ffn_router': _L1_ffn_in['router'], 'L1_ffn_experts_gate': _L1_ffn_in['experts_gate'], 'L1_ffn_experts_up': _L1_ffn_in['experts_up'], 'L1_ffn_experts_down': _L1_ffn_in['experts_down'], 'L1_ffn_shared_gate': _L1_ffn_in['shared_gate'], 'L1_ffn_shared_up': _L1_ffn_in['shared_up'], 'L1_ffn_shared_down': _L1_ffn_in['shared_down']}
    _x0 = _d['L0_attn_x']
    _d['L0_attn_x'] = jax.random.normal(jax.random.fold_in(jax.random.key(seed), 1), (2, 2048, 256), dtype=_x0.dtype)
    del _x0
    return _d

def reference(L0_attn_x, L0_attn_wq, L0_attn_wk, L0_attn_wv, L0_attn_wo, L0_attn_head_dirs, L0_attn_scale, L0_ffn_router_w, L0_ffn_rn_g, L0_ffn_rn_b, L0_ffn_w1, L0_ffn_ln_g, L0_ffn_ln_b, L0_ffn_w2, L0_ffn_on_g, L0_ffn_on_b, L1_attn_w_attn, L1_attn_b_attn, L1_attn_w_k2, L1_attn_b_k2, L1_attn_w_proj, L1_attn_b_proj, L1_ffn_router, L1_ffn_experts_gate, L1_ffn_experts_up, L1_ffn_experts_down, L1_ffn_shared_gate, L1_ffn_shared_up, L1_ffn_shared_down):

    def _L0_attn_ref(x, wq, wk, wv, wo, head_dirs, scale):
        import jax, jax.numpy as jnp
        import numpy as np
        B, T, C, H = (2, 512, 256, 16)
        b, t, c = x.shape
        h = head_dirs.shape[0]
        hd = c // h
        q3 = (x @ wq).reshape(b, t, h, 3).transpose(0, 2, 1, 3)
        k3 = (x @ wk).reshape(b, t, h, 3).transpose(0, 2, 1, 3)
        v = (x @ wv).reshape(b, t, h, hd).transpose(0, 2, 1, 3)
        q_on_dir = jnp.einsum('bhtd,hd->bht', q3, head_dirs)
        k_on_dir = jnp.einsum('bhtd,hd->bht', k3, head_dirs)
        dot_scores = jnp.einsum('bhtd,bhsd->bhts', q3, k3) * scale
        geo_bias = q_on_dir[..., :, None] * k_on_dir[..., None, :]
        scores = dot_scores + geo_bias
        causal = jnp.tril(jnp.ones((t, t), dtype=bool))
        scores = jnp.where(causal, scores, -jnp.inf)
        attn = jax.nn.softmax(scores, axis=-1)
        out = jnp.einsum('bhts,bhsd->bhtd', attn, v)
        out = out.transpose(0, 2, 1, 3).reshape(b, t, c)
        return out @ wo

    def _L0_ffn_ref(h, router_w, rn_g, rn_b, w1, ln_g, ln_b, w2, on_g, on_b):
        import jax, jax.numpy as jnp
        import numpy as np
        EPS_LN = 1e-05
        EPS_GATE = 1e-08

        def layer_norm(x, gamma, beta):
            mu = jnp.mean(x, axis=-1, keepdims=True)
            var = jnp.mean(jnp.square(x - mu), axis=-1, keepdims=True)
            return (x - mu) * jax.lax.rsqrt(var + EPS_LN) * gamma + beta
        D = h.shape[-1]
        h_norm = layer_norm(h, rn_g, rn_b)
        g = jax.nn.softmax(jnp.einsum('bsd,ed->bse', h_norm, router_w), axis=-1)
        top2_w, top2_idx = jax.lax.top_k(g, 2)
        top2_w = top2_w / (jnp.sum(top2_w, axis=-1, keepdims=True) + EPS_GATE)
        hid = jnp.einsum('bsd,edh->bseh', h, w1)
        hid = jax.nn.relu(layer_norm(hid, ln_g, ln_b))
        expert_out = jnp.einsum('bseh,ehd->bsed', hid, w2)
        idx = jnp.broadcast_to(top2_idx[..., None], top2_idx.shape + (D,))
        top2_out = jnp.take_along_axis(expert_out, idx, axis=-2)
        out = jnp.sum(top2_out * top2_w[..., None], axis=-2)
        return layer_norm(out, on_g, on_b)

    def _L1_attn_ref(x, w_attn, b_attn, w_k2, b_k2, w_proj, b_proj):
        import math
        import jax, jax.numpy as jnp
        import numpy as np
        N_EMBD = 256
        N_HEAD = 16
        B, T = (2, 512)

        def _heads(t):
            b, s, d = t.shape
            return t.reshape(b, s, N_HEAD, d // N_HEAD).transpose(0, 2, 1, 3)
        b, t, d = x.shape
        hd = d // N_HEAD
        scale = 1.0 / math.sqrt(hd)
        qk = x @ w_attn.T + b_attn
        q, k = jnp.split(qk, 2, axis=-1)
        q, k, v = (_heads(q), _heads(k), _heads(x))
        scores = jnp.einsum('bhqd,bhkd->bhqk', q, k) * scale
        causal = jnp.tril(jnp.ones((t, t), dtype=bool))
        scores = jnp.where(causal, scores, -jnp.inf)
        y_ar = jnp.einsum('bhqk,bhkd->bhqd', jax.nn.softmax(scores, axis=-1), v)
        e = v[:, :, 1:, :] - y_ar[:, :, :-1, :]
        q2 = q[:, :, 1:, :]
        k2 = _heads(x[:, :-1] @ w_k2.T + b_k2)
        qa = -jax.nn.leaky_relu(-q2 * scale, negative_slope=0.02)
        ka = jax.nn.sigmoid(k2 * scale * 0.02)
        ma = jnp.einsum('bhqd,bhkd->bhqk', qa, ka)
        ma = jnp.where(jnp.tril(jnp.ones((t - 1, t - 1), dtype=bool)), ma, 0.0)
        y_ma = jnp.einsum('bhqk,bhkd->bhqd', ma, e)
        y_ma = jnp.concatenate([jnp.zeros_like(y_ma[:, :, :1, :]), y_ma], axis=2)

        def merge(z):
            return z.transpose(0, 2, 1, 3).reshape(b, t, d)
        out = merge(y_ar) @ w_proj.T + b_proj + (merge(y_ma) @ w_proj.T + b_proj)
        return out

    def _L1_ffn_ref(x, router, experts_gate, experts_up, experts_down, shared_gate, shared_up, shared_down):
        import jax, jax.numpy as jnp
        import numpy as np
        TOP_K = 2
        NUM_EXPERTS = 8
        b, s, h = x.shape
        E = router.shape[1]
        shared_act = jax.nn.silu(jnp.einsum('bsh,hd->bsd', x, shared_gate))
        shared_up_out = jnp.einsum('bsh,hd->bsd', x, shared_up)
        shared_out = jnp.einsum('bsd,dh->bsh', shared_act * shared_up_out, shared_down)
        router_probs = jax.nn.softmax(jnp.einsum('bsh,he->bse', x, router), axis=-1)
        topk_probs, topk_idx = jax.lax.top_k(router_probs, TOP_K)
        coef = jnp.sum(jax.nn.one_hot(topk_idx, E, dtype=x.dtype) * topk_probs[..., None], axis=2)
        coef = coef.reshape(b * s, E)
        x_flat = x.reshape(b * s, h)
        gate = jnp.einsum('th,ehd->etd', x_flat, experts_gate)
        up = jnp.einsum('th,ehd->etd', x_flat, experts_up)
        expert_out = jnp.einsum('etd,edh->eth', jax.nn.silu(gate) * up, experts_down)
        routed = jnp.einsum('eth,te->th', expert_out, coef)
        return routed.reshape(b, s, h) + shared_out
    x = L0_attn_x
    xn = _layernorm(x, axis=-1)
    x = x + _L0_attn_ref(xn, L0_attn_wq, L0_attn_wk, L0_attn_wv, L0_attn_wo, L0_attn_head_dirs, L0_attn_scale) + _L0_ffn_ref(xn, L0_ffn_router_w, L0_ffn_rn_g, L0_ffn_rn_b, L0_ffn_w1, L0_ffn_ln_g, L0_ffn_ln_b, L0_ffn_w2, L0_ffn_on_g, L0_ffn_on_b)
    xn = _layernorm(x, axis=-1)
    x = x + _L1_attn_ref(xn, L1_attn_w_attn, L1_attn_b_attn, L1_attn_w_k2, L1_attn_b_k2, L1_attn_w_proj, L1_attn_b_proj) + _L1_ffn_ref(xn, L1_ffn_router, L1_ffn_experts_gate, L1_ffn_experts_up, L1_ffn_experts_down, L1_ffn_shared_gate, L1_ffn_shared_up, L1_ffn_shared_down)
    return x

_drawn_inputs = setup_inputs


def setup_inputs(seed=0):
    import zlib

    import numpy as np

    out = dict(_drawn_inputs(seed))
    spreads = {'L0_ffn_rn_g': (1.0, 0.2),
     'L0_ffn_rn_b': (0.0, 0.1),
     'L0_ffn_ln_g': (1.0, 0.2),
     'L0_ffn_ln_b': (0.0, 0.1),
     'L0_ffn_on_g': (1.0, 0.2),
     'L0_ffn_on_b': (0.0, 0.1),
     'L1_attn_b_attn': (0.0, 0.1),
     'L1_attn_b_k2': (0.0, 2.0),
     'L1_attn_b_proj': (0.0, 0.1)}
    factors = {'L1_attn_w_k2': 200.0}
    for name, (base, spread) in spreads.items():
        noise = np.random.default_rng([zlib.crc32(name.encode()), seed]).standard_normal(out[name].shape)
        drawn = base * np.exp(spread * noise) if base else spread * noise
        out[name] = jnp.asarray(drawn.astype(out[name].dtype))
    for name, factor in factors.items():
        out[name] = (out[name] * factor).astype(out[name].dtype)
    return out
```

```python
from contextlib import ExitStack

import concourse.bass as bass
from concourse import mybir

ALU = mybir.AluOpType
ACT = mybir.ActivationFunctionType
F32 = mybir.dt.float32
BF16 = mybir.dt.bfloat16
AX_X = mybir.AxisListType.X

P = 128
EPS_LN = 1e-5
EPS_GATE = 1e-8
MASKED = -3.0e38
GT = 4
TOK = GT * P
SLOT = 32


def scratch(nc, name, shape, dt):
    return nc.dram_tensor(name, shape, dt).ap()


class Pools:

    def __init__(self, nc, ctx, stage):
        self.nc, self.ctx, self.stage = nc, ctx, stage

    def sb(self, name, shape, dt=F32):
        return self.ctx.enter_context(self.nc.sbuf_tensor(f"{self.stage}_{name}", shape, dt))

    def psum(self, name, shape=(P, 512), dt=F32):
        return self.ctx.enter_context(self.nc.psum_tensor(f"{self.stage}_{name}", list(shape), dt))

    def sem(self, name):
        return self.ctx.enter_context(self.nc.semaphore(f"{self.stage}_{name}"))


class Chain:

    def __init__(self, engine, sem, start=0):
        self.engine, self.sem, self.start, self.steps = engine, sem, start, 0

    def step(self, instruction):
        instruction.then_inc(self.sem, 1)
        self.steps += 1
        return self.steps

    def settle(self):
        self.engine.wait_ge(self.sem, self.start + self.steps)

    def link(self, instruction):
        self.step(instruction)
        self.settle()


class Shapes:
    def __init__(self, a):
        self.B, self.T, self.C = a["L0_attn_x"].shape
        self.H = a["L0_attn_head_dirs"].shape[0]
        self.D3 = a["L0_attn_head_dirs"].shape[1]
        self.HD = self.C // self.H
        self.KC = self.C // P
        self.TILES = self.B * self.T // P
        self.TB = self.T // P
        self.G = self.TILES // GT
        self.GB = self.TB // GT
        self.HG = self.H // 4
        self.E0, _, self.F0 = a["L0_ffn_w1"].shape
        self.E1, _, self.F1 = a["L1_ffn_experts_gate"].shape


def apart(engine, tick):
    engine.sem_inc(tick, 1)


def make_identity(eng, nc, m, sem, base):
    nc.gpsimd.memset(m, 0.0).then_inc(sem, 1)
    eng.wait_ge(sem, base + 1)
    nc.gpsimd.affine_select(out=m, in_=m, compare_op=ALU.not_equal, fill=1.0, base=0,
                            pattern=[[-1, P]], channel_multiplier=1).then_inc(sem, 1)


def stage_prep0(nc, a, S, keep, d):
    H, D3, HD, KC, C = S.H, S.D3, S.HD, S.KC, S.C
    W3 = H * D3
    NP = 2 * W3 + C + S.E0
    V0, R0 = 2 * W3, 2 * W3 + C
    with ExitStack() as ctx:
        pool = Pools(nc, ctx, "prep0")
        sb, psum, sem = pool.sb, pool.psum, pool.sem
        x_all = sb("x_all", [P, S.TILES, C])
        wp = sb("wp", [P, KC, NP])
        rwT = sb("rwT", [P, KC, S.E0])
        rgb = sb("rgb", [P, 2, KC])
        gbw = sb("gbw", [P, KC, 2 * S.E0])
        ones = sb("ones", [P, P])
        GB = sb("GB", [P, 2 * S.E0])
        dirs = sb("dirs", [P, W3])
        scl = sb("scl", [P, 1])
        half = sb("half", [P, S.TILES])
        stat = sb("stat", [P, GT, 6])
        mv = sb("mv", [P, GT, 2])
        ve = sb("ve", [P, GT])
        rstd = sb("rstd", [P, GT])
        stat2 = sb("stat2", [P, GT, 6])
        mvg = sb("mvg", [P, GT, 2])
        mv2 = sb("mv2", [P, S.TILES, 2])
        rl = sb("rl", [P, S.TILES, S.E0])
        xn = sb("xn", [P, GT, C])
        xnT = sb("xnT", [P, KC, GT, P])
        va = sb("va", [P, GT, H, SLOT])
        qk = sb("qk", [P, 2, GT * H, D3])
        sc1 = sb("sc1", [P, GT * H, D3])
        sc2 = sb("sc2", [P, GT * H])
        part = [sb(f"part{n}", [P, 2, GT * H, D3], BF16) for n in range(3)]
        QA = sb("QA", [P, GT * H, SLOT], BF16)
        KA = sb("KA", [P, GT * H, SLOT], BF16)
        QT = sb("QT", [P, S.HG, TOK], BF16)
        KT = sb("KT", [P, S.HG, TOK], BF16)
        big = [sb(f"big{n}", [P, S.TILES, S.E0]) for n in range(5)]
        row = [sb(f"row{n}", [P, S.TILES]) for n in range(3)]
        pT = [psum(f"pT{t}") for t in range(GT)]
        pP = [psum(f"pP{t}") for t in range(GT)]

        loaded, weights = sem("loaded"), sem("weights")
        pool_set, ones_set = sem("pool_set"), sem("ones_set")
        var_ready, rstd_ready = sem("var_ready"), sem("rstd_ready")
        xn_ready, xnT_psum, xnT_ready = sem("xn_ready"), sem("xnT_psum"), sem("xnT_ready")
        proj_done, qk_taken, v_taken = sem("proj_done"), sem("qk_taken"), sem("v_taken")
        parts_ready, ka_ready, qa_ready = sem("parts_ready"), sem("ka_ready"), sem("qa_ready")
        turned, turned_taken = sem("turned"), sem("turned_taken")
        stored = sem("stored")
        chain, gate_exp, logits, gb_psum = sem("chain"), sem("gate_exp"), sem("logits"), sem("gb_psum")
        last_rstd = sem("last_rstd")
        tick = sem("tick")

        STEPS = GT * 5 + 13
        HEAD = 8
        STORES = 5

        block = ctx.enter_context(nc.Block())

        @block.sync
        def _(sp):
            sp.sem_inc(stored, 1)
            xt = a["L0_attn_x"].rearrange("b t c -> (b t) c").rearrange("(n p) c -> p n c", p=P)
            for g in range(S.G):
                sp.dma_start(x_all[:, g * GT:(g + 1) * GT], xt[:, g * GT:(g + 1) * GT]).then_inc(loaded, 16)
            with sp.Fori(0, S.G) as it:
                tok = bass.ds(it * TOK, TOK)
                sp.wait_ge(xnT_ready, GT * it + GT)
                apart(sp, tick)
                sp.dma_start(d["xnT0"].rearrange("k p t -> p k t")[:, :, tok],
                             xnT[:].rearrange("p k t j -> p k (t j)")).then_inc(stored, 16)
                sp.wait_ge(v_taken, 1 + GT * it + GT)
                apart(sp, tick)
                sp.dma_start(d["va0"][:, bass.ds(it * GT, GT), :],
                             va[:].rearrange("p t h n -> p t (h n)")).then_inc(stored, 16)
                sp.wait_ge(qa_ready, it + 1)
                apart(sp, tick)
                sp.dma_start(d["qa0"][:, bass.ds(it * GT, GT), :],
                             QA[:].rearrange("p (t h) n -> p t (h n)", t=GT)).then_inc(stored, 16)
                sp.wait_ge(turned_taken, 1 + 4 * it + 4)
                apart(sp, tick)
                sp.dma_start(d["qT0"].rearrange("g p t -> p g t")[:, :, tok], QT[:]).then_inc(stored, 16)
                sp.dma_start(d["kT0"].rearrange("g p t -> p g t")[:, :, tok], KT[:]).then_inc(stored, 16)
            sp.wait_ge(stored, 1 + 16 * STORES * S.G)

        @block.gpsimd
        def _(pool_e):
            pool_e.sem_inc(ka_ready, 1)
            pool_e.dma_start(wp[:, :, 0:W3], a["L0_attn_wq"].rearrange("(k p) n -> p k n", p=P)).then_inc(weights, 16)
            pool_e.dma_start(wp[:, :, W3:2 * W3], a["L0_attn_wk"].rearrange("(k p) n -> p k n", p=P)).then_inc(weights, 16)
            pool_e.dma_start(wp[:, :, V0:R0], a["L0_attn_wv"].rearrange("(k p) n -> p k n", p=P)).then_inc(weights, 16)
            with nc.allow_non_contiguous_dma(reason="the router's weights turned, a few KB once"):
                for k in range(KC):
                    pool_e.dma_start(rwT[:, k, :], a["L0_ffn_router_w"].rearrange("e (k p) -> p k e", p=P)[:, k, :])\
                        .then_inc(weights, 16)
                pool_e.dma_start(rgb[:, 0, :], a["L0_ffn_rn_g"].rearrange("(k p) -> p k", p=P)).then_inc(weights, 16)
                pool_e.dma_start(rgb[:, 1, :], a["L0_ffn_rn_b"].rearrange("(k p) -> p k", p=P)).then_inc(weights, 16)
            pool_e.dma_start(dirs[:], a["L0_attn_head_dirs"].rearrange("h d -> (h d)").partition_broadcast(P))\
                .then_inc(weights, 16)
            pool_e.dma_start(scl[:], a["L0_attn_scale"].partition_broadcast(P)).then_inc(weights, 16)
            nc.gpsimd.memset(ones[:], 1.0).then_inc(ones_set, 1)
            nc.gpsimd.memset(half[:], -0.5).then_inc(ones_set, 1)
            make_identity(pool_e, nc, keep["ident"][:], pool_set, 0)
            make_identity(pool_e, nc, keep["identb"][:], pool_set, 2)
            nc.gpsimd.memset(keep["mask_qk"][:], 0.0).then_inc(pool_set, 1)
            nc.gpsimd.memset(keep["mask_kq"][:], 0.0).then_inc(pool_set, 1)
            pool_e.wait_ge(pool_set, 6)
            nc.gpsimd.affine_select(out=keep["mask_qk"][:], in_=keep["mask_qk"][:], compare_op=ALU.is_ge,
                                    fill=MASKED, base=0, pattern=[[-1, P]], channel_multiplier=1).then_inc(pool_set, 1)
            nc.gpsimd.affine_select(out=keep["mask_kq"][:], in_=keep["mask_kq"][:], compare_op=ALU.is_ge,
                                    fill=MASKED, base=0, pattern=[[1, P]], channel_multiplier=-1).then_inc(pool_set, 1)
            nc.gpsimd.memset(va[:], 0.0).then_inc(pool_set, 1)
            nc.gpsimd.memset(QA[:], 0.0).then_inc(pool_set, 1)
            nc.gpsimd.memset(KA[:], 0.0).then_inc(pool_set, 1)
            pool_e.wait_ge(pool_set, 11)
            nc.gpsimd.memset(va[:, :, :, HD:HD + 1], 1.0).then_inc(pool_set, 1)
            nc.gpsimd.memset(KA[:, :, 27:29], 1.0).then_inc(pool_set, 1)
            with pool_e.Fori(0, S.G) as it:
                pool_e.wait_ge(var_ready, it + 1)
                nc.gpsimd.tensor_tensor(rstd[:], ve[:], half[:, 0:GT], ALU.pow).then_inc(rstd_ready, 1)
                pool_e.wait_ge(parts_ready, it + 1)
                pool_e.wait_ge(turned, 1 + 4 * it)
                apart(pool_e, tick)
                for b in range(3):
                    dst = KA[:, :, 0:27].rearrange("p n (a b d) -> p n a b d", a=3, b=3)[:, :, :, b, :]
                    src = part[b][:, 1].unsqueeze(2).broadcast_to([P, GT * H, 3, D3])
                    nc.gpsimd.tensor_copy(dst, src).then_inc(ka_ready, 1)
            pool_e.wait_ge(var_ready, S.G + 1)
            nc.gpsimd.tensor_tensor(row[1][:], row[0][:], half[:], ALU.pow).then_inc(last_rstd, 1)

        @block.vector
        def _(dve):
            dve.sem_inc(qk_taken, 1)
            dve.wait_ge(weights, 16 * 9)
            c = Chain(dve, chain)
            for k in range(KC):
                for n in range(2):
                    c.step(nc.vector.tensor_scalar(gbw[:, k, n * S.E0:(n + 1) * S.E0], rwT[:, k, :],
                                                   rgb[:, n, k:k + 1], None, ALU.mult))
            for k in range(KC):
                c.step(nc.vector.tensor_scalar(wp[:, k, R0:NP], rwT[:, k, :], rgb[:, 0, k:k + 1], None, ALU.mult))
            dve.wait_ge(gb_psum, 1)
            c.step(nc.vector.tensor_copy(GB[:], pP[0][:, 0:2 * S.E0]))
            c.link(nc.vector.memset(rl[:], 0.0))
            assert c.steps == HEAD
            dve.wait_ge(loaded, 16 * S.G)
            dve.wait_ge(ones_set, 2)
            dve.wait_ge(pool_set, 13)
            with dve.Fori(0, S.G) as it:
                c = Chain(dve, chain, HEAD + it * STEPS)
                for t in range(GT):
                    c.step(nc.vector.bn_stats(stat[:, t, :], x_all[:, bass.ds(it * GT + t, 1), :]
                                              .rearrange("p a c -> p (a c)")))
                c.settle()
                apart(dve, tick)
                for t in range(GT):
                    c.step(nc.vector.bn_aggr(mv[:, t, :], stat[:, t, :]))
                c.settle()
                c.step(nc.vector.tensor_scalar(ve[:], mv[:, :, 1], EPS_LN, None, ALU.add))
                c.settle()
                dve.sem_inc(var_ready, 1)
                dve.wait_ge(rstd_ready, it + 1)
                for t in range(GT):
                    nc.vector.tensor_scalar(xn[:, t, :], x_all[:, bass.ds(it * GT + t, 1), :].rearrange("p a c -> p (a c)"),
                                            mv[:, t, 0:1], rstd[:, t:t + 1], ALU.subtract, ALU.mult).then_inc(xn_ready, 1)
                dve.wait_ge(xn_ready, GT * it + GT)
                for t in range(GT):
                    c.step(nc.vector.bn_stats(stat2[:, t, :], xn[:, t, :]))
                c.settle()
                apart(dve, tick)
                for t in range(GT):
                    c.step(nc.vector.bn_aggr(mvg[:, t, :], stat2[:, t, :]))
                c.settle()
                c.step(nc.vector.tensor_copy(mv2[:, bass.ds(it * GT, GT), :], mvg[:]))
                for t in range(GT):
                    dve.wait_ge(proj_done, GT * it + t + 1)
                    c.step(nc.vector.tensor_copy(
                        qk[:].rearrange("p s (t h) e -> p s t (h e)", t=GT)[:, :, t, :],
                        pP[t][:, 0:2 * W3].rearrange("p (s n) -> p s n", s=2)))
                    nc.vector.tensor_copy(rl[:, bass.ds(it * GT + t, 1), :].rearrange("p a c -> p (a c)"),
                                          pP[t][:, R0:NP]).then_inc(qk_taken, 1)
                c.settle()
                q4 = qk[:, 0].rearrange("p (t h) e -> p t (h e)", t=GT)
                dir4 = dirs[:].unsqueeze(1).broadcast_to([P, GT, W3])
                s4 = sc1[:].rearrange("p (t h) e -> p t (h e)", t=GT)
                c.link(nc.vector.tensor_tensor(s4, q4, dir4, ALU.mult))
                c.link(nc.vector.tensor_reduce(sc2[:], sc1[:], AX_X, ALU.add))
                c.link(
                    nc.vector.tensor_tensor(
                        s4.rearrange("p t (h e) -> p t h e", e=D3),
                        sc2[:].rearrange("p (t h) -> p t h", t=GT).unsqueeze(3).broadcast_to([P, GT, H, D3]),
                        dirs[:].rearrange("p (h e) -> p h e", e=D3).unsqueeze(1).broadcast_to([P, GT, H, D3]),
                        ALU.mult))
                c.link(nc.vector.scalar_tensor_tensor(qk[:, 0], qk[:, 0], scl[:, 0:1], sc1[:], ALU.mult, ALU.add))
                dve.wait_ge(ka_ready, 1 + 3 * it)
                c.link(nc.vector.tensor_copy(part[0][:], qk[:]))
                c.link(nc.vector.tensor_tensor(qk[:], qk[:], part[0][:], ALU.subtract))
                c.link(nc.vector.tensor_copy(part[1][:], qk[:]))
                c.link(nc.vector.tensor_tensor(qk[:], qk[:], part[1][:], ALU.subtract))
                c.step(nc.vector.tensor_copy(part[2][:], qk[:]))
                c.settle()
                dve.sem_inc(parts_ready, 1)
                dve.wait_ge(turned, 1 + 4 * it)
                dve.wait_ge(stored, 1 + 16 * STORES * it)
                for p in range(3):
                    dst = QA[:, :, 9 * p:9 * p + 9].rearrange("p n (b d) -> p n b d", b=3)
                    src = part[p][:, 0].unsqueeze(2).broadcast_to([P, GT * H, 3, D3])
                    if p < 2:
                        c.step(nc.vector.tensor_copy(dst, src))
                    else:
                        c.settle()
                        nc.vector.tensor_copy(dst, src).then_inc(qa_ready, 1)
                assert c.steps == STEPS, c.steps

            E = S.E0
            c = Chain(dve, chain, HEAD + S.G * STEPS)
            mu2, var2 = mv2[:, :, 0], mv2[:, :, 1]
            c.link(nc.vector.tensor_scalar(row[0][:], var2, EPS_LN, None, ALU.add))
            dve.sem_inc(var_ready, 1)
            be = lambda v: v.unsqueeze(1).broadcast_to([P, S.TILES, E])
            bt = lambda v: v.unsqueeze(2).broadcast_to([P, S.TILES, E])
            c.link(nc.vector.tensor_tensor(big[0][:], bt(mu2), be(GB[:, 0:E]), ALU.mult))
            c.link(nc.vector.tensor_tensor(big[1][:], rl[:], big[0][:], ALU.subtract))
            dve.wait_ge(last_rstd, 1)
            c.link(nc.vector.tensor_tensor(big[0][:], big[1][:], bt(row[1][:]), ALU.mult))
            c.link(nc.vector.tensor_tensor(big[1][:], big[0][:], be(GB[:, E:2 * E]), ALU.add))
            top_two(nc, dve, c, S.TILES, E, big, row, gate_exp, logits, keep["gate0"], True)

        @block.scalar
        def _(act):
            act.sem_inc(turned_taken, 1)
            act.sem_inc(v_taken, 1)
            act.wait_ge(pool_set, 13)
            with act.Fori(0, S.G) as it:
                act.wait_ge(stored, 1 + 16 * STORES * it)
                for t in range(GT):
                    act.wait_ge(xnT_psum, GT * it + t + 1)
                    nc.scalar.copy(xnT[:, :, t, :], pT[t][:, 0:C].rearrange("p (k j) -> p k j", k=KC))\
                        .then_inc(xnT_ready, 1)
                for t in range(GT):
                    act.wait_ge(proj_done, GT * it + t + 1)
                    act.wait_ge(qk_taken, 1 + GT * it + t + 1)
                    nc.scalar.copy(va[:, t, :, 0:HD], pP[t][:, V0:R0].rearrange("p (h e) -> p h e", e=HD))\
                        .then_inc(v_taken, 1)
                for n in range(2):
                    for m, dst in enumerate((QT, KT)):
                        act.wait_ge(turned, 1 + 4 * it + 2 * n + m + 1)
                        nc.scalar.copy(dst[:, 2 * n:2 * n + 2, :],
                                       pT[2 * n + m][:].bitcast(BF16).rearrange("p (g j) -> p g j", g=2))\
                            .then_inc(turned_taken, 1)
            act.wait_ge(logits, 1)
            nc.scalar.activation(big[3][:], big[2][:], ACT.Exp).then_inc(gate_exp, 1)

        @block.tensor
        def _(pe):
            pe.sem_inc(turned, 1)
            pe.wait_ge(ones_set, 2)
            pe.wait_ge(chain, 4)
            for k in range(KC):
                last = nc.tensor.matmul(pP[0][:, 0:2 * S.E0], ones[:], gbw[:, k, :], start=(k == 0), stop=(k == KC - 1))
            last.then_inc(gb_psum, 1)
            pe.wait_ge(chain, HEAD)
            pe.wait_ge(pool_set, 4)
            with pe.Fori(0, S.G) as it:
                pe.wait_ge(turned_taken, 1 + 4 * it)
                for t in range(GT):
                    pe.wait_ge(xn_ready, GT * it + t + 1)
                    for k in range(KC):
                        last = nc.tensor.transpose(pT[t][:, k * P:(k + 1) * P], xn[:, t, k * P:(k + 1) * P],
                                                   keep["ident"][:])
                    last.then_inc(xnT_psum, 1)
                pe.wait_ge(qk_taken, 1 + GT * it)
                pe.wait_ge(v_taken, 1 + GT * it)
                for t in range(GT):
                    pe.wait_ge(xnT_ready, GT * it + t + 1)
                    for k in range(KC):
                        last = nc.tensor.matmul(pP[t][:, 0:NP], xnT[:, k, t, :], wp[:, k, :],
                                                start=(k == 0), stop=(k == KC - 1))
                    last.then_inc(proj_done, 1)
                pe.wait_ge(qa_ready, it + 1)
                pe.wait_ge(ka_ready, 1 + 3 * it + 3)
                for n in range(2):
                    for m, src in enumerate((QA, KA)):
                        bank = pT[2 * n + m][:].bitcast(BF16)
                        for g in range(2):
                            for t in range(GT):
                                rows = src[:].rearrange("p (t g h) n -> p t g (h n)", t=GT, g=S.HG)[:, t, 2 * n + g, :]
                                last = nc.tensor.transpose(bank[:, g * TOK + t * P:g * TOK + (t + 1) * P], rows,
                                                           keep["identb"][:])
                        last.then_inc(turned, 1)


def top_two(nc, dve, c, N, E, big, row, exp_done, logits_ready, gate, renormalise):
    bt = lambda v: v.unsqueeze(2).broadcast_to([P, N, E])
    c.link(nc.vector.tensor_reduce(row[2][:], big[1][:], AX_X, ALU.max))
    nc.vector.tensor_tensor(big[2][:], big[1][:], bt(row[2][:]), ALU.subtract).then_inc(logits_ready, 1)
    dve.wait_ge(exp_done, 1)
    c.link(nc.vector.tensor_reduce(row[0][:], big[3][:], AX_X, ALU.add))
    c.link(nc.vector.reciprocal(row[1][:], row[0][:]))
    c.link(nc.vector.tensor_tensor(big[0][:], big[3][:], bt(row[1][:]), ALU.mult))
    c.link(nc.vector.memset(big[1][:], 0.0))
    for f in range(E):
        for lo, hi, op in ((0, f, ALU.is_gt), (f + 1, E, ALU.is_ge)):
            if lo < hi:
                c.link(nc.vector.tensor_tensor(big[2][:, :, lo:hi], big[0][:, :, f:f + 1].broadcast_to([P, N, hi - lo]),
                                               big[0][:, :, lo:hi], op))
                c.link(nc.vector.tensor_tensor(big[1][:, :, lo:hi], big[1][:, :, lo:hi], big[2][:, :, lo:hi], ALU.add))
    out = big[4] if renormalise else gate
    c.link(nc.vector.scalar_tensor_tensor(out[:], big[1][:], 1.5, big[0][:], ALU.is_lt, ALU.mult))
    if renormalise:
        c.link(nc.vector.tensor_reduce(row[0][:], out[:], AX_X, ALU.add))
        c.link(nc.vector.tensor_scalar(row[2][:], row[0][:], EPS_GATE, None, ALU.add))
        c.link(nc.vector.reciprocal(row[1][:], row[2][:]))
        c.link(nc.vector.tensor_tensor(gate[:], out[:], bt(row[1][:]), ALU.mult))


SCORE_BANKS = 3
MAX_BANKS = 2
PROBS = 6
WORK_BANKS = 2


def slot_plan(S, attend, maxima, ffn, turns):
    steps, m = [], 0
    if attend:
        for g in range(S.GB):
            for kt in range(GT * (g + 1)):
                for j in range(4):
                    steps.append((m, "score", (g, kt, j, m)))
                    steps.append((m + 2.5, "value", (g, kt, j, m)))
                    m += 1
            steps.append((m + 1.51, "sums_out", (g,)))
            steps.append((m + 5.51, "turn_out", (g,)))
    if maxima:
        k, n = 0, sum(4 * GT * (g + 1) for g in range(S.GB))
        for g in range(S.GB):
            for t in range(GT):
                for j in range(4):
                    for c in range(g + 1):
                        at = 4 + k * 150.0 / n
                        steps.append((at, "peak", (g, t, j, c, k)))
                        k += 1
            steps.append((at + 0.01, "shift", (g,)))
            for h in range(turns):
                steps.append((at + 3.11 + 1.5 * h, "turn_q", (g, h)))
    if ffn == 0:
        for n in range(GT * S.E0):
            at = 10 * n + 0.3
            steps += [(at, "hidden", (n,)), (at + 2, "norm", (n,)), (at + 6, "turn_hidden", (n,)),
                      (at + 9, "out", (n,))]
            if n % S.E0 == S.E0 - 1:
                steps += [(at + 9.1, "out_stats", (n // S.E0,)), (at + 11.1, "out_norm", (n // S.E0,))]
    if ffn == 1:
        for e in range(S.E1 + S.KC):
            at = 16 * e + 0.3
            steps += [(at, "gate", (e,)), (at + 3, "up", (e,)), (at + 9, "down", (e, 0)), (at + 12, "down", (e, 1))]
    held = [(at, at + 2.01) for at, kind, _ in steps if kind == "hidden"]
    for n, (at, kind, args) in enumerate(steps):
        if kind in ("turn_q", "turn_out"):
            for lo, hi in held:
                if lo < at < hi:
                    steps[n] = (hi + 0.001 * (at - lo), kind, args)
    steps.sort(key=lambda s: s[0])
    return [(kind, args) for _, kind, args in steps]


EMPTIES = {"turn_out": "dve", "turn_q": "dve", "hidden": "dve", "turn_hidden": "act", "out": "dve",
           "gate": "dve", "up": "dve", "down": "dve"}


class Works:

    def __init__(self, plan):
        self.use, self.release, self.before = {}, {}, {}
        self.count = {"dve": 0, "act": 0}
        filling = [step for step in plan if step[0] in EMPTIES]
        for n, step in enumerate(filling):
            self.use[step] = n
        for kind, args in plan:
            step = ("hidden", args) if kind == "norm" else (kind, args)
            if kind in EMPTIES and kind != "hidden" or kind == "norm":
                who = EMPTIES[step[0]]
                self.release[step] = self.count[who]
                self.count[who] += 1
        for n, step in enumerate(filling):
            earlier = filling[n - WORK_BANKS] if n >= WORK_BANKS else None
            self.before[step] = (EMPTIES[earlier[0]], self.release[earlier]) if earlier else None
        self.total = len(filling)


def stage_layer(nc, a, S, keep, d, layer):
    H, HD, KC, C = S.H, S.HD, S.KC, S.C
    stack = layer == 0
    qw = 1 if stack else 4
    hw = SLOT if stack else P
    m_row = 27 if stack else 96
    turns = 1 if stack else 2
    UNITS = S.HG * S.B
    T = S.T
    full = slot_plan(S, True, True, layer, turns)
    first = slot_plan(S, False, True, None, turns)
    final = slot_plan(S, True, False, layer, turns)
    works = {id(p): Works(p) for p in (full, first, final)}
    W0, W1 = works[id(first)], works[id(full)]
    NM = sum(1 for s in full if s[0] == "score")
    NX = sum(1 for s in full if s[0] == "peak")
    NE = GT * S.E0 if layer == 0 else S.E1 + KC
    LOADS = (4 if stack else 1) + 3

    with ExitStack() as ctx:
        pool = Pools(nc, ctx, f"layer{layer}")
        sb, psum, sem = pool.sb, pool.psum, pool.sem
        KZ = [sb(f"KZ{n}", [P, 4, T], BF16) for n in range(2)]
        QT = [sb(f"QT{n}", [P, qw, T], BF16) for n in range(2)]
        QA = [sb(f"QA{n}", [P, S.TB, qw * P], BF16) for n in range(2)]
        V = [sb(f"V{n}", [P, S.TB, 4 * SLOT]) for n in range(2)]
        XT = [sb(f"XT{n}", [P, KC, TOK]) for n in range(2)]
        probs = [sb(f"probs{n}", [P, TOK]) for n in range(PROBS)]
        peaks = sb("peaks", [P, GT * 4, S.GB])
        nm = sb("nm", [P, GT * 4])
        sumsT = sb("sumsT", [P, TOK])
        inv = sb("inv", [P, GT * 4])
        y = sb("y", [P, GT, 4, HD])
        acc = sb("acc", [P, GT, C])
        if layer == 0:
            w1 = sb("w1", [P, KC, S.E0, S.F0])
            w2 = sb("w2", [P, S.E0, S.F0 // P, C])
            lng = sb("lng", [P, S.E0, S.F0])
            lnb = sb("lnb", [P, S.E0, S.F0])
            ong = sb("ong", [P, 2, C])
            half = sb("half", [P, 1])
            hstat, hmv, hve, hrstd = sb("hstat", [P, 6]), sb("hmv", [P, 2]), sb("hve", [P, 1]), sb("hrstd", [P, 1])
            ostat, omv, ove, orstd = sb("ostat", [P, 6]), sb("omv", [P, 2]), sb("ove", [P, 1]), sb("orstd", [P, 1])
            hn = [sb(f"hn{n}", [P, S.F0]) for n in range(2)]
            hT = [sb(f"hT{n}", [P, S.F0 // P, P]) for n in range(2)]
            fo = sb("fo", [P, C])
            WLOADS = S.E0 * 4 + 2
        else:
            NX1 = S.E1 + KC
            wg = sb("wg", [P, KC, NX1 * P])
            wu = sb("wu", [P, KC, NX1 * P])
            wd = sb("wd", [P, NX1, C])
            coef = sb("coef", [P, S.TILES, S.E1])
            th = [sb(f"th{n}", [P, TOK]) for n in range(2)]
            gh = [sb(f"gh{n}", [P, TOK]) for n in range(2)]
            hT = [sb(f"hT{n}", [P, TOK]) for n in range(2)]
            WLOADS = 2 * S.E1 + 4
        score_b = [psum(f"score{n}") for n in range(SCORE_BANKS)]
        max_b = [psum(f"max{n}") for n in range(MAX_BANKS)]
        sums_b = psum("sums")
        work_b = [psum(f"work{n}") for n in range(WORK_BANKS)]

        unit_in, w_in = sem("unit_in"), sem("w_in")
        group_in = [sem(f"group_in{n}") for n in range(2)]
        slot_done = sem("slot_done")
        score_full, exp_done, value_done = sem("score_full"), sem("exp_done"), sem("value_done")
        sums_taken = sem("sums_taken")
        peak_full, peak_taken = sem("peak_full"), sem("peak_taken")
        shift_ready = sem("shift_ready")
        work_full, work_dve, work_act = sem("work_full"), sem("work_dve"), sem("work_act")
        y_stored = sem("y_stored")
        chain, tick, setup = sem("chain"), sem("tick"), sem("setup")
        hvar, hrstd_ready, hid_ready = sem("hvar"), sem("hrstd_ready"), sem("hid_ready")
        ovar, orstd_ready, fo_ready, fo_done, ff_stored = (sem("ovar"), sem("orstd_ready"), sem("fo_ready"),
                                                           sem("fo_done"), sem("ff_stored"))
        pool_chain, fo_chain, tanh_done = sem("pool_chain"), sem("fo_chain"), sem("tanh_done")

        def per_slot(plan, *kinds):
            return sum(1 for s in plan if s[0] in kinds)

        def wbase(u):
            return W0.total + u * W1.total

        def wait_work_free(pe, u, wk, step):
            before = wk.before[step]
            if before is None:
                pe.wait_ge(work_dve, 1 + W0.count["dve"] + u * W1.count["dve"] if u is not None else 1)
                pe.wait_ge(work_act, 1 + u * W1.count["act"] if u is not None else 1)
            elif before[0] == "dve":
                pe.wait_ge(work_dve, 2 + before[1] + ((W0.count["dve"] + u * W1.count["dve"]) if u is not None else 0))
            else:
                pe.wait_ge(work_act, 2 + before[1] + u * W1.count["act"])

        def filled(u, wk, step):
            return 1 + wk.use[step] + (wbase(u) if u is not None else 0)

        def freed(u, wk, step, who="dve"):
            if who == "dve":
                return 2 + wk.release[step] + ((W0.count["dve"] + u * W1.count["dve"]) if u is not None else 0)
            return 2 + wk.release[step] + u * W1.count["act"]

        def bank(wk, step, u):
            return work_b[wk.use[step] % WORK_BANKS]

        assert W0.total % WORK_BANKS == 0 and W1.total % WORK_BANKS == 0

        def slots(engine, body):
            body(first, None, 1)
            with engine.Fori(0, UNITS // 2 - 1) as i:
                for parity in range(2):
                    body(full, 2 * i + parity, parity)
            body(full, UNITS - 2, 0)
            body(final, UNITS - 1, 1)

        block = ctx.enter_context(nc.Block())

        @block.sync
        def _(sp):
            def load_unit(hg, b):
                p = b
                rows = slice(b * T, (b + 1) * T)
                if stack:
                    for j in range(4):
                        sp.dma_start(KZ[p][SLOT * j:SLOT * (j + 1), j, :],
                                     d["kT0"][bass.ds(hg, 1), SLOT * j:SLOT * (j + 1), rows]
                                     .rearrange("a p t -> p (a t)")).then_inc(unit_in, 16)
                    sp.dma_start(QT[p][:, 0, :], d["qT0"][bass.ds(hg, 1), :, rows].rearrange("a p t -> p (a t)"))\
                        .then_inc(unit_in, 16)
                else:
                    sp.dma_start(KZ[p][:], d["kT1"][bass.ds(hg, 1), :, :, rows].rearrange("a p j t -> p (a j) t"))\
                        .then_inc(unit_in, 16)
                    sp.dma_start(QT[p][:], d["qT1"][bass.ds(hg, 1), :, :, rows].rearrange("a p j t -> p (a j) t"))\
                        .then_inc(unit_in, 16)
                tiles = slice(b * S.TB, (b + 1) * S.TB)
                sp.dma_start(QA[p][:], d[f"qa{layer}"][:, tiles, bass.ds(hg * qw * P, qw * P)]).then_inc(unit_in, 16)
                sp.dma_start(V[p][:], d[f"va{layer}"][:, tiles, bass.ds(hg * 4 * SLOT, 4 * SLOT)]).then_inc(unit_in, 16)

            def load_group(c, parity):
                sp.dma_start(XT[parity][:], d[f"xnT{layer}"].rearrange("k p t -> p k t")[:, :, bass.ds(c * TOK, TOK)])\
                    .then_inc(group_in[parity], 16)

            sp.sem_inc(y_stored, 1)
            sp.sem_inc(ff_stored, 1)
            if stack:
                sp.wait_ge(setup, 3)
            load_unit(0, 0)
            load_group(0, 0)

            def slot(i, parity, last):
                u = 2 * i + parity
                if not last:
                    sp.wait_ge(slot_done, 1 + u)
                    apart(sp, tick)
                    if parity == 0:
                        load_unit(i, 1)
                    else:
                        load_unit(i + 1, 0)
                    load_group(u + 1, 1 - parity)
                plan = final if last else full
                wk = works[id(plan)]
                for step in plan:
                    kind, args = step
                    if kind == "turn_out":
                        g, = args
                        sp.wait_ge(work_dve, freed(u, wk, step))
                        apart(sp, tick)
                        sp.dma_start(d[f"y{layer}"][bass.ds(i, 1), :, parity * S.TB + g * GT:parity * S.TB + (g + 1) * GT, :]
                                     .rearrange("a p t n -> p (a t) n"),
                                     y[:].rearrange("p t h e -> p t (h e)")).then_inc(y_stored, 16)
                    elif kind == "out_norm":
                        t, = args
                        sp.wait_ge(fo_done, GT * u + t + 1)
                        apart(sp, tick)
                        sp.dma_start(d["ff0"][:, bass.ds(GT * u + t, 1), :].rearrange("p a c -> p (a c)"), fo[:])\
                            .then_inc(ff_stored, 16)
                if layer == 1:
                    sp.wait_ge(work_dve, freed(u, wk, ("down", (NE - 1, 1))))
                    apart(sp, tick)
                    sp.dma_start(d["ff1"][:, bass.ds(GT * u, GT), :], acc[:]).then_inc(ff_stored, 16)

            with sp.Fori(0, UNITS // 2 - 1) as i:
                for parity in range(2):
                    slot(i, parity, False)
            slot(UNITS // 2 - 1, 0, False)
            slot(UNITS // 2 - 1, 1, True)
            sp.wait_ge(y_stored, 1 + 16 * S.GB * UNITS)
            sp.wait_ge(ff_stored, 1 + 16 * (GT * UNITS if layer == 0 else UNITS))

        @block.gpsimd
        def _(pool_e):
            if layer == 0:
                for e in range(S.E0):
                    pool_e.dma_start(w1[:, :, e, :], a["L0_ffn_w1"][e].rearrange("(k p) f -> p k f", p=P)).then_inc(w_in, 16)
                    pool_e.dma_start(w2[:, e], a["L0_ffn_w2"][e].rearrange("(k p) c -> p k c", p=P)).then_inc(w_in, 16)
                    pool_e.dma_start(lng[:, e], a["L0_ffn_ln_g"][e].partition_broadcast(P)).then_inc(w_in, 16)
                    pool_e.dma_start(lnb[:, e], a["L0_ffn_ln_b"][e].partition_broadcast(P)).then_inc(w_in, 16)
                pool_e.dma_start(ong[:, 0], a["L0_ffn_on_g"].partition_broadcast(P)).then_inc(w_in, 16)
                pool_e.dma_start(ong[:, 1], a["L0_ffn_on_b"].partition_broadcast(P)).then_inc(w_in, 16)
                nc.gpsimd.memset(KZ[0][:], 0.0).then_inc(setup, 1)
                nc.gpsimd.memset(KZ[1][:], 0.0).then_inc(setup, 1)
                nc.gpsimd.memset(half[:], -0.5).then_inc(setup, 1)
                pool_e.wait_ge(w_in, 16 * WLOADS)
                pool_e.wait_ge(setup, 3)
            else:
                for w, name, shared in ((wg, "L1_ffn_experts_gate", "L1_ffn_shared_gate"),
                                        (wu, "L1_ffn_experts_up", "L1_ffn_shared_up")):
                    for e in range(S.E1):
                        pool_e.dma_start(w[:, :, e * P:(e + 1) * P], a[name][e].rearrange("(k p) f -> p k f", p=P))\
                            .then_inc(w_in, 16)
                    pool_e.dma_start(w[:, :, S.E1 * P:], a[shared].rearrange("(k p) f -> p k f", p=P)).then_inc(w_in, 16)
                pool_e.dma_start(wd[:, 0:S.E1, :], a["L1_ffn_experts_down"].rearrange("e p c -> p e c")).then_inc(w_in, 16)
                pool_e.dma_start(wd[:, S.E1:, :], a["L1_ffn_shared_down"].rearrange("(e p) c -> p e c", p=P))\
                    .then_inc(w_in, 16)

            def body(plan, u, parity):
                wk = works[id(plan)]
                for step in plan:
                    kind, args = step
                    if kind == "hidden":
                        n, = args
                        pool_e.wait_ge(hvar, NE * u + n + 1)
                        nc.gpsimd.tensor_tensor(hrstd[:], hve[:], half[:], ALU.pow).then_inc(hrstd_ready, 1)
                    elif kind == "norm":
                        n, = args
                        e = n % S.E0
                        pool_e.wait_ge(work_dve, freed(u, wk, ("hidden", args)))
                        nc.gpsimd.tensor_tensor(hn[n % 2][:], hn[n % 2][:], lng[:, e], ALU.mult).then_inc(pool_chain, 1)
                        pool_e.wait_ge(pool_chain, NE * u + n + 1 + 0)
                        nc.gpsimd.tensor_tensor(hn[n % 2][:], hn[n % 2][:], lnb[:, e], ALU.add).then_inc(hid_ready, 1)
                    elif kind == "out_stats":
                        t, = args
                        pool_e.wait_ge(ovar, GT * u + t + 1)
                        nc.gpsimd.tensor_tensor(orstd[:], ove[:], half[:], ALU.pow).then_inc(orstd_ready, 1)
                    elif kind == "out_norm":
                        t, = args
                        pool_e.wait_ge(fo_ready, GT * u + t + 1)
                        nc.gpsimd.tensor_tensor(fo[:], fo[:], ong[:, 0], ALU.mult).then_inc(fo_chain, 1)
                        pool_e.wait_ge(fo_chain, GT * u + t + 1)
                        nc.gpsimd.tensor_tensor(fo[:], fo[:], ong[:, 1], ALU.add).then_inc(fo_done, 1)

            if layer == 0:
                slots(pool_e, body)

        @block.scalar
        def _(act):
            act.sem_inc(exp_done, SCORE_BANKS)
            act.sem_inc(work_act, 1)

            def body(plan, u, parity):
                wk = works[id(plan)]
                for step in plan:
                    kind, args = step
                    if kind == "score":
                        g, kt, j, m = args
                        q0 = max(0, kt - GT * g) * P
                        act.wait_ge(score_full, NM * u + m + 1)
                        act.wait_ge(value_done, NM * u + m + 1)
                        nc.scalar.activation(probs[m % PROBS][:, q0:TOK], score_b[m % SCORE_BANKS][:, q0:TOK], ACT.Exp)\
                            .then_inc(exp_done, 1)
                    elif kind == "turn_hidden":
                        n, = args
                        act.wait_ge(work_full, filled(u, wk, step))
                        act.wait_ge(work_full, filled(u, wk, ("out", (n - 2,))) if n >= 2 else wbase(u))
                        nc.scalar.activation(hT[n % 2][:], bank(wk, step, u)[:].rearrange("p (k j) -> p k j", j=P), ACT.Relu)\
                            .then_inc(work_act, 1)
                    elif kind == "gate":
                        e, = args
                        act.wait_ge(work_full, filled(u, wk, step))
                        act.wait_ge(work_dve, freed(u, wk, ("gate", (e - 2,))) if e >= 2
                                    else 1 + W0.count["dve"] + u * W1.count["dve"])
                        nc.scalar.activation(th[e % 2][:], bank(wk, step, u)[:], ACT.Tanh, scale=0.5).then_inc(tanh_done, 1)

            slots(act, body)

        @block.vector
        def _(dve):
            dve.sem_inc(sums_taken, 1)
            dve.sem_inc(peak_taken, MAX_BANKS)
            dve.sem_inc(work_dve, 1)
            if layer == 1:
                dve.wait_ge(w_in, 16 * WLOADS)
                nc.vector.tensor_scalar(coef[:], keep["gate1"][:], 0.5, None, ALU.mult).then_inc(setup, 1)
                dve.wait_ge(setup, 1)
            shift_steps = 2 * S.GB
            ffn_steps = (2 * NE + 2 * GT) if layer == 0 else 0
            out_steps = S.GB
            base_first = shift_steps
            per_full = shift_steps + ffn_steps + out_steps

            def body(plan, u, parity):
                wk = works[id(plan)]
                nxt = 1 - parity
                c = Chain(dve, chain, (base_first + u * per_full) if u is not None else 0)
                ahead = (1 + u) if u is not None else 0
                for step in plan:
                    kind, args = step
                    if kind == "peak":
                        g, t, j, ch, k = args
                        w = TOK if ch < g else (t + 1) * P
                        dve.wait_ge(peak_full, NX * ahead + k + 1)
                        nc.vector.tensor_reduce(peaks[:, 4 * t + j, ch:ch + 1], max_b[k % MAX_BANKS][:, 0:w], AX_X, ALU.max)\
                            .then_inc(peak_taken, 1)
                    elif kind == "shift":
                        g, = args
                        k_last = sum(4 * GT * (x + 1) for x in range(g + 1))
                        rows = QA[nxt][:].rearrange("p t (j n) -> p t j n", j=4)[:, g * GT:(g + 1) * GT]
                        nm3 = nm[:].rearrange("p (t j) -> p t j", j=4)
                        dve.wait_ge(peak_taken, MAX_BANKS + NX * ahead + k_last)
                        if g == 0:
                            dve.wait_ge(unit_in, 16 * LOADS * (ahead + 1))
                        c.link(nc.vector.tensor_reduce(nm[:], peaks[:, :, 0:g + 1], AX_X, ALU.max, negate=True))
                        c.link(nc.vector.tensor_copy(rows[:, :, :, m_row], nm3))
                        nc.vector.tensor_tensor(rows[:, :, :, m_row + 1], nm3, rows[:, :, :, m_row], ALU.subtract)\
                            .then_inc(shift_ready, 1)
                    elif kind == "turn_q":
                        g, h = args
                        dve.wait_ge(work_full, filled(u, wk, step))
                        src = bank(wk, step, u)[:].bitcast(BF16)
                        cols = slice(g * TOK, (g + 1) * TOK)
                        if stack:
                            nc.vector.tensor_copy(QT[nxt][:, 0, cols], src[:, 0:TOK]).then_inc(work_dve, 1)
                        else:
                            nc.vector.tensor_copy(QT[nxt][:, 2 * h:2 * h + 2, cols],
                                                  src.rearrange("p (j t) -> p j t", j=2)).then_inc(work_dve, 1)
                    elif kind == "sums_out":
                        g, = args
                        m_last = sum(4 * GT * (x + 1) for x in range(g + 1))
                        dve.wait_ge(value_done, PROBS + NM * u + m_last)
                        nc.vector.tensor_copy(sumsT[:], sums_b[:]).then_inc(sums_taken, 1)
                    elif kind == "turn_out":
                        g, = args
                        dve.wait_ge(work_full, filled(u, wk, step))
                        src = bank(wk, step, u)[:].rearrange("p (n e) -> p n e", e=SLOT)
                        c.link(nc.vector.reciprocal(inv[:].unsqueeze(2), src[:, :, HD:HD + 1]))
                        dve.wait_ge(y_stored, 1 + 16 * (S.GB * u + g))
                        nc.vector.tensor_tensor(y[:].rearrange("p t h e -> p (t h) e"), src[:, :, 0:HD],
                                                inv[:].unsqueeze(2).broadcast_to([P, GT * 4, HD]), ALU.mult)\
                            .then_inc(work_dve, 1)
                    elif kind == "hidden":
                        n, = args
                        dve.wait_ge(work_full, filled(u, wk, step))
                        c.link(nc.vector.bn_stats(hstat[:], bank(wk, step, u)[:]))
                        apart(dve, tick)
                        c.link(nc.vector.bn_aggr(hmv[:], hstat[:]))
                        nc.vector.tensor_scalar(hve[:], hmv[:, 1:2], EPS_LN, None, ALU.add).then_inc(hvar, 1)
                    elif kind == "norm":
                        n, = args
                        hid = ("hidden", args)
                        dve.wait_ge(hrstd_ready, NE * u + n + 1)
                        dve.wait_ge(work_full, filled(u, wk, ("turn_hidden", (n - 2,))) if n >= 2 else wbase(u))
                        nc.vector.tensor_scalar(hn[n % 2][:], bank(wk, hid, u)[:], hmv[:, 0:1], hrstd[:, 0:1],
                                                ALU.subtract, ALU.mult).then_inc(work_dve, 1)
                    elif kind == "out":
                        n, = args
                        t, e = divmod(n, S.E0)
                        gate = keep["gate0"][:, bass.ds(GT * u + t, 1), e:e + 1].rearrange("p a b -> p (a b)")
                        src = bank(wk, step, u)[:, 0:C]
                        dve.wait_ge(work_full, filled(u, wk, step))
                        if e == 0:
                            nc.vector.tensor_scalar(acc[:, t], src, gate, None, ALU.mult).then_inc(work_dve, 1)
                        else:
                            dve.wait_ge(work_dve, freed(u, wk, ("out", (n - 1,))))
                            nc.vector.scalar_tensor_tensor(acc[:, t], src, gate, acc[:, t], ALU.mult, ALU.add)\
                                .then_inc(work_dve, 1)
                    elif kind == "out_stats":
                        t, = args
                        dve.wait_ge(work_dve, freed(u, wk, ("out", (t * S.E0 + S.E0 - 1,))))
                        c.link(nc.vector.bn_stats(ostat[:], acc[:, t]))
                        apart(dve, tick)
                        c.link(nc.vector.bn_aggr(omv[:], ostat[:]))
                        nc.vector.tensor_scalar(ove[:], omv[:, 1:2], EPS_LN, None, ALU.add).then_inc(ovar, 1)
                    elif kind == "out_norm":
                        t, = args
                        dve.wait_ge(orstd_ready, GT * u + t + 1)
                        dve.wait_ge(ff_stored, 1 + 16 * (GT * u + t))
                        nc.vector.tensor_scalar(fo[:], acc[:, t], omv[:, 0:1], orstd[:, 0:1], ALU.subtract, ALU.mult)\
                            .then_inc(fo_ready, 1)
                    elif kind == "gate":
                        e, = args
                        dve.wait_ge(tanh_done, NE * u + e + 1)
                        nc.vector.scalar_tensor_tensor(gh[e % 2][:], th[e % 2][:], 1.0, bank(wk, step, u)[:], ALU.add, ALU.mult)\
                            .then_inc(work_dve, 1)
                    elif kind == "up":
                        e, = args
                        dve.wait_ge(work_full, filled(u, wk, step))
                        dve.wait_ge(work_dve, freed(u, wk, ("gate", args)))
                        dve.wait_ge(work_full, filled(u, wk, ("down", (e - 2, 1))) if e >= 2 else wbase(u))
                        nc.vector.tensor_tensor(hT[e % 2][:], gh[e % 2][:], bank(wk, step, u)[:], ALU.mult)\
                            .then_inc(work_dve, 1)
                    elif kind == "down":
                        e, h = args
                        dve.wait_ge(work_full, filled(u, wk, step))
                        if e == 0:
                            dve.wait_ge(ff_stored, 1 + 16 * u)
                        else:
                            dve.wait_ge(work_dve, freed(u, wk, ("down", (e - 1, h))))
                        for n in range(2):
                            t = 2 * h + n
                            src = bank(wk, step, u)[:, n * C:(n + 1) * C]
                            g = 0.5 if e >= S.E1 else coef[:, bass.ds(GT * u + t, 1), e:e + 1].rearrange("p a b -> p (a b)")
                            if e == 0:
                                last = nc.vector.tensor_scalar(acc[:, t], src, g, None, ALU.mult)
                            else:
                                last = nc.vector.scalar_tensor_tensor(acc[:, t], src, g, acc[:, t], ALU.mult, ALU.add)
                            if n == 0:
                                last.then_inc(tick, 1)
                        last.then_inc(work_dve, 1)
                if plan is first:
                    assert c.steps == base_first, c.steps
                if plan is full:
                    assert c.steps == per_full, (c.steps, per_full)

            slots(dve, body)

        @block.tensor
        def _(pe):
            pe.sem_inc(value_done, PROBS)
            pe.wait_ge(w_in, 16 * WLOADS)

            def body(plan, u, parity):
                wk = works[id(plan)]
                nxt = 1 - parity
                ahead = (1 + u) if u is not None else 0
                last = None
                for step in plan:
                    kind, args = step
                    if kind == "score":
                        g, kt, j, m = args
                        q0 = max(0, kt - GT * g) * P
                        if m == 0:
                            pe.wait_ge(work_dve, 1 + W0.count["dve"] + u * W1.count["dve"])
                        pe.wait_ge(exp_done, NM * u + m + 1)
                        dst = score_b[m % SCORE_BANKS]
                        keys = KZ[parity][:, j, kt * P:(kt + 1) * P]
                        last = nc.tensor.matmul(dst[:, q0:TOK], keys,
                                                QT[parity][:, 0 if stack else j, g * TOK + q0:(g + 1) * TOK],
                                                start=True, stop=kt < GT * g)
                        if kt >= GT * g:
                            last = nc.tensor.matmul(dst[:, q0:q0 + P], keep["identb"][:], keep["mask_kq"][:],
                                                    start=False, stop=True)
                        last.then_inc(score_full, 1)
                    elif kind == "value":
                        g, kt, j, m = args
                        q0 = max(0, kt - GT * g) * P
                        if kt == 0 and j == 0:
                            pe.wait_ge(sums_taken, S.GB * u + g + 1)
                        pe.wait_ge(exp_done, SCORE_BANKS + NM * u + m + 1)
                        last = nc.tensor.matmul(sums_b[SLOT * j:SLOT * (j + 1), q0:TOK],
                                                V[parity][:, kt, SLOT * j:SLOT * (j + 1)],
                                                probs[m % PROBS][:, q0:TOK],
                                                start=kt == 0, stop=kt == GT * (g + 1) - 1)
                        last.then_inc(value_done, 1)
                    elif kind == "peak":
                        g, t, j, ch, k = args
                        w = TOK if ch < g else (t + 1) * P
                        if k == 0:
                            pe.wait_ge(unit_in, 16 * LOADS * (ahead + 1))
                        pe.wait_ge(peak_taken, NX * ahead + k + 1)
                        dst = max_b[k % MAX_BANKS]
                        qt = (g * GT + t) * P
                        last = nc.tensor.matmul(dst[:, 0:w], QT[nxt][:, 0 if stack else j, qt:qt + P],
                                                KZ[nxt][:, j, ch * TOK:ch * TOK + w], start=True, stop=ch < g)
                        if ch == g:
                            last = nc.tensor.matmul(dst[:, w - P:w], keep["identb"][:], keep["mask_qk"][:],
                                                    start=False, stop=True)
                        last.then_inc(peak_full, 1)
                    elif kind == "turn_q":
                        g, h = args
                        pe.wait_ge(shift_ready, S.GB * ahead + g + 1)
                        wait_work_free(pe, u, wk, step)
                        dst = bank(wk, step, u)[:].bitcast(BF16)
                        for jj in range(1 if stack else 2):
                            for t in range(GT):
                                rows = QA[nxt][:, g * GT + t, (2 * h + jj) * P:(2 * h + jj + 1) * P]
                                last = nc.tensor.transpose(dst[:, jj * TOK + t * P:jj * TOK + (t + 1) * P], rows,
                                                           keep["identb"][:])
                        last.then_inc(work_full, 1)
                    elif kind == "turn_out":
                        g, = args
                        pe.wait_ge(sums_taken, S.GB * u + g + 2)
                        wait_work_free(pe, u, wk, step)
                        for t in range(GT):
                            last = nc.tensor.transpose(bank(wk, step, u)[:, t * P:(t + 1) * P],
                                                       sumsT[:, t * P:(t + 1) * P], keep["ident"][:])
                        last.then_inc(work_full, 1)
                    elif kind == "hidden":
                        n, = args
                        t, e = divmod(n, S.E0)
                        if n == 0:
                            pe.wait_ge(group_in[parity], 8 * u - 8 * parity + 16)
                        wait_work_free(pe, u, wk, step)
                        for k in range(KC):
                            last = nc.tensor.matmul(bank(wk, step, u)[:], XT[parity][:, k, t * P:(t + 1) * P],
                                                    w1[:, k, e, :], start=(k == 0), stop=(k == KC - 1))
                        last.then_inc(work_full, 1)
                    elif kind == "turn_hidden":
                        n, = args
                        pe.wait_ge(hid_ready, NE * u + n + 1)
                        wait_work_free(pe, u, wk, step)
                        for k in range(S.F0 // P):
                            last = nc.tensor.transpose(bank(wk, step, u)[:, k * P:(k + 1) * P],
                                                       hn[n % 2][:, k * P:(k + 1) * P], keep["ident"][:])
                        last.then_inc(work_full, 1)
                    elif kind == "out":
                        n, = args
                        e = n % S.E0
                        pe.wait_ge(work_act, freed(u, wk, ("turn_hidden", args), "act"))
                        wait_work_free(pe, u, wk, step)
                        for k in range(S.F0 // P):
                            last = nc.tensor.matmul(bank(wk, step, u)[:, 0:C], hT[n % 2][:, k], w2[:, e, k, :],
                                                    start=(k == 0), stop=(k == S.F0 // P - 1))
                        last.then_inc(work_full, 1)
                    elif kind in ("gate", "up"):
                        e, = args
                        w = wg if kind == "gate" else wu
                        if e == 0:
                            pe.wait_ge(group_in[parity], 8 * u - 8 * parity + 16)
                        wait_work_free(pe, u, wk, step)
                        for k in range(KC):
                            last = nc.tensor.matmul(bank(wk, step, u)[:], w[:, k, e * P:(e + 1) * P], XT[parity][:, k],
                                                    start=(k == 0), stop=(k == KC - 1))
                        last.then_inc(work_full, 1)
                    elif kind == "down":
                        e, h = args
                        if h == 0:
                            pe.wait_ge(work_dve, freed(u, wk, ("up", (e,))))
                        wait_work_free(pe, u, wk, step)
                        for n in range(2):
                            t = 2 * h + n
                            last = nc.tensor.matmul(bank(wk, step, u)[:, n * C:(n + 1) * C], hT[e % 2][:, t * P:(t + 1) * P],
                                                    wd[:, e, :], start=True, stop=True)
                        last.then_inc(work_full, 1)
                pe.drain().then_inc(slot_done, 1)

            slots(pe, body)


def stage_layer0(nc, a, S, keep, d):
    stage_layer(nc, a, S, keep, d, 0)


def stage_layer1(nc, a, S, keep, d):
    stage_layer(nc, a, S, keep, d, 1)


def stage_mid(nc, a, S, keep, d):
    H, HD, KC, C, E = S.H, S.HD, S.KC, S.C, S.E1
    HT = GT * H
    NQ = 2 * C
    SCALE = HD ** -0.5
    with ExitStack() as ctx:
        pool = Pools(nc, ctx, "mid")
        sb, psum, sem = pool.sb, pool.psum, pool.sem
        wnat = sb("wnat", [P, (NQ + C) // P, C])
        wqk = sb("wqk", [P, KC, NQ])
        wk2r = sb("wk2r", [P, KC, C + E])
        wo = sb("wo", [P, KC, C])
        bias = sb("bias", [P, NQ + C])
        half = sb("half", [P, GT])
        yg = sb("yg", [P, GT, C])
        yT = sb("yT", [P, KC, GT, P])
        xg = sb("xg", [P, GT, C])
        fg = sb("fg", [P, GT, C])
        x1 = sb("x1", [P, GT, C])
        stat, mv, ve, rstd = sb("stat", [P, GT, 6]), sb("mv", [P, GT, 2]), sb("ve", [P, GT]), sb("rstd", [P, GT])
        xn = sb("xn", [P, GT, C])
        xnT = sb("xnT", [P, KC, GT, P])
        va = sb("va", [P, GT, H, SLOT])
        qk = sb("qk", [P, 2, GT, C])
        k2 = sb("k2", [P, GT, C])
        qal = sb("qal", [P, GT, C])
        kal = sb("kal", [P, GT, C])
        part = [sb(f"part{n}", [P, 2, HT, HD], BF16) for n in range(3)]
        QA = sb("QA", [P, HT, P], BF16)
        KA = sb("KA", [P, HT, P], BF16)
        QT = sb("QT", [P, H, TOK], BF16)
        KT = sb("KT", [P, H, TOK], BF16)
        rl = sb("rl", [P, S.TILES, E])
        big = [sb(f"big{n}", [P, S.TILES, E]) for n in range(4)]
        big.insert(1, rl)
        row = [sb(f"row{n}", [P, S.TILES]) for n in range(3)]
        pT = [psum(f"pT{t}") for t in range(GT)]
        pP = [psum(f"pP{t}") for t in range(GT)]

        w_in, loaded, seen, set_up = sem("w_in"), sem("loaded"), sem("seen"), sem("set_up")
        w_turned, w_taken = sem("w_turned"), sem("w_taken")
        yT_psum, yT_ready, wo_done = sem("yT_psum"), sem("yT_ready"), sem("wo_done")
        x1_ready, var_ready, rstd_ready = sem("x1_ready"), sem("var_ready"), sem("rstd_ready")
        xn_ready, xnT_psum, xnT_ready, va_ready = sem("xn_ready"), sem("xnT_psum"), sem("xnT_ready"), sem("va_ready")
        proj_done, qk_taken, k2_ready, kal_ready = sem("proj_done"), sem("qk_taken"), sem("k2_ready"), sem("kal_ready")
        qal_ready, parts_ready, qa_ready, ka_ready = sem("qal_ready"), sem("parts_ready"), sem("qa_ready"), sem("ka_ready")
        turned, q_taken, k_taken = sem("turned"), sem("q_taken"), sem("k_taken")
        stored, chain, tick, yg_ready = sem("stored"), sem("chain"), sem("tick"), sem("yg_ready")
        gate_exp, logits = sem("gate_exp"), sem("logits")

        LOADS = S.HG + 2
        STORES = 7 + 2 * S.HG
        NW = (NQ + C) // P

        block = ctx.enter_context(nc.Block())

        @block.sync
        def _(sp):
            xt = a["L0_attn_x"].rearrange("b t c -> (b t) c").rearrange("(n p) c -> p n c", p=P)

            def load(g):
                tiles = bass.ds(g * GT, GT)
                for hg in range(S.HG):
                    w = C // S.HG
                    sp.dma_start(yg[:, :, hg * w:(hg + 1) * w], d["y0"][hg][:, tiles, :]).then_inc(loaded, 16)
                sp.dma_start(xg[:], xt[:, tiles, :]).then_inc(loaded, 16)
                sp.dma_start(fg[:], d["ff0"][:, tiles, :]).then_inc(loaded, 16)

            sp.sem_inc(stored, 1)
            load(0)

            def group(it, more):
                tiles, tok = bass.ds(it * GT, GT), bass.ds(it * TOK, TOK)

                def store(out, src):
                    sp.dma_start(out, src).then_inc(stored, 16)

                sp.wait_ge(seen, it + 1)
                apart(sp, tick)
                if more:
                    load(it + 1)
                store(d["x1"][:, tiles, :], x1[:])
                sp.wait_ge(xn_ready, it * GT + GT)
                apart(sp, tick)
                store(d["xn1"][0:S.TILES * P, :].rearrange("(n p) c -> p n c", p=P)[:, tiles, :], xn[:])
                sp.wait_ge(va_ready, it + 1)
                apart(sp, tick)
                store(d["va1"][:, tiles, :], va[:].rearrange("p t h n -> p t (h n)"))
                sp.wait_ge(xnT_ready, it * GT + GT)
                apart(sp, tick)
                store(d["xnT1"].rearrange("k p t -> p k t")[:, :, tok], xnT[:].rearrange("p k t j -> p k (t j)"))
                sp.wait_ge(qal_ready, it + 1)
                apart(sp, tick)
                store(d["qal"][:, tiles, :], qal[:])
                sp.wait_ge(kal_ready, it + 1)
                apart(sp, tick)
                store(d["kal"][:, tiles, :], kal[:])
                sp.wait_ge(qa_ready, it + 1)
                apart(sp, tick)
                store(d["qa1"][:, tiles, :], QA[:].rearrange("p (t h) n -> p t (h n)", t=GT))
                sp.wait_ge(q_taken, 1 + 8 * it + 8)
                apart(sp, tick)
                for hg in range(S.HG):
                    store(d["qT1"][hg][:, :, tok], QT[:, 4 * hg:4 * hg + 4, :])
                sp.wait_ge(k_taken, 1 + 8 * it + 8)
                apart(sp, tick)
                for hg in range(S.HG):
                    store(d["kT1"][hg][:, :, tok], KT[:, 4 * hg:4 * hg + 4, :])

            with sp.Fori(0, S.G - 1) as it:
                group(it, True)
            group(S.G - 1, False)
            sp.dma_start(d["xn1"][S.TILES * P:S.TILES * P + 1, :], xn[0:1, 0, :]).then_inc(stored, 16)
            sp.wait_ge(stored, 1 + 16 * (STORES * S.G + 1))

        @block.gpsimd
        def _(pool_e):
            def load(out, src):
                pool_e.dma_start(out, src).then_inc(w_in, 16)

            load(wnat[:, 0:NQ // P, :], a["L1_attn_w_attn"].rearrange("(n p) c -> p n c", p=P))
            load(wnat[:, NQ // P:, :], a["L1_attn_w_k2"].rearrange("(n p) c -> p n c", p=P))
            load(wk2r[:, :, C:], a["L1_ffn_router"].rearrange("(k p) e -> p k e", p=P))
            load(wo[:], a["L0_attn_wo"].rearrange("(k p) c -> p k c", p=P))
            load(bias[:, 0:NQ], a["L1_attn_b_attn"].partition_broadcast(P))
            load(bias[:, NQ:], a["L1_attn_b_k2"].partition_broadcast(P))
            nc.gpsimd.memset(half[:], -0.5).then_inc(set_up, 1)
            nc.gpsimd.memset(va[:], 0.0).then_inc(set_up, 1)
            nc.gpsimd.memset(QA[:], 0.0).then_inc(set_up, 1)
            nc.gpsimd.memset(KA[:], 0.0).then_inc(set_up, 1)
            pool_e.wait_ge(set_up, 4)
            nc.gpsimd.memset(va[:, :, :, HD:HD + 1], 1.0).then_inc(set_up, 1)
            nc.gpsimd.memset(KA[:, :, 6 * HD:6 * HD + 2], 1.0).then_inc(set_up, 1)
            with pool_e.Fori(0, S.G) as it:
                pool_e.wait_ge(var_ready, it + 1)
                nc.gpsimd.tensor_tensor(rstd[:], ve[:], half[:], ALU.pow).then_inc(rstd_ready, 1)

        STEPS = GT * 2 + 8

        @block.vector
        def _(dve):
            dve.sem_inc(qk_taken, 1)
            dve.sem_inc(k_taken, 1)
            dve.wait_ge(w_in, 16 * 6)
            dve.wait_ge(set_up, 6)
            with dve.Fori(0, S.G) as it:
                c = Chain(dve, chain, it * STEPS)
                dve.wait_ge(loaded, 16 * LOADS * (it + 1))
                dve.wait_ge(stored, 1 + 16 * STORES * it)
                c.link(nc.vector.tensor_tensor(x1[:], xg[:], fg[:], ALU.add))
                for t in range(GT):
                    dve.wait_ge(wo_done, GT * it + t + 1)
                    nc.vector.tensor_tensor(x1[:, t], pP[t][:, 0:C], x1[:, t], ALU.add).then_inc(x1_ready, 1)
                dve.wait_ge(x1_ready, GT * it + GT)
                dve.sem_inc(seen, 1)
                for t in range(GT):
                    c.step(nc.vector.bn_stats(stat[:, t, :], x1[:, t]))
                c.settle()
                apart(dve, tick)
                for t in range(GT):
                    c.step(nc.vector.bn_aggr(mv[:, t, :], stat[:, t, :]))
                c.settle()
                nc.vector.tensor_scalar(ve[:], mv[:, :, 1], EPS_LN, None, ALU.add).then_inc(var_ready, 1)
                dve.wait_ge(rstd_ready, it + 1)
                for t in range(GT):
                    nc.vector.tensor_scalar(xn[:, t, :], x1[:, t], mv[:, t, 0:1], rstd[:, t:t + 1],
                                            ALU.subtract, ALU.mult).then_inc(xn_ready, 1)
                for t in range(GT):
                    dve.wait_ge(proj_done, GT * it + t + 1)
                    c_qk = nc.vector.tensor_tensor(qk[:, :, t, :], pP[t][:].rearrange("p (s n) -> p s n", s=2),
                                                   bias[:, 0:NQ].rearrange("p (s n) -> p s n", s=2), ALU.add)
                    c_qk.then_inc(tick, 1)
                    nc.vector.tensor_tensor(k2[:, t, :], pT[t][:, 0:C], bias[:, NQ:], ALU.add).then_inc(k2_ready, 1)
                    nc.vector.tensor_copy(rl[:, bass.ds(it * GT + t, 1), :].rearrange("p a c -> p (a c)"),
                                          pT[t][:, C:C + E]).then_inc(qk_taken, 1)
                dve.wait_ge(qk_taken, 1 + GT * it + GT)
                c.link(nc.vector.tensor_scalar(qk[:, 0], qk[:, 0], SCALE, None, ALU.mult))
                nc.vector.scalar_tensor_tensor(qal[:], qk[:, 0], 0.02, qk[:, 0], ALU.mult, ALU.min).then_inc(qal_ready, 1)
                q = qk[:].rearrange("p s t (h e) -> p s (t h) e", e=HD)
                c.link(nc.vector.tensor_copy(part[0][:], q))
                dve.wait_ge(qal_ready, it + 1)
                c.link(nc.vector.tensor_tensor(q, q, part[0][:], ALU.subtract))
                c.link(nc.vector.tensor_copy(part[1][:], q))
                c.link(nc.vector.tensor_tensor(q, q, part[1][:], ALU.subtract))
                nc.vector.tensor_copy(part[2][:], q).then_inc(parts_ready, 1)
                dve.wait_ge(parts_ready, it + 1)
                kslot = KA[:, :, 0:6 * HD].rearrange("p n (s e) -> p n s e", e=HD)
                c.step(nc.vector.tensor_copy(kslot[:, :, 0:6:3, :], part[0][:, 1].unsqueeze(2).broadcast_to([P, HT, 2, HD])))
                c.step(nc.vector.tensor_copy(kslot[:, :, 1:5:3, :], part[1][:, 1].unsqueeze(2).broadcast_to([P, HT, 2, HD])))
                nc.vector.tensor_copy(kslot[:, :, 5, :], part[0][:, 1]).then_inc(tick, 1)
                c.settle()
                nc.vector.tensor_copy(kslot[:, :, 2, :], part[2][:, 1]).then_inc(ka_ready, 1)
                for n in range(8):
                    dve.wait_ge(turned, 16 * it + 2 * n + 2)
                    nc.vector.tensor_copy(KT[:, 2 * n:2 * n + 2, :],
                                          pT[(2 * n + 1) % 4][:].bitcast(BF16).rearrange("p (g j) -> p g j", g=2))\
                        .then_inc(k_taken, 1)
                assert c.steps == STEPS, c.steps
            c = Chain(dve, chain, S.G * STEPS)
            top_two(nc, dve, c, S.TILES, E, big, row, gate_exp, logits, keep["gate1"], False)

        @block.scalar
        def _(act):
            act.sem_inc(q_taken, 1)
            for n in range(NW):
                act.wait_ge(w_turned, n + 1)
                dst = wqk[:, :, n * P:(n + 1) * P] if n < NQ // P else wk2r[:, :, (n - NQ // P) * P:(n - NQ // P + 1) * P]
                nc.scalar.copy(dst, pT[n % GT][:, 0:C].rearrange("p (k j) -> p k j", k=KC)).then_inc(w_taken, 1)
            act.wait_ge(set_up, 6)
            with act.Fori(0, S.G) as it:
                act.wait_ge(stored, 1 + 16 * STORES * it)
                for t in range(GT):
                    act.wait_ge(yT_psum, GT * it + t + 1)
                    nc.scalar.copy(yT[:, :, t, :], pT[t][:, 0:C].rearrange("p (k j) -> p k j", k=KC)).then_inc(yT_ready, 1)
                for t in range(GT):
                    act.wait_ge(xnT_psum, GT * it + t + 1)
                    nc.scalar.copy(xnT[:, :, t, :], pT[t][:, 0:C].rearrange("p (k j) -> p k j", k=KC)).then_inc(xnT_ready, 1)
                nc.scalar.copy(va[:, :, :, 0:HD], xn[:].rearrange("p t (h e) -> p t h e", e=HD)).then_inc(va_ready, 1)
                act.wait_ge(k2_ready, GT * it + GT)
                nc.scalar.activation(kal[:], k2[:], ACT.Sigmoid, scale=0.02 * SCALE).then_inc(kal_ready, 1)
                act.wait_ge(parts_ready, it + 1)
                qslot = QA[:, :, 0:6 * HD].rearrange("p n (s e) -> p n s e", e=HD)
                for lo, hi, n in ((0, 3, 0), (3, 5, 1)):
                    nc.scalar.copy(qslot[:, :, lo:hi, :], part[n][:, 0].unsqueeze(2).broadcast_to([P, HT, hi - lo, HD]))\
                        .then_inc(tick, 1)
                nc.scalar.copy(qslot[:, :, 5, :], part[2][:, 0]).then_inc(qa_ready, 1)
                for n in range(8):
                    act.wait_ge(turned, 16 * it + 2 * n + 1)
                    nc.scalar.copy(QT[:, 2 * n:2 * n + 2, :],
                                   pT[(2 * n) % 4][:].bitcast(BF16).rearrange("p (g j) -> p g j", g=2)).then_inc(q_taken, 1)
            act.wait_ge(logits, 1)
            nc.scalar.activation(big[3][:], big[2][:], ACT.Exp).then_inc(gate_exp, 1)

        @block.tensor
        def _(pe):
            pe.wait_ge(w_in, 16 * 6)
            for n in range(NW):
                if n >= GT:
                    pe.wait_ge(w_taken, n - GT + 1)
                for k in range(KC):
                    last = nc.tensor.transpose(pT[n % GT][:, k * P:(k + 1) * P], wnat[:, n, k * P:(k + 1) * P],
                                               keep["ident"][:])
                last.then_inc(w_turned, 1)
            pe.wait_ge(w_taken, NW)
            with pe.Fori(0, S.G) as it:
                pe.wait_ge(loaded, 16 * LOADS * (it + 1))
                pe.wait_ge(q_taken, 1 + 8 * it)
                pe.wait_ge(k_taken, 1 + 8 * it)
                for t in range(GT):
                    for k in range(KC):
                        last = nc.tensor.transpose(pT[t][:, k * P:(k + 1) * P], yg[:, t, k * P:(k + 1) * P], keep["ident"][:])
                    last.then_inc(yT_psum, 1)
                pe.wait_ge(qk_taken, 1 + GT * it)
                for t in range(GT):
                    pe.wait_ge(yT_ready, GT * it + t + 1)
                    for k in range(KC):
                        last = nc.tensor.matmul(pP[t][:, 0:C], yT[:, k, t, :], wo[:, k, :], start=(k == 0), stop=(k == KC - 1))
                    last.then_inc(wo_done, 1)
                for t in range(GT):
                    pe.wait_ge(xn_ready, GT * it + t + 1)
                    for k in range(KC):
                        last = nc.tensor.transpose(pT[t][:, k * P:(k + 1) * P], xn[:, t, k * P:(k + 1) * P], keep["ident"][:])
                    last.then_inc(xnT_psum, 1)
                for t in range(GT):
                    pe.wait_ge(xnT_ready, GT * it + t + 1)
                    for k in range(KC):
                        nc.tensor.matmul(pP[t][:], xnT[:, k, t, :], wqk[:, k, :], start=(k == 0), stop=(k == KC - 1))
                    for k in range(KC):
                        last = nc.tensor.matmul(pT[t][:, 0:C + E], xnT[:, k, t, :], wk2r[:, k, :],
                                                start=(k == 0), stop=(k == KC - 1))
                    last.then_inc(proj_done, 1)
                pe.wait_ge(qk_taken, 1 + GT * it + GT)
                pe.wait_ge(qa_ready, it + 1)
                pe.wait_ge(ka_ready, it + 1)
                for n in range(8):
                    for m, src in enumerate((QA, KA)):
                        if n >= 2:
                            pe.wait_ge(q_taken if m == 0 else k_taken, 1 + 8 * it + n - 1)
                        bank = pT[(2 * n + m) % 4][:].bitcast(BF16)
                        for j in range(2):
                            for t in range(GT):
                                last = nc.tensor.transpose(bank[:, j * TOK + t * P:j * TOK + (t + 1) * P],
                                                           src[:, t * H + 2 * n + j, :], keep["identb"][:])
                        last.then_inc(turned, 1)


def stage_final(nc, a, S, keep, d):
    H, HD, KC, C = S.H, S.HD, S.KC, S.C
    HH = P // HD
    NB = H // 4
    UNROLL = 4
    LOADS = 6
    LAST = S.TILES - 1
    with ExitStack() as ctx:
        pool = Pools(nc, ctx, "final")
        sb, psum, sem = pool.sb, pool.psum, pool.sem

        def two(name, shape):
            return [sb(f"{name}{n}", shape) for n in range(2)]

        def four(name):
            return [sb(f"{name}{n}", [P, C]) for n in range(UNROLL)]

        wnat = sb("wnat", [P, KC, C])
        wT = sb("wT", [P, KC, C])
        bias2 = sb("bias2", [P, C])
        heads = sb("heads", [P, KC, HH])
        causal = sb("causal", [P, P])
        carry = sb("carry", [P, S.TILES])
        state = sb("state", [P, KC, HH, HD])
        grown = sb("grown", [P, KC, HH, HD])
        q_in, k_in, y_in, xs_in, x_in, f_in = (four("q_in"), four("k_in"), four("y_in"), four("xs_in"),
                                               four("x_in"), four("f_in"))
        qT, kT = two("qT", [P, KC, P]), two("kT", [P, KC, P])
        qz = two("qz", [P, KC, HH, P])
        at = two("at", [P, H, P])
        e = two("e", [P, C])
        yt = two("yt", [P, C])
        yT = two("yT", [P, KC, P])
        rest = two("rest", [P, C])
        o = two("o", [P, C])
        turn_b, out_b, state_b, proj_b = psum("turn_b"), psum("out_b"), psum("state_b"), psum("proj_b")
        prod_b = [psum(f"prod_b{n}") for n in range(NB)]

        w_in, set_up, bias_ready = sem("w_in"), sem("set_up"), sem("bias_ready")
        w_turned, w_taken, tick = sem("w_turned"), sem("w_taken"), sem("tick")
        loaded = [sem(f"loaded{n}") for n in range(UNROLL)]
        stored = [sem(f"stored{n}") for n in range(2)]
        turned, turned_taken, qz_ready = sem("turned"), sem("turned_taken"), sem("qz_ready")
        prod_full, prod_taken, e_ready = sem("prod_full"), sem("prod_taken"), sem("e_ready")
        out_full, yt_ready = sem("out_full"), sem("yt_ready")
        state_full, grown_ready, state_ready = sem("state_full"), sem("grown_ready"), sem("state_ready")
        yt_turned, yT_ready, proj_full, o_ready = sem("yt_turned"), sem("yT_ready"), sem("proj_full"), sem("o_ready")
        sum_ready, rest_ready = sem("sum_ready"), sem("rest_ready")


        def tile(i, k):
            return UNROLL * i + k, k % 2, (UNROLL // 2) * i + k // 2

        block = ctx.enter_context(nc.Block())

        @block.sync
        def _(sp):
            out_rows = d["out"].rearrange("b t c -> (b t) c")

            def load(i, k):
                n, m = UNROLL * i + k, k % UNROLL
                one = bass.ds(n, 1)
                for buf, name in ((q_in, "qal"), (k_in, "kal"), (x_in, "x1"), (f_in, "ff1")):
                    sp.dma_start(buf[m][:], d[name][:, one, :].rearrange("p a c -> p (a c)")).then_inc(loaded[m], 16)
                sp.dma_start(y_in[m][:].rearrange("p (g c) -> p g c", g=S.HG),
                             d["y1"][:, :, one, :].rearrange("g p a c -> p g (a c)")).then_inc(loaded[m], 16)
                sp.dma_start(xs_in[m][:], d["xn1"][bass.ds(n * P + 1, P), :]).then_inc(loaded[m], 16)

            def refill(i, k):
                n, _, _ = tile(i, k)
                sp.wait_ge(rest_ready, n + 1)
                apart(sp, tick)
                sp.wait_ge(yt_ready, 1 + n + 1)
                apart(sp, tick)
                load(i, k + UNROLL)

            def store(i, k):
                n, par, _ = tile(i, k)
                sp.wait_ge(o_ready, 2 + n + 1)
                apart(sp, tick)
                sp.dma_start(out_rows[bass.ds(n * P, P), :], o[par][:]).then_inc(stored[par], 16)

            for par in range(2):
                sp.sem_inc(stored[par], 1)
            for k in range(UNROLL):
                load(0, k)
            with sp.Fori(0, S.TILES // UNROLL - 1) as i:
                for k in range(UNROLL):
                    refill(i, k)
                    store(i, k)
            for k in range(S.TILES - UNROLL, S.TILES):
                store(0, k)
            for par in range(2):
                sp.wait_ge(stored[par], 1 + 16 * (S.TILES // 2))

        @block.gpsimd
        def _(pool_e):
            pool_e.dma_start(wnat[:], a["L1_attn_w_proj"].rearrange("(n p) c -> p n c", p=P)).then_inc(w_in, 16)
            pool_e.dma_start(bias2[:], a["L1_attn_b_proj"].partition_broadcast(P)).then_inc(w_in, 16)
            nc.gpsimd.memset(causal[:], 1.0).then_inc(set_up, 1)
            nc.gpsimd.memset(heads[:], 1.0).then_inc(set_up, 1)
            nc.gpsimd.memset(carry[:], 1.0).then_inc(set_up, 1)
            nc.gpsimd.memset(state[:], 0.0).then_inc(set_up, 1)
            pool_e.wait_ge(set_up, 4)
            nc.gpsimd.affine_select(out=causal[:], in_=causal[:], compare_op=ALU.is_gt, fill=0.0, base=0,
                                    pattern=[[1, P]], channel_multiplier=-1).then_inc(set_up, 1)
            nc.gpsimd.affine_select(out=heads[:], in_=heads[:], compare_op=ALU.is_ge, fill=0.0, base=0,
                                    pattern=[[0, KC], [-HD, HH]], channel_multiplier=1).then_inc(set_up, 1)
            pool_e.wait_ge(set_up, 6)
            nc.gpsimd.affine_select(out=heads[:], in_=heads[:], compare_op=ALU.is_ge, fill=0.0, base=HD - 1,
                                    pattern=[[0, KC], [HD, HH]], channel_multiplier=-1).then_inc(set_up, 1)
            for b in range(S.B):
                end = (b + 1) * S.TB - 1
                nc.gpsimd.memset(carry[:, end:end + 1], 0.0).then_inc(set_up, 1)
            pool_e.wait_ge(w_in, 32)
            nc.gpsimd.tensor_tensor(bias2[:], bias2[:], bias2[:], ALU.add).then_inc(bias_ready, 1)
            pool_e.wait_ge(bias_ready, 1)
            pool_e.wait_ge(set_up, 7 + S.B)

            with pool_e.Fori(0, S.TILES // UNROLL) as i:
                for k in range(UNROLL):
                    n, par, _ = tile(i, k)
                    pool_e.wait_ge(turned_taken, 2 + 2 * n + 2)
                    pool_e.wait_ge(prod_full, NB * n + NB)
                    for f in range(KC):
                        nc.gpsimd.tensor_tensor(qz[par][:, f], qT[par][:, f].unsqueeze(1).broadcast_to([P, HH, P]),
                                                heads[:, f].unsqueeze(2).broadcast_to([P, HH, P]), ALU.mult)\
                            .then_inc(qz_ready, 1)
                    pool_e.wait_ge(loaded[k], 16 * LOADS * (i + 1))
                    nc.gpsimd.tensor_tensor(x_in[k][:], x_in[k][:], f_in[k][:], ALU.add).then_inc(sum_ready, 1)
                    pool_e.wait_ge(sum_ready, n + 1)
                    pool_e.wait_ge(o_ready, n + 1)
                    nc.gpsimd.tensor_tensor(rest[par][:], x_in[k][:], bias2[:], ALU.add).then_inc(rest_ready, 1)

        @block.vector
        def _(dve):
            dve.sem_inc(prod_taken, NB)
            dve.sem_inc(yt_ready, 1)
            dve.sem_inc(grown_ready, 1)
            dve.sem_inc(state_ready, 1)
            dve.sem_inc(o_ready, 2)
            dve.wait_ge(set_up, 7 + S.B)

            def errors(i, k):
                n, par, _ = tile(i, k)
                m = k % UNROLL
                dve.wait_ge(loaded[m], 16 * LOADS * (i + k // UNROLL + 1))
                dve.wait_ge(out_full, n + 1)
                nc.vector.tensor_tensor(e[par][:], xs_in[m][:], y_in[m][:], ALU.subtract).then_inc(e_ready, 1)

            def mask(i, k):
                n, par, _ = tile(i, k)
                dve.wait_ge(out_full, n + 1)
                for b in range(NB):
                    dve.wait_ge(prod_full, 2 * NB + NB * n + b + 1)
                    nc.vector.tensor_tensor(at[par][:, 4 * b:4 * b + 4, :], prod_b[b][:].rearrange("p (h t) -> p h t", h=4),
                                            causal[:].unsqueeze(1).broadcast_to([P, 4, P]), ALU.mult)\
                        .then_inc(prod_taken, 1)

            def values(i, k):
                n, par, _ = tile(i, k)
                dve.wait_ge(out_full, 2 + n + 1)
                dve.wait_ge(yt_turned, n + 1)
                nc.vector.tensor_tensor(yt[par][:], out_b[:, 0:C], y_in[k % UNROLL][:], ALU.add).then_inc(yt_ready, 1)
                dve.wait_ge(state_full, n + 1)
                dve.wait_ge(state_ready, 1 + n)
                nc.vector.tensor_tensor(grown[:].rearrange("p f h c -> p (f h c)"), state_b[:, 0:C],
                                        state[:].rearrange("p f h c -> p (f h c)"), ALU.add).then_inc(grown_ready, 1)
                dve.wait_ge(grown_ready, 1 + n + 1)
                nc.vector.scalar_tensor_tensor(state[:].rearrange("p f h c -> p (f h) c"),
                                               grown[:].rearrange("p f h c -> p (f h) c"), carry[:, bass.ds(n, 1)],
                                               heads[:].rearrange("p f h -> p (f h)").unsqueeze(2)
                                               .broadcast_to([P, H, HD]),
                                               ALU.mult, ALU.mult).then_inc(state_ready, 1)

            def finish(i, k):
                n, par, before = tile(i, k)
                dve.wait_ge(proj_full, 2 + n + 1)
                dve.wait_ge(rest_ready, n + 1)
                dve.wait_ge(stored[par], 1 + 16 * before)
                nc.vector.tensor_tensor(o[par][:], proj_b[:, 0:C], rest[par][:], ALU.add).then_inc(o_ready, 1)

            def step(i, k):
                errors(i, k + 1)
                values(i, k)
                mask(i, k + 1)
                finish(i, k - 1)

            errors(0, 0)
            mask(0, 0)
            errors(0, 1)
            values(0, 0)
            mask(0, 1)
            with dve.Fori(0, (S.TILES - UNROLL) // UNROLL) as i:
                for k in range(1, UNROLL + 1):
                    step(i, k)
            for n in range(S.TILES - UNROLL + 1, LAST):
                step(0, n)
            values(0, LAST)
            finish(0, LAST - 1)
            finish(0, LAST)

        @block.scalar
        def _(act):
            act.sem_inc(turned_taken, 2)
            act.wait_ge(w_turned, 1)
            nc.scalar.copy(wT[:], prod_b[0][:].rearrange("p (k n) -> p k n", k=KC)).then_inc(w_taken, 1)

            def turn(i, k):
                n, par, _ = tile(i, k)
                act.wait_ge(turned, n + 1)
                act.wait_ge(out_full, n + 1)
                nc.scalar.copy(qT[par][:], turn_b[:, 0:C].rearrange("p (f t) -> p f t", f=KC)).then_inc(turned_taken, 1)
                nc.scalar.copy(kT[par][:], turn_b[:, C:2 * C].rearrange("p (f t) -> p f t", f=KC)).then_inc(turned_taken, 1)

            def turn_y(i, k):
                n, par, _ = tile(i, k)
                act.wait_ge(yt_turned, 2 + n + 1)
                act.wait_ge(proj_full, n + 1)
                nc.scalar.copy(yT[par][:], proj_b[:, C:2 * C].rearrange("p (f t) -> p f t", f=KC)).then_inc(yT_ready, 1)

            for k in range(3):
                turn(0, k)
            with act.Fori(0, (S.TILES - UNROLL) // UNROLL) as i:
                for k in range(1, UNROLL + 1):
                    turn_y(i, k - 1)
                    turn(i, k + 2)
            turn_y(0, LAST - 3)
            turn(0, LAST)
            for n in range(LAST - 2, LAST + 1):
                turn_y(0, n)

        @block.tensor
        def _(pe):
            pe.sem_inc(out_full, 2)
            pe.sem_inc(prod_full, 2 * NB)
            pe.sem_inc(yt_turned, 2)
            pe.sem_inc(proj_full, 2)
            pe.wait_ge(w_in, 32)
            for k in range(KC):
                for m in range(KC):
                    last = nc.tensor.transpose(prod_b[0][:, k * C + m * P:k * C + (m + 1) * P],
                                               wnat[:, m, k * P:(k + 1) * P], keep["ident"][:])
            last.then_inc(w_turned, 1)
            pe.wait_ge(w_taken, 1)

            def turn(i, k):
                n, par, _ = tile(i, k)
                m = k % UNROLL
                pe.wait_ge(loaded[m], 16 * LOADS * (i + k // UNROLL + 1))
                pe.wait_ge(turned_taken, 2 + 2 * n)
                for s, rows in enumerate((q_in[m], k_in[m])):
                    for f in range(KC):
                        last = nc.tensor.transpose(turn_b[:, s * C + f * P:s * C + (f + 1) * P],
                                                   rows[:, f * P:(f + 1) * P], keep["ident"][:])
                last.then_inc(turned, 1)

            def products(i, k):
                n, par, _ = tile(i, k)
                for b in range(NB):
                    f, h = divmod(4 * b, HH)
                    if h == 0:
                        pe.wait_ge(qz_ready, 2 * n + f + 1)
                    pe.wait_ge(prod_taken, NB * n + b + 1)
                    nc.tensor.matmul(prod_b[b][:], kT[par][:, f], qz[par][:, f, h:h + 4, :],
                                     start=True, stop=True).then_inc(prod_full, 1)

            def values(i, k):
                n, par, _ = tile(i, k)
                pe.wait_ge(e_ready, n + 1)
                pe.wait_ge(grown_ready, 1 + n)
                for f in range(KC):
                    half = slice(f * P, (f + 1) * P)
                    last = nc.tensor.matmul(state_b[:, half], k_in[k % UNROLL][:, half], e[par][:, half],
                                            start=True, stop=True)
                last.then_inc(state_full, 1)
                pe.wait_ge(state_ready, 1 + n)
                pe.wait_ge(yt_ready, 1 + n)
                for f in range(KC):
                    half = slice(f * P, (f + 1) * P)
                    nc.tensor.matmul(out_b[:, half], qT[par][:, f], state[:, f], start=True, stop=False)
                    if f == 0:
                        pe.wait_ge(prod_taken, NB + NB * n + NB)
                    for h in range(f * HH, (f + 1) * HH):
                        cols = slice(h * HD, (h + 1) * HD)
                        last = nc.tensor.matmul(out_b[:, cols], at[par][:, h, :], e[par][:, cols],
                                                start=False, stop=h % HH == HH - 1)
                last.then_inc(out_full, 1)

            def turn_y(i, k):
                n, par, _ = tile(i, k)
                pe.wait_ge(yt_ready, 1 + n + 1)
                pe.wait_ge(o_ready, 2 + n)
                for f in range(KC):
                    last = nc.tensor.transpose(proj_b[:, C + f * P:C + (f + 1) * P], yt[par][:, f * P:(f + 1) * P],
                                               keep["ident"][:])
                last.then_inc(yt_turned, 1)

            def project(i, k):
                n, par, _ = tile(i, k)
                pe.wait_ge(yT_ready, n + 1)
                for f in range(KC):
                    last = nc.tensor.matmul(proj_b[:, 0:C], yT[par][:, f], wT[:, f], start=(f == 0), stop=(f == KC - 1))
                last.then_inc(proj_full, 1)

            turn(0, 0)
            turn(0, 1)
            products(0, 0)
            values(0, 0)
            turn(0, 2)
            products(0, 1)
            with pe.Fori(0, (S.TILES - UNROLL) // UNROLL) as i:
                for k in range(1, UNROLL + 1):
                    turn_y(i, k - 1)
                    values(i, k)
                    turn(i, k + 2)
                    products(i, k + 1)
                    project(i, k - 1)
            for n in range(LAST - 2, LAST + 1):
                turn_y(0, n - 1)
                values(0, n)
                if n + 2 <= LAST:
                    turn(0, n + 2)
                if n + 1 <= LAST:
                    products(0, n + 1)
                project(0, n - 1)
            turn_y(0, LAST)
            project(0, LAST)


STAGES = [stage_prep0, stage_layer0, stage_mid, stage_layer1, stage_final]


def build(nc, a, out):
    S = Shapes(a)
    nc.disable_value_cache = True
    HG, NT, TK = S.HG, S.TILES, S.TILES * P
    d = {
        "xnT0": scratch(nc, "xnT0", (S.KC, P, TK), F32),
        "va0": scratch(nc, "va0", (P, NT, S.H * SLOT), F32),
        "qa0": scratch(nc, "qa0", (P, NT, S.H * SLOT), BF16),
        "qT0": scratch(nc, "qT0", (HG, P, TK), BF16),
        "kT0": scratch(nc, "kT0", (HG, P, TK), BF16),
        "y0": scratch(nc, "y0", (HG, P, NT, 4 * S.HD), F32),
        "ff0": scratch(nc, "ff0", (P, NT, S.C), F32),
        "x1": scratch(nc, "x1", (P, NT, S.C), F32),
        "xnT1": scratch(nc, "xnT1", (S.KC, P, TK), F32),
        "va1": scratch(nc, "va1", (P, NT, S.H * SLOT), F32),
        "qa1": scratch(nc, "qa1", (P, NT, S.H * P), BF16),
        "qT1": scratch(nc, "qT1", (HG, P, 4, TK), BF16),
        "kT1": scratch(nc, "kT1", (HG, P, 4, TK), BF16),
        "y1": scratch(nc, "y1", (HG, P, NT, 4 * S.HD), F32),
        "ff1": scratch(nc, "ff1", (P, NT, S.C), F32),
        "qal": scratch(nc, "qal", (P, NT, S.C), F32),
        "kal": scratch(nc, "kal", (P, NT, S.C), F32),
        "xn1": scratch(nc, "xn1", (TK + 1, S.C), F32),
    }
    with ExitStack() as ctx:
        def sb(name, shape, dt=F32):
            return ctx.enter_context(nc.sbuf_tensor(name, shape, dt))
        keep = {
            "ident": sb("ident", [P, P]), "identb": sb("identb", [P, P], BF16),
            "mask_qk": sb("mask_qk", [P, P], BF16), "mask_kq": sb("mask_kq", [P, P], BF16),
            "gate0": sb("gate0", [P, NT, S.E0]), "gate1": sb("gate1", [P, NT, S.E1]),
        }
        d["out"] = out
        for stage in STAGES:
            stage(nc, a, S, keep, d)


def kernel(**inputs):
    import numpy as _np
    import concourse.bacc as _bacc
    from concourse import mybir as _mybir
    from concourse.bass_utils import run_bass_kernel_spmd as _run

    nc = _bacc.Bacc("TRN2", target_bir_lowering=False, num_devices=1)
    arrays, args = {}, {}
    for name, value in inputs.items():
        v = _np.ascontiguousarray(value)
        arrays[f"in_{name}"] = v
        args[name] = nc.dram_tensor(f"in_{name}", v.shape, _mybir.dt.from_np(v.dtype), kind="ExternalInput").ap()
    shape = inputs["L0_attn_x"].shape
    out = nc.dram_tensor("out_0", shape, F32, kind="ExternalOutput").ap()
    build(nc, args, out)
    r = _run(nc, [arrays], core_ids=[0])
    return r.results[0]["out_0"]
```

```python
from contextlib import ExitStack

import concourse.bass as bass
from concourse import mybir

ALU = mybir.AluOpType
ACT = mybir.ActivationFunctionType
F32 = mybir.dt.float32
BF16 = mybir.dt.bfloat16
AX_X = mybir.AxisListType.X

P = 128
EPS_LN = 1e-5
EPS_GATE = 1e-8
MASKED = -3.0e38
GT = 4
TOK = GT * P
SLOT = 32


def scratch(nc, name, shape, dt):
    return nc.dram_tensor(name, shape, dt).ap()


class Pools:

    def __init__(self, nc, ctx, stage):
        self.nc, self.ctx, self.stage = nc, ctx, stage

    def sb(self, name, shape, dt=F32):
        return self.ctx.enter_context(self.nc.sbuf_tensor(f"{self.stage}_{name}", shape, dt))

    def psum(self, name, shape=(P, 512), dt=F32):
        return self.ctx.enter_context(self.nc.psum_tensor(f"{self.stage}_{name}", list(shape), dt))

    def sem(self, name):
        return self.ctx.enter_context(self.nc.semaphore(f"{self.stage}_{name}"))


class Chain:

    def __init__(self, engine, sem, start=0):
        self.engine, self.sem, self.start, self.steps = engine, sem, start, 0

    def step(self, instruction):
        instruction.then_inc(self.sem, 1)
        self.steps += 1
        return self.steps

    def settle(self):
        self.engine.wait_ge(self.sem, self.start + self.steps)

    def link(self, instruction):
        self.step(instruction)
        self.settle()


class Shapes:
    def __init__(self, a):
        self.B, self.T, self.C = a["L0_attn_x"].shape
        self.H = a["L0_attn_head_dirs"].shape[0]
        self.D3 = a["L0_attn_head_dirs"].shape[1]
        self.HD = self.C // self.H
        self.KC = self.C // P
        self.TILES = self.B * self.T // P
        self.TB = self.T // P
        self.G = self.TILES // GT
        self.GB = self.TB // GT
        self.HG = self.H // 4
        self.E0, _, self.F0 = a["L0_ffn_w1"].shape
        self.E1, _, self.F1 = a["L1_ffn_experts_gate"].shape


def apart(engine, tick):
    engine.sem_inc(tick, 1)


def make_identity(eng, nc, m, sem, base):
    nc.gpsimd.memset(m, 0.0).then_inc(sem, 1)
    eng.wait_ge(sem, base + 1)
    nc.gpsimd.affine_select(out=m, in_=m, compare_op=ALU.not_equal, fill=1.0, base=0,
                            pattern=[[-1, P]], channel_multiplier=1).then_inc(sem, 1)


def stage_prep0(nc, a, S, keep, d):
    H, D3, HD, KC, C = S.H, S.D3, S.HD, S.KC, S.C
    W3 = H * D3
    NP = 2 * W3 + C + S.E0
    V0, R0 = 2 * W3, 2 * W3 + C
    with ExitStack() as ctx:
        pool = Pools(nc, ctx, "prep0")
        sb, psum, sem = pool.sb, pool.psum, pool.sem
        x_all = sb("x_all", [P, S.TILES, C])
        wp = sb("wp", [P, KC, NP])
        rwT = sb("rwT", [P, KC, S.E0])
        rgb = sb("rgb", [P, 2, KC])
        gbw = sb("gbw", [P, KC, 2 * S.E0])
        ones = sb("ones", [P, P])
        GB = sb("GB", [P, 2 * S.E0])
        dirs = sb("dirs", [P, W3])
        scl = sb("scl", [P, 1])
        half = sb("half", [P, S.TILES])
        stat = sb("stat", [P, GT, 6])
        mv = sb("mv", [P, GT, 2])
        ve = sb("ve", [P, GT])
        rstd = sb("rstd", [P, GT])
        stat2 = sb("stat2", [P, GT, 6])
        mvg = sb("mvg", [P, GT, 2])
        mv2 = sb("mv2", [P, S.TILES, 2])
        rl = sb("rl", [P, S.TILES, S.E0])
        xn = sb("xn", [P, GT, C])
        xnT = sb("xnT", [P, KC, GT, P])
        va = sb("va", [P, GT, H, SLOT])
        qk = sb("qk", [P, 2, GT * H, D3])
        sc1 = sb("sc1", [P, GT * H, D3])
        sc2 = sb("sc2", [P, GT * H])
        part = [sb(f"part{n}", [P, 2, GT * H, D3], BF16) for n in range(3)]
        QA = sb("QA", [P, GT * H, SLOT], BF16)
        KA = sb("KA", [P, GT * H, SLOT], BF16)
        QT = sb("QT", [P, S.HG, TOK], BF16)
        KT = sb("KT", [P, S.HG, TOK], BF16)
        big = [sb(f"big{n}", [P, S.TILES, S.E0]) for n in range(5)]
        row = [sb(f"row{n}", [P, S.TILES]) for n in range(3)]
        pT = [psum(f"pT{t}") for t in range(GT)]
        pP = [psum(f"pP{t}") for t in range(GT)]

        first_loaded, loaded, weights = sem("first_loaded"), sem("loaded"), sem("weights")
        pool_set, ones_set = sem("pool_set"), sem("ones_set")
        var_ready, rstd_ready = sem("var_ready"), sem("rstd_ready")
        xn_ready, xnT_psum, xnT_ready = sem("xn_ready"), sem("xnT_psum"), sem("xnT_ready")
        proj_done, qk_taken, v_taken = sem("proj_done"), sem("qk_taken"), sem("v_taken")
        parts_ready, ka_ready, qa_ready = sem("parts_ready"), sem("ka_ready"), sem("qa_ready")
        turned, turned_taken = sem("turned"), sem("turned_taken")
        rows_stored, q_stored, turned_stored = sem("rows_stored"), sem("q_stored"), sem("turned_stored")
        chain, gate_exp, logits, gb_psum = sem("chain"), sem("gate_exp"), sem("logits"), sem("gb_psum")
        last_rstd = sem("last_rstd")
        tick = sem("tick")

        HEAD = 8
        NORM = 4 * GT + 2
        STEPS = GT * 5 + 13

        block = ctx.enter_context(nc.Block())

        @block.sync
        def _(sp):
            for stored in (rows_stored, q_stored, turned_stored):
                sp.sem_inc(stored, 1)
            xt = a["L0_attn_x"].rearrange("b t c -> (b t) c").rearrange("(n p) c -> p n c", p=P)
            for g in range(S.G):
                sp.dma_start(x_all[:, g * GT:(g + 1) * GT], xt[:, g * GT:(g + 1) * GT])\
                    .then_inc(loaded if g else first_loaded, 16)
            sp.wait_ge(weights, 16 * 9)
            with nc.allow_non_contiguous_dma(reason="the experts' norms turned, a few KB once"):
                load_experts0(sp, a, keep)

            def store_rows(it):
                sp.wait_ge(xnT_ready, GT * it + GT)
                apart(sp, tick)
                sp.dma_start(d["xnT0"].rearrange("k p t -> p k t")[:, :, bass.ds(it * TOK, TOK)],
                             xnT[:].rearrange("p k t j -> p k (t j)")).then_inc(rows_stored, 16)
                sp.wait_ge(v_taken, 1 + GT * it + GT)
                apart(sp, tick)
                sp.dma_start(d["va0"][:, bass.ds(it * GT, GT), :],
                             va[:].rearrange("p t h n -> p t (h n)")).then_inc(rows_stored, 16)

            def store_turned(it):
                tok = bass.ds(it * TOK, TOK)
                sp.wait_ge(turned_taken, 1 + 4 * it + 4)
                apart(sp, tick)
                sp.dma_start(d["qT0"].rearrange("g p t -> p g t")[:, :, tok], QT[:]).then_inc(turned_stored, 16)
                sp.dma_start(d["kT0"].rearrange("g p t -> p g t")[:, :, tok], KT[:]).then_inc(turned_stored, 16)

            def store_q(it):
                sp.wait_ge(qa_ready, it + 1)
                apart(sp, tick)
                sp.dma_start(d["qa0"][:, bass.ds(it * GT, GT), :],
                             QA[:].rearrange("p (t h) n -> p t (h n)", t=GT)).then_inc(q_stored, 16)

            store_rows(0)
            store_q(0)
            with sp.Fori(1, S.G) as it:
                store_rows(it)
                store_turned(it - 1)
                store_q(it)
            store_turned(S.G - 1)
            sp.wait_ge(rows_stored, 1 + 32 * S.G)
            sp.wait_ge(q_stored, 1 + 16 * S.G)
            sp.wait_ge(turned_stored, 1 + 32 * S.G)

        @block.gpsimd
        def _(pool_e):
            pool_e.sem_inc(ka_ready, 1)
            pool_e.dma_start(wp[:, :, 0:W3], a["L0_attn_wq"].rearrange("(k p) n -> p k n", p=P)).then_inc(weights, 16)
            pool_e.dma_start(wp[:, :, W3:2 * W3], a["L0_attn_wk"].rearrange("(k p) n -> p k n", p=P)).then_inc(weights, 16)
            pool_e.dma_start(wp[:, :, V0:R0], a["L0_attn_wv"].rearrange("(k p) n -> p k n", p=P)).then_inc(weights, 16)
            with nc.allow_non_contiguous_dma(reason="the router's weights turned, a few KB once"):
                for k in range(KC):
                    pool_e.dma_start(rwT[:, k, :], a["L0_ffn_router_w"].rearrange("e (k p) -> p k e", p=P)[:, k, :])\
                        .then_inc(weights, 16)
                pool_e.dma_start(rgb[:, 0, :], a["L0_ffn_rn_g"].rearrange("(k p) -> p k", p=P)).then_inc(weights, 16)
                pool_e.dma_start(rgb[:, 1, :], a["L0_ffn_rn_b"].rearrange("(k p) -> p k", p=P)).then_inc(weights, 16)
            pool_e.dma_start(dirs[:], a["L0_attn_head_dirs"].rearrange("h d -> (h d)").partition_broadcast(P))\
                .then_inc(weights, 16)
            pool_e.dma_start(scl[:], a["L0_attn_scale"].partition_broadcast(P)).then_inc(weights, 16)
            nc.gpsimd.memset(ones[:], 1.0).then_inc(ones_set, 1)
            nc.gpsimd.memset(half[:], -0.5).then_inc(ones_set, 1)
            make_identity(pool_e, nc, keep["ident"][:], pool_set, 0)
            make_identity(pool_e, nc, keep["identb"][:], pool_set, 2)
            nc.gpsimd.memset(keep["mask_qk"][:], 0.0).then_inc(pool_set, 1)
            nc.gpsimd.memset(keep["mask_kq"][:], 0.0).then_inc(pool_set, 1)
            pool_e.wait_ge(pool_set, 6)
            nc.gpsimd.affine_select(out=keep["mask_qk"][:], in_=keep["mask_qk"][:], compare_op=ALU.is_ge,
                                    fill=MASKED, base=0, pattern=[[-1, P]], channel_multiplier=1).then_inc(pool_set, 1)
            nc.gpsimd.affine_select(out=keep["mask_kq"][:], in_=keep["mask_kq"][:], compare_op=ALU.is_ge,
                                    fill=MASKED, base=0, pattern=[[1, P]], channel_multiplier=-1).then_inc(pool_set, 1)
            nc.gpsimd.memset(va[:], 0.0).then_inc(pool_set, 1)
            nc.gpsimd.memset(QA[:], 0.0).then_inc(pool_set, 1)
            nc.gpsimd.memset(KA[:], 0.0).then_inc(pool_set, 1)
            pool_e.wait_ge(pool_set, 11)
            nc.gpsimd.memset(va[:, :, :, HD:HD + 1], 1.0).then_inc(pool_set, 1)
            nc.gpsimd.memset(KA[:, :, 27:29], 1.0).then_inc(pool_set, 1)

            def group(it, last):
                if not last:
                    pool_e.wait_ge(var_ready, it + 2)
                    nc.gpsimd.tensor_tensor(rstd[:], ve[:], half[:, 0:GT], ALU.pow).then_inc(rstd_ready, 1)
                pool_e.wait_ge(parts_ready, it + 1)
                pool_e.wait_ge(turned, 1 + 4 * it)
                apart(pool_e, tick)
                for b in range(3):
                    dst = KA[:, :, 0:27].rearrange("p n (a b d) -> p n a b d", a=3, b=3)[:, :, :, b, :]
                    src = part[b][:, 1].unsqueeze(2).broadcast_to([P, GT * H, 3, D3])
                    nc.gpsimd.tensor_copy(dst, src).then_inc(ka_ready, 1)

            pool_e.wait_ge(var_ready, 1)
            nc.gpsimd.tensor_tensor(rstd[:], ve[:], half[:, 0:GT], ALU.pow).then_inc(rstd_ready, 1)
            with pool_e.Fori(0, S.G - 1) as it:
                group(it, False)
            group(S.G - 1, True)
            pool_e.wait_ge(var_ready, S.G + 1)
            nc.gpsimd.tensor_tensor(row[1][:], row[0][:], half[:], ALU.pow).then_inc(last_rstd, 1)

        @block.vector
        def _(dve):
            dve.sem_inc(qk_taken, 1)
            dve.wait_ge(weights, 16 * 9)
            c = Chain(dve, chain)
            for k in range(KC):
                for n in range(2):
                    c.step(nc.vector.tensor_scalar(gbw[:, k, n * S.E0:(n + 1) * S.E0], rwT[:, k, :],
                                                   rgb[:, n, k:k + 1], None, ALU.mult))
            for k in range(KC):
                c.step(nc.vector.tensor_scalar(wp[:, k, R0:NP], rwT[:, k, :], rgb[:, 0, k:k + 1], None, ALU.mult))
            dve.wait_ge(gb_psum, 1)
            c.step(nc.vector.tensor_copy(GB[:], pP[0][:, 0:2 * S.E0]))
            c.link(nc.vector.memset(rl[:], 0.0))
            assert c.steps == HEAD
            dve.wait_ge(first_loaded, 16)
            dve.wait_ge(ones_set, 2)
            dve.wait_ge(pool_set, 13)

            def variances(it, c):
                for t in range(GT):
                    c.step(nc.vector.bn_stats(stat[:, t, :], x_all[:, bass.ds(it * GT + t, 1), :]
                                              .rearrange("p a c -> p (a c)")))
                c.settle()
                apart(dve, tick)
                for t in range(GT):
                    c.step(nc.vector.bn_aggr(mv[:, t, :], stat[:, t, :]))
                c.settle()
                c.step(nc.vector.tensor_scalar(ve[:], mv[:, :, 1], EPS_LN, None, ALU.add))
                c.settle()
                dve.sem_inc(var_ready, 1)

            def normalise(it):
                dve.wait_ge(rstd_ready, it + 1)
                for t in range(GT):
                    nc.vector.tensor_scalar(xn[:, t, :], x_all[:, bass.ds(it * GT + t, 1), :].rearrange("p a c -> p (a c)"),
                                            mv[:, t, 0:1], rstd[:, t:t + 1], ALU.subtract, ALU.mult).then_inc(xn_ready, 1)

            def router_moments(it, c):
                dve.wait_ge(xn_ready, GT * it + GT)
                for t in range(GT):
                    c.step(nc.vector.bn_stats(stat2[:, t, :], xn[:, t, :]))
                c.settle()
                apart(dve, tick)
                for t in range(GT):
                    c.step(nc.vector.bn_aggr(mvg[:, t, :], stat2[:, t, :]))
                c.settle()
                c.step(nc.vector.tensor_copy(mv2[:, bass.ds(it * GT, GT), :], mvg[:]))

            def group(it, last):
                c = Chain(dve, chain, HEAD + NORM + it * STEPS)
                if not last:
                    variances(it + 1, c)
                for t in range(GT):
                    dve.wait_ge(proj_done, GT * it + t + 1)
                    c.step(nc.vector.tensor_copy(
                        qk[:].rearrange("p s (t h) e -> p s t (h e)", t=GT)[:, :, t, :],
                        pP[t][:, 0:2 * W3].rearrange("p (s n) -> p s n", s=2)))
                    nc.vector.tensor_copy(rl[:, bass.ds(it * GT + t, 1), :].rearrange("p a c -> p (a c)"),
                                          pP[t][:, R0:NP]).then_inc(qk_taken, 1)
                c.settle()
                if not last:
                    normalise(it + 1)
                q4 = qk[:, 0].rearrange("p (t h) e -> p t (h e)", t=GT)
                dir4 = dirs[:].unsqueeze(1).broadcast_to([P, GT, W3])
                s4 = sc1[:].rearrange("p (t h) e -> p t (h e)", t=GT)
                c.link(nc.vector.tensor_tensor(s4, q4, dir4, ALU.mult))
                c.link(nc.vector.tensor_reduce(sc2[:], sc1[:], AX_X, ALU.add))
                c.link(
                    nc.vector.tensor_tensor(
                        s4.rearrange("p t (h e) -> p t h e", e=D3),
                        sc2[:].rearrange("p (t h) -> p t h", t=GT).unsqueeze(3).broadcast_to([P, GT, H, D3]),
                        dirs[:].rearrange("p (h e) -> p h e", e=D3).unsqueeze(1).broadcast_to([P, GT, H, D3]),
                        ALU.mult))
                c.link(nc.vector.scalar_tensor_tensor(qk[:, 0], qk[:, 0], scl[:, 0:1], sc1[:], ALU.mult, ALU.add))
                dve.wait_ge(ka_ready, 1 + 3 * it)
                c.link(nc.vector.tensor_copy(part[0][:], qk[:]))
                c.link(nc.vector.tensor_tensor(qk[:], qk[:], part[0][:], ALU.subtract))
                c.link(nc.vector.tensor_copy(part[1][:], qk[:]))
                c.link(nc.vector.tensor_tensor(qk[:], qk[:], part[1][:], ALU.subtract))
                c.step(nc.vector.tensor_copy(part[2][:], qk[:]))
                c.settle()
                dve.sem_inc(parts_ready, 1)
                dve.wait_ge(turned, 1 + 4 * it)
                dve.wait_ge(q_stored, 1 + 16 * it)
                for p in range(3):
                    dst = QA[:, :, 9 * p:9 * p + 9].rearrange("p n (b d) -> p n b d", b=3)
                    src = part[p][:, 0].unsqueeze(2).broadcast_to([P, GT * H, 3, D3])
                    if p < 2:
                        c.step(nc.vector.tensor_copy(dst, src))
                    else:
                        c.settle()
                        nc.vector.tensor_copy(dst, src).then_inc(qa_ready, 1)
                if not last:
                    router_moments(it + 1, c)
                    assert c.steps == STEPS, c.steps

            c = Chain(dve, chain, HEAD)
            variances(0, c)
            normalise(0)
            router_moments(0, c)
            assert c.steps == NORM
            dve.wait_ge(loaded, 16 * (S.G - 1))
            with dve.Fori(0, S.G - 1) as it:
                group(it, False)
            group(S.G - 1, True)

            E = S.E0
            c = Chain(dve, chain, HEAD + S.G * STEPS)
            mu2, var2 = mv2[:, :, 0], mv2[:, :, 1]
            c.link(nc.vector.tensor_scalar(row[0][:], var2, EPS_LN, None, ALU.add))
            dve.sem_inc(var_ready, 1)
            be = lambda v: v.unsqueeze(1).broadcast_to([P, S.TILES, E])
            bt = lambda v: v.unsqueeze(2).broadcast_to([P, S.TILES, E])
            c.link(nc.vector.tensor_tensor(big[0][:], bt(mu2), be(GB[:, 0:E]), ALU.mult))
            c.link(nc.vector.tensor_tensor(big[1][:], rl[:], big[0][:], ALU.subtract))
            dve.wait_ge(last_rstd, 1)
            c.link(nc.vector.tensor_tensor(big[0][:], big[1][:], bt(row[1][:]), ALU.mult))
            c.link(nc.vector.tensor_tensor(big[1][:], big[0][:], be(GB[:, E:2 * E]), ALU.add))
            top_two(nc, dve, c, S.TILES, E, big, row, gate_exp, logits, keep["gate0"], True)

        @block.scalar
        def _(act):
            act.sem_inc(turned_taken, 1)
            act.sem_inc(v_taken, 1)
            act.wait_ge(pool_set, 13)

            def rows(it):
                act.wait_ge(rows_stored, 1 + 32 * it)
                for t in range(GT):
                    act.wait_ge(xnT_psum, GT * it + t + 1)
                    nc.scalar.copy(xnT[:, :, t, :], pT[t][:, 0:C].rearrange("p (k j) -> p k j", k=KC))\
                        .then_inc(xnT_ready, 1)
                for t in range(GT):
                    act.wait_ge(proj_done, GT * it + t + 1)
                    act.wait_ge(qk_taken, 1 + GT * it + t + 1)
                    nc.scalar.copy(va[:, t, :, 0:HD], pP[t][:, V0:R0].rearrange("p (h e) -> p h e", e=HD))\
                        .then_inc(v_taken, 1)

            def take_turned(it):
                act.wait_ge(turned_stored, 1 + 32 * it)
                for n in range(2):
                    for m, dst in enumerate((QT, KT)):
                        act.wait_ge(turned, 1 + 4 * it + 2 * n + m + 1)
                        nc.scalar.copy(dst[:, 2 * n:2 * n + 2, :],
                                       pT[2 * n + m][:].bitcast(BF16).rearrange("p (g j) -> p g j", g=2))\
                            .then_inc(turned_taken, 1)

            rows(0)
            with act.Fori(1, S.G) as it:
                rows(it)
                take_turned(it - 1)
            take_turned(S.G - 1)
            act.wait_ge(logits, 1)
            nc.scalar.activation(big[3][:], big[2][:], ACT.Exp).then_inc(gate_exp, 1)

        @block.tensor
        def _(pe):
            pe.sem_inc(turned, 1)
            pe.wait_ge(ones_set, 2)
            pe.wait_ge(chain, 4)
            for k in range(KC):
                last = nc.tensor.matmul(pP[0][:, 0:2 * S.E0], ones[:], gbw[:, k, :], start=(k == 0), stop=(k == KC - 1))
            last.then_inc(gb_psum, 1)
            pe.wait_ge(chain, HEAD)
            pe.wait_ge(pool_set, 4)

            def project(it):
                for t in range(GT):
                    pe.wait_ge(xn_ready, GT * it + t + 1)
                    for k in range(KC):
                        last = nc.tensor.transpose(pT[t][:, k * P:(k + 1) * P], xn[:, t, k * P:(k + 1) * P],
                                                   keep["ident"][:])
                    last.then_inc(xnT_psum, 1)
                pe.wait_ge(qk_taken, 1 + GT * it)
                pe.wait_ge(v_taken, 1 + GT * it)
                for t in range(GT):
                    pe.wait_ge(xnT_ready, GT * it + t + 1)
                    for k in range(KC):
                        last = nc.tensor.matmul(pP[t][:, 0:NP], xnT[:, k, t, :], wp[:, k, :],
                                                start=(k == 0), stop=(k == KC - 1))
                    last.then_inc(proj_done, 1)

            def turn(it):
                pe.wait_ge(qa_ready, it + 1)
                pe.wait_ge(ka_ready, 1 + 3 * it + 3)
                for n in range(2):
                    for m, src in enumerate((QA, KA)):
                        bank = pT[2 * n + m][:].bitcast(BF16)
                        for g in range(2):
                            for t in range(GT):
                                rows = src[:].rearrange("p (t g h) n -> p t g (h n)", t=GT, g=S.HG)[:, t, 2 * n + g, :]
                                last = nc.tensor.transpose(bank[:, g * TOK + t * P:g * TOK + (t + 1) * P], rows,
                                                           keep["identb"][:])
                        last.then_inc(turned, 1)

            project(0)
            with pe.Fori(1, S.G) as it:
                pe.wait_ge(turned_taken, 4 * it - 3)
                project(it)
                turn(it - 1)
            pe.wait_ge(turned_taken, 1 + 4 * (S.G - 1))
            turn(S.G - 1)


def top_two(nc, dve, c, N, E, big, row, exp_done, logits_ready, gate, renormalise):
    bt = lambda v: v.unsqueeze(2).broadcast_to([P, N, E])
    c.link(nc.vector.tensor_reduce(row[2][:], big[1][:], AX_X, ALU.max))
    nc.vector.tensor_tensor(big[2][:], big[1][:], bt(row[2][:]), ALU.subtract).then_inc(logits_ready, 1)
    dve.wait_ge(exp_done, 1)
    c.link(nc.vector.tensor_reduce(row[0][:], big[3][:], AX_X, ALU.add))
    c.link(nc.vector.reciprocal(row[1][:], row[0][:]))
    c.link(nc.vector.tensor_tensor(big[0][:], big[3][:], bt(row[1][:]), ALU.mult))
    c.link(nc.vector.memset(big[1][:], 0.0))
    for f in range(E):
        for lo, hi, op in ((0, f, ALU.is_gt), (f + 1, E, ALU.is_ge)):
            if lo < hi:
                c.link(nc.vector.tensor_tensor(big[2][:, :, lo:hi], big[0][:, :, f:f + 1].broadcast_to([P, N, hi - lo]),
                                               big[0][:, :, lo:hi], op))
                c.link(nc.vector.tensor_tensor(big[1][:, :, lo:hi], big[1][:, :, lo:hi], big[2][:, :, lo:hi], ALU.add))
    out = big[4] if renormalise else gate
    c.link(nc.vector.scalar_tensor_tensor(out[:], big[1][:], 1.5, big[0][:], ALU.is_lt, ALU.mult))
    if renormalise:
        c.link(nc.vector.tensor_reduce(row[0][:], out[:], AX_X, ALU.add))
        c.link(nc.vector.tensor_scalar(row[2][:], row[0][:], EPS_GATE, None, ALU.add))
        c.link(nc.vector.reciprocal(row[1][:], row[2][:]))
        c.link(nc.vector.tensor_tensor(gate[:], out[:], bt(row[1][:]), ALU.mult))


SCORE_BANKS = 2
MAX_BANKS = 3
PROBS = 6
PEAKS = ((12.0, 154.0), (24.0, 154.0))
FIRST_PEAKS = (0.0, 154.0)
HID_STEP = 8.9
NORM_AT, TURN_AT, OUT_AT = 2.6, 16.0, 23.0
VALUE_LAG = 4.5
WORK_BANKS = 2


EMPTIES = {"turn_out": "dve", "turn_q": "dve", "hidden": "dve", "turn_hidden": "act", "out": "dve",
           "gate": "dve", "up": "dve", "down": "dve"}
LATER = {"dve": {"hidden": 1.2, "out": 1.2, "gate": 1.8, "up": 1.2, "down": 1.2}, "act": {"gate": 1.0}}


def slot_plan(S, attend, maxima, ffn, turns, peaks=(0.0, 150.0), experts_from=2.0):
    steps, m = [], 0
    if attend:
        for g in range(S.GB):
            for kt in range(GT * (g + 1)):
                for j in range(4):
                    steps.append((m, "score", (g, kt, j, m)))
                    steps.append((m + VALUE_LAG, "value", (g, kt, j, m)))
                    m += 1
            steps.append((m + VALUE_LAG - 0.99, "sums_out", (g,)))
            steps.append((m + VALUE_LAG + 3.01, "turn_out", (g,)))
    if maxima:
        k, n = 0, sum(4 * GT * (g + 1) for g in range(S.GB))
        for g in range(S.GB):
            for t in range(GT):
                for j in range(4):
                    for c in range(g + 1):
                        at = peaks[0] + k * (peaks[1] - peaks[0]) / n
                        steps.append((at, "peak", (g, t, j, c, k)))
                        k += 1
            steps.append((at + 0.01, "shift", (g,)))
            for h in range(turns):
                steps.append((at + 3.11 + 1.5 * h, "turn_q", (g, h)))
    if ffn == 0:
        for n in range(GT * S.E0):
            at = HID_STEP * n + experts_from + 0.3
            steps += [(at, "hidden", (n,)), (at + NORM_AT, "norm", (n,)), (at + TURN_AT, "turn_hidden", (n,)),
                      (at + TURN_AT + 1.1, "relu", (n,)), (at + OUT_AT, "out", (n,))]
            if n % S.E0 == S.E0 - 1:
                steps += [(at + OUT_AT + 1.3, "out_stats", (n // S.E0,)), (at + OUT_AT + 3.3, "out_norm", (n // S.E0,))]
    if ffn == 1:
        for e in range(S.E1 + S.KC):
            at = 15.8 * e + experts_from + 0.3
            steps += [(at, "gate", (e,)), (at + 3, "up", (e,)), (at + 9, "down", (e, 0)), (at + 12, "down", (e, 1))]
    held = [(at, at + NORM_AT + 0.01) for at, kind, _ in steps if kind == "hidden"]
    held += [(at, at + 1.11) for at, kind, _ in steps if kind == "turn_hidden"]
    for n, (at, kind, args) in enumerate(steps):
        if kind in ("turn_q", "turn_out"):
            for lo, hi in held:
                if lo < at < hi:
                    steps[n] = (hi + 0.001 * (at - lo), kind, args)
    return sorted(steps, key=lambda s: s[0])


class Plan:

    def __init__(self, steps):
        self.pe = [(kind, args) for _, kind, args in steps]
        filling = [(at, (kind, args)) for at, kind, args in steps if kind in EMPTIES]
        latest = {step: filling[n + WORK_BANKS][0] - 0.001 for n, (_, step) in enumerate(filling[:-WORK_BANKS])}
        for who in ("dve", "act"):
            later = LATER[who]
            order = []
            for n, (at, kind, args) in enumerate(steps):
                if kind in later:
                    at = max(at, min(at + later[kind], latest.get((kind, args), at + later[kind])))
                order.append((at, n, (kind, args)))
            order.sort()
            if who == "dve":
                self.dve = [step for _, _, step in order]
            else:
                self.act = [step for _, _, step in order]
        self.use, self.release, self.before = {}, {}, {}
        self.count = {"dve": 0, "act": 0}
        for n, (_, step) in enumerate(filling):
            self.use[step] = n
        for who, order in (("dve", self.dve), ("act", self.act)):
            for kind, args in order:
                step = ({"norm": "hidden", "relu": "turn_hidden"}.get(kind, kind), args)
                if step[0] in EMPTIES and EMPTIES[step[0]] == who and kind not in ("hidden", "turn_hidden"):
                    self.release[step] = self.count[who]
                    self.count[who] += 1
        for n, (_, step) in enumerate(filling):
            earlier = filling[n - WORK_BANKS][1] if n >= WORK_BANKS else None
            self.before[step] = (EMPTIES[earlier[0]], self.release[earlier]) if earlier else None
        self.total = len(filling)


def load_experts0(sp, a, keep):
    w1, w2, ln, ong, w_in = (keep[name] for name in ("w1", "w2", "ln", "ong", "w_in0"))
    for e in range(w1.shape[2]):
        sp.dma_start(w1[:, :, e, :], a["L0_ffn_w1"][e].rearrange("(k p) f -> p k f", p=P)).then_inc(w_in, 16)
        sp.dma_start(w2[:, e], a["L0_ffn_w2"][e].rearrange("(k p) c -> p k c", p=P)).then_inc(w_in, 16)
    sp.dma_start(ong[:, 0], a["L0_ffn_on_g"].partition_broadcast(P)).then_inc(w_in, 16)
    sp.dma_start(ong[:, 1], a["L0_ffn_on_b"].partition_broadcast(P)).then_inc(w_in, 16)
    for n, name in enumerate(("L0_ffn_ln_g", "L0_ffn_ln_b")):
        for e in range(w1.shape[2]):
            sp.dma_start(ln[:, n, e], a[name][e].rearrange("(k p) -> p k", p=P)).then_inc(w_in, 16)


def load_experts1(sp, a, keep):
    wg, wu, wd, w_in = (keep[name] for name in ("wg", "wu", "wd", "w_in1"))
    E = a["L1_ffn_experts_gate"].shape[0]
    for w, name, shared in ((wg, "L1_ffn_experts_gate", "L1_ffn_shared_gate"),
                            (wu, "L1_ffn_experts_up", "L1_ffn_shared_up")):
        for e in range(E):
            sp.dma_start(w[:, :, e * P:(e + 1) * P], a[name][e].rearrange("(k p) f -> p k f", p=P)).then_inc(w_in, 16)
        sp.dma_start(w[:, :, E * P:], a[shared].rearrange("(k p) f -> p k f", p=P)).then_inc(w_in, 16)
    sp.dma_start(wd[:, 0:E, :], a["L1_ffn_experts_down"].rearrange("e p c -> p e c")).then_inc(w_in, 16)
    sp.dma_start(wd[:, E:, :], a["L1_ffn_shared_down"].rearrange("(e p) c -> p e c", p=P)).then_inc(w_in, 16)


def stage_layer(nc, a, S, keep, d, layer):
    H, HD, KC, C = S.H, S.HD, S.KC, S.C
    stack = layer == 0
    qw = 1 if stack else 4
    hw = SLOT if stack else P
    m_row = 27 if stack else 96
    turns = 1 if stack else 2
    UNITS = S.HG * S.B
    T = S.T
    full = Plan(slot_plan(S, True, True, layer, turns, PEAKS[layer]))
    first = Plan(slot_plan(S, False, True, layer, turns, FIRST_PEAKS, 12.0))
    final = Plan(slot_plan(S, True, False, None, turns))
    NM = sum(1 for s in full.pe if s[0] == "score")
    NX = sum(1 for s in full.pe if s[0] == "peak")
    NE = GT * S.E0 if layer == 0 else S.E1 + KC
    PAIRS = (4 if stack else 1) + 1

    with ExitStack() as ctx:
        pool = Pools(nc, ctx, f"layer{layer}")
        sb, psum, sem = pool.sb, pool.psum, pool.sem
        KZ = [sb(f"KZ{n}", [P, 4, T], BF16) for n in range(2)]
        QT = [sb(f"QT{n}", [P, qw, T], BF16) for n in range(2)]
        QA = sb("QA", [P, S.TB, qw * P], BF16)
        V = [sb(f"V{n}", [P, S.TB, 4 * SLOT]) for n in range(2)]
        XT = [sb(f"XT{n}", [P, KC, TOK]) for n in range(2)]
        probs = [sb(f"probs{n}", [P, TOK]) for n in range(PROBS)]
        peaks = sb("peaks", [P, GT * 4, S.GB])
        nm = sb("nm", [P, GT * 4])
        sumsT = sb("sumsT", [P, TOK])
        inv = sb("inv", [P, GT * 4])
        y = sb("y", [P, GT, 4, HD])
        acc = sb("acc", [P, GT, C])
        if layer == 0:
            w1, w2, ln, ong = (keep[name] for name in ("w1", "w2", "ln", "ong"))
            half = sb("half", [P, 1])
            hstat, hmv, hve, hrstd = sb("hstat", [P, 6]), sb("hmv", [P, 2]), sb("hve", [P, 1]), sb("hrstd", [P, 1])
            ostat, omv, ove, orstd = sb("ostat", [P, 6]), sb("omv", [P, 2]), sb("ove", [P, 1]), sb("orstd", [P, 1])
            hn = [sb(f"hn{n}", [P, S.F0]) for n in range(2)]
            hT = [sb(f"hT{n}", [P, S.F0 // P, P]) for n in range(2)]
            fo = sb("fo", [P, C])
            w_in, WLOADS = keep["w_in0"], S.E0 * 4 + 2
        else:
            wg, wu, wd = keep["wg"], keep["wu"], keep["wd"]
            coef = sb("coef", [P, S.TILES, S.E1])
            th = [sb(f"th{n}", [P, TOK]) for n in range(2)]
            gh = [sb(f"gh{n}", [P, TOK]) for n in range(2)]
            hT = [sb(f"hT{n}", [P, TOK]) for n in range(2)]
            w_in, WLOADS = keep["w_in1"], 2 * S.E1 + 4
        score_b = [psum(f"score{n}") for n in range(SCORE_BANKS)]
        max_b = [psum(f"max{n}") for n in range(MAX_BANKS)]
        sums_b = psum("sums")
        work_b = [psum(f"work{n}") for n in range(WORK_BANKS)]

        pairs_in, rows_in = sem("pairs_in"), sem("rows_in")
        group_in = [sem(f"group_in{n}") for n in range(2)]
        slot_done = sem("slot_done")
        score_full, exp_done, value_done = sem("score_full"), sem("exp_done"), sem("value_done")
        sums_taken = sem("sums_taken")
        peak_full, peak_taken = sem("peak_full"), sem("peak_taken")
        shift_ready = sem("shift_ready")
        work_full, work_dve, work_act = sem("work_full"), sem("work_dve"), sem("work_act")
        y_stored = sem("y_stored")
        cleared = [sem(f"cleared{n}") for n in range(2)]
        chain, tick, setup = sem("chain"), sem("tick"), sem("setup")
        hvar, hrstd_ready = sem("hvar"), sem("hrstd_ready")
        ovar, orstd_ready, fo_ready, fo_done, ff_stored = (sem("ovar"), sem("orstd_ready"), sem("fo_ready"),
                                                           sem("fo_done"), sem("ff_stored"))
        fo_chain, tanh_done = sem("fo_chain"), sem("tanh_done")

        def wbase(u):
            return first.total + u * full.total if u is not None else 0

        def emptied(u, who):
            return 1 + (first.count[who] + u * full.count[who] if u is not None else 0)

        def wait_work_free(pe, u, plan, step):
            before = plan.before[step]
            if before is None:
                pe.wait_ge(work_dve, emptied(u, "dve"))
                pe.wait_ge(work_act, emptied(u, "act"))
            elif before[0] == "dve":
                pe.wait_ge(work_dve, emptied(u, "dve") + before[1] + 1)
            else:
                pe.wait_ge(work_act, emptied(u, "act") + before[1] + 1)

        def filled(u, plan, step):
            return 1 + plan.use[step] + wbase(u)

        def freed(u, plan, step, who="dve"):
            return emptied(u, who) + plan.release[step] + 1

        def bank(plan, step, u):
            return work_b[plan.use[step] % WORK_BANKS]

        assert first.total % WORK_BANKS == 0 and full.total % WORK_BANKS == 0

        def slots(engine, body):
            body(first, None, 1)
            with engine.Fori(0, UNITS // 2 - 1) as i:
                for parity in range(2):
                    body(full, 2 * i + parity, parity)
            body(full, UNITS - 2, 0)
            body(final, UNITS - 1, 1)

        block = ctx.enter_context(nc.Block())

        @block.sync
        def _(sp):
            def load_unit(hg, b):
                p = b
                rows = slice(b * T, (b + 1) * T)
                if stack:
                    for j in range(4):
                        sp.dma_start(KZ[p][SLOT * j:SLOT * (j + 1), j, :],
                                     d["kT0"][bass.ds(hg, 1), SLOT * j:SLOT * (j + 1), rows]
                                     .rearrange("a p t -> p (a t)")).then_inc(pairs_in, 16)
                    sp.dma_start(QT[p][:, 0, :], d["qT0"][bass.ds(hg, 1), :, rows].rearrange("a p t -> p (a t)"))\
                        .then_inc(pairs_in, 16)
                else:
                    sp.dma_start(KZ[p][:], d["kT1"][bass.ds(hg, 1), :, :, rows].rearrange("a p j t -> p (a j) t"))\
                        .then_inc(pairs_in, 16)
                    sp.dma_start(QT[p][:], d["qT1"][bass.ds(hg, 1), :, :, rows].rearrange("a p j t -> p (a j) t"))\
                        .then_inc(pairs_in, 16)
                tiles = slice(b * S.TB, (b + 1) * S.TB)
                sp.dma_start(QA[:], d[f"qa{layer}"][:, tiles, bass.ds(hg * qw * P, qw * P)]).then_inc(rows_in, 16)
                sp.dma_start(V[p][:], d[f"va{layer}"][:, tiles, bass.ds(hg * 4 * SLOT, 4 * SLOT)]).then_inc(rows_in, 16)

            def load_group(c, parity):
                sp.dma_start(XT[parity][:], d[f"xnT{layer}"].rearrange("k p t -> p k t")[:, :, bass.ds(c * TOK, TOK)])\
                    .then_inc(group_in[parity], 16)

            sp.sem_inc(y_stored, 1)
            sp.sem_inc(ff_stored, 1)
            if stack:
                sp.wait_ge(cleared[0], 1)
            load_unit(0, 0)
            load_group(0, 0)
            load_group(1, 1)
            if stack:
                sp.wait_ge(cleared[1], 1)

            def load_next(i, parity, group):
                sp.wait_ge(slot_done, 1 + 2 * i + parity)
                apart(sp, tick)
                if parity == 0:
                    load_unit(i, 1)
                else:
                    load_unit(i + 1, 0)
                if group:
                    load_group(2 * i + parity + 2, parity)

            def stores(plan, i, parity, u):
                c = (1 + u) if u is not None else 0
                for step in plan.dve:
                    kind, args = step
                    if kind == "turn_out":
                        g, = args
                        sp.wait_ge(work_dve, freed(u, plan, step))
                        apart(sp, tick)
                        sp.dma_start(d[f"y{layer}"][bass.ds(i, 1), :, parity * S.TB + g * GT:parity * S.TB + (g + 1) * GT, :]
                                     .rearrange("a p t n -> p (a t) n"),
                                     y[:].rearrange("p t h e -> p t (h e)")).then_inc(y_stored, 16)
                    elif kind == "out_norm":
                        t, = args
                        sp.wait_ge(fo_done, GT * c + t + 1)
                        apart(sp, tick)
                        sp.dma_start(d["ff0"][:, bass.ds(GT * c + t, 1), :].rearrange("p a c -> p (a c)"), fo[:])\
                            .then_inc(ff_stored, 16)
                if layer == 1 and plan is not final:
                    sp.wait_ge(work_dve, freed(u, plan, ("down", (NE - 1, 1))))
                    apart(sp, tick)
                    sp.dma_start(d["ff1"][:, bass.ds(GT * c, GT), :], acc[:]).then_inc(ff_stored, 16)

            stores(first, None, 1, None)
            with sp.Fori(0, UNITS // 2 - 1) as i:
                for parity in range(2):
                    load_next(i, parity, True)
                    stores(full, i, parity, 2 * i + parity)
            load_next(UNITS // 2 - 1, 0, False)
            stores(full, UNITS // 2 - 1, 0, UNITS - 2)
            stores(final, UNITS // 2 - 1, 1, UNITS - 1)
            sp.wait_ge(y_stored, 1 + 16 * S.GB * UNITS)
            sp.wait_ge(ff_stored, 1 + 16 * (GT * UNITS if layer == 0 else UNITS))

        @block.gpsimd
        def _(pool_e):
            if layer == 0:
                nc.gpsimd.memset(half[:], -0.5).then_inc(setup, 1)
                nc.gpsimd.memset(KZ[1][:], 0.0).then_inc(cleared[1], 1)
                pool_e.wait_ge(setup, 1)
                pool_e.wait_ge(w_in, 16 * WLOADS)

            def body(plan, u, parity):
                nxt = 1 - parity
                c = (1 + u) if u is not None else 0
                for step in plan.dve:
                    kind, args = step
                    if kind == "hidden":
                        n, = args
                        pool_e.wait_ge(hvar, NE * c + n + 1)
                        nc.gpsimd.tensor_tensor(hrstd[:], hve[:], half[:], ALU.pow).then_inc(hrstd_ready, 1)
                    elif kind == "out_stats":
                        t, = args
                        pool_e.wait_ge(ovar, GT * c + t + 1)
                        nc.gpsimd.tensor_tensor(orstd[:], ove[:], half[:], ALU.pow).then_inc(orstd_ready, 1)
                    elif kind == "out_norm":
                        t, = args
                        pool_e.wait_ge(fo_ready, GT * c + t + 1)
                        nc.gpsimd.tensor_tensor(fo[:], fo[:], ong[:, 0], ALU.mult).then_inc(fo_chain, 1)
                        pool_e.wait_ge(fo_chain, GT * c + t + 1)
                        nc.gpsimd.tensor_tensor(fo[:], fo[:], ong[:, 1], ALU.add).then_inc(fo_done, 1)

            if layer == 0:
                slots(pool_e, body)

        @block.scalar
        def _(act):
            act.sem_inc(exp_done, SCORE_BANKS)
            act.sem_inc(work_act, 1)
            if layer == 0:
                act.wait_ge(w_in, 16 * WLOADS)

            def relu(plan, u, n, half):
                e, parts = n % S.E0, S.F0 // P
                src = bank(plan, ("turn_hidden", (n,)), u)
                for k in range(half * parts // 2, (half + 1) * parts // 2):
                    last = nc.scalar.activation(hT[n % 2][:, k], src[:, k * P:(k + 1) * P], ACT.Relu,
                                                bias=ln[:, 1, e, k:k + 1], scale=ln[:, 0, e, k:k + 1])
                    last.then_inc(work_act if k == parts - 1 else tick, 1)

            def body(plan, u, parity):
                nxt = 1 - parity
                c = (1 + u) if u is not None else 0
                for step in plan.act:
                    kind, args = step
                    if kind == "score":
                        g, kt, j, m = args
                        q0 = max(0, kt - GT * g) * P
                        act.wait_ge(score_full, NM * u + m + 1)
                        act.wait_ge(value_done, NM * u + m + 1)
                        nc.scalar.activation(probs[m % PROBS][:, q0:TOK], score_b[m % SCORE_BANKS][:, q0:TOK], ACT.Exp)\
                            .then_inc(exp_done, 1)
                    elif kind == "turn_hidden":
                        n, = args
                        act.wait_ge(work_full, filled(u, plan, step))
                        if n >= 2 or u is not None:
                            act.wait_ge(work_full, filled(u, plan, ("out", (n - 2,))) if n >= 2 else wbase(u))
                        relu(plan, u, n, 0)
                    elif kind == "relu":
                        relu(plan, u, args[0], 1)
                    elif kind == "gate":
                        e, = args
                        act.wait_ge(work_full, filled(u, plan, step))
                        act.wait_ge(work_dve, freed(u, plan, ("gate", (e - 2,))) if e >= 2
                                    else emptied(u, "dve"))
                        nc.scalar.activation(th[e % 2][:], bank(plan, step, u)[:], ACT.Tanh, scale=0.5).then_inc(tanh_done, 1)

            slots(act, body)

        @block.vector
        def _(dve):
            if stack:
                nc.vector.memset(KZ[0][:], 0.0).then_inc(cleared[0], 1)
            dve.sem_inc(sums_taken, 1)
            dve.sem_inc(peak_taken, MAX_BANKS)
            dve.sem_inc(work_dve, 1)
            if layer == 1:
                nc.vector.tensor_scalar(coef[:], keep["gate1"][:], 0.5, None, ALU.mult).then_inc(setup, 1)
                dve.wait_ge(setup, 1)
            shift_steps = 2 * S.GB
            ffn_steps = (2 * NE + 2 * GT) if layer == 0 else 0
            out_steps = S.GB
            base_first = shift_steps + ffn_steps
            per_full = shift_steps + ffn_steps + out_steps

            def body(plan, u, parity):
                c = (1 + u) if u is not None else 0
                nxt = 1 - parity
                links = Chain(dve, chain, (base_first + u * per_full) if u is not None else 0)
                ahead = c
                for step in plan.dve:
                    kind, args = step
                    if kind == "peak":
                        g, t, j, ch, k = args
                        w = TOK if ch < g else (t + 1) * P
                        dve.wait_ge(peak_full, NX * ahead + k + 1)
                        nc.vector.tensor_reduce(peaks[:, 4 * t + j, ch:ch + 1], max_b[k % MAX_BANKS][:, 0:w], AX_X, ALU.max)\
                            .then_inc(peak_taken, 1)
                    elif kind == "shift":
                        g, = args
                        k_last = sum(4 * GT * (x + 1) for x in range(g + 1))
                        rows = QA[:].rearrange("p t (j n) -> p t j n", j=4)[:, g * GT:(g + 1) * GT]
                        nm3 = nm[:].rearrange("p (t j) -> p t j", j=4)
                        dve.wait_ge(peak_taken, MAX_BANKS + NX * ahead + k_last)
                        if g == 0:
                            dve.wait_ge(rows_in, 32 * (ahead + 1))
                        links.link(nc.vector.tensor_reduce(nm[:], peaks[:, :, 0:g + 1], AX_X, ALU.max, negate=True))
                        links.link(nc.vector.tensor_copy(rows[:, :, :, m_row], nm3))
                        nc.vector.tensor_tensor(rows[:, :, :, m_row + 1], nm3, rows[:, :, :, m_row], ALU.subtract)\
                            .then_inc(shift_ready, 1)
                    elif kind == "turn_q":
                        g, h = args
                        dve.wait_ge(work_full, filled(u, plan, step))
                        src = bank(plan, step, u)[:].bitcast(BF16)
                        cols = slice(g * TOK, (g + 1) * TOK)
                        if stack:
                            nc.vector.tensor_copy(QT[nxt][:, 0, cols], src[:, 0:TOK]).then_inc(work_dve, 1)
                        else:
                            nc.vector.tensor_copy(QT[nxt][:, 2 * h:2 * h + 2, cols],
                                                  src.rearrange("p (j t) -> p j t", j=2)).then_inc(work_dve, 1)
                    elif kind == "sums_out":
                        g, = args
                        m_last = sum(4 * GT * (x + 1) for x in range(g + 1))
                        dve.wait_ge(value_done, PROBS + NM * u + m_last)
                        nc.vector.tensor_copy(sumsT[:], sums_b[:]).then_inc(sums_taken, 1)
                    elif kind == "turn_out":
                        g, = args
                        dve.wait_ge(work_full, filled(u, plan, step))
                        src = bank(plan, step, u)[:].rearrange("p (n e) -> p n e", e=SLOT)
                        links.link(nc.vector.reciprocal(inv[:].unsqueeze(2), src[:, :, HD:HD + 1]))
                        dve.wait_ge(y_stored, 1 + 16 * (S.GB * u + g))
                        nc.vector.tensor_tensor(y[:].rearrange("p t h e -> p (t h) e"), src[:, :, 0:HD],
                                                inv[:].unsqueeze(2).broadcast_to([P, GT * 4, HD]), ALU.mult)\
                            .then_inc(work_dve, 1)
                    elif kind == "hidden":
                        n, = args
                        dve.wait_ge(work_full, filled(u, plan, step))
                        links.link(nc.vector.bn_stats(hstat[:], bank(plan, step, u)[:]))
                        apart(dve, tick)
                        links.link(nc.vector.bn_aggr(hmv[:], hstat[:]))
                        nc.vector.tensor_scalar(hve[:], hmv[:, 1:2], EPS_LN, None, ALU.add).then_inc(hvar, 1)
                    elif kind == "norm":
                        n, = args
                        hid = ("hidden", args)
                        dve.wait_ge(hrstd_ready, NE * c + n + 1)
                        if n >= 2 or u is not None:
                            dve.wait_ge(work_full, filled(u, plan, ("turn_hidden", (n - 2,))) if n >= 2 else wbase(u))
                        nc.vector.tensor_scalar(hn[n % 2][:], bank(plan, hid, u)[:], hmv[:, 0:1], hrstd[:, 0:1],
                                                ALU.subtract, ALU.mult).then_inc(work_dve, 1)
                    elif kind == "out":
                        n, = args
                        t, e = divmod(n, S.E0)
                        gate = keep["gate0"][:, bass.ds(GT * c + t, 1), e:e + 1].rearrange("p a b -> p (a b)")
                        src = bank(plan, step, u)[:, 0:C]
                        dve.wait_ge(work_full, filled(u, plan, step))
                        if e == 0:
                            nc.vector.tensor_scalar(acc[:, t], src, gate, None, ALU.mult).then_inc(work_dve, 1)
                        else:
                            dve.wait_ge(work_dve, freed(u, plan, ("out", (n - 1,))))
                            nc.vector.scalar_tensor_tensor(acc[:, t], src, gate, acc[:, t], ALU.mult, ALU.add)\
                                .then_inc(work_dve, 1)
                    elif kind == "out_stats":
                        t, = args
                        dve.wait_ge(work_dve, freed(u, plan, ("out", (t * S.E0 + S.E0 - 1,))))
                        links.link(nc.vector.bn_stats(ostat[:], acc[:, t]))
                        apart(dve, tick)
                        links.link(nc.vector.bn_aggr(omv[:], ostat[:]))
                        nc.vector.tensor_scalar(ove[:], omv[:, 1:2], EPS_LN, None, ALU.add).then_inc(ovar, 1)
                    elif kind == "out_norm":
                        t, = args
                        dve.wait_ge(orstd_ready, GT * c + t + 1)
                        dve.wait_ge(ff_stored, 1 + 16 * (GT * c + t))
                        nc.vector.tensor_scalar(fo[:], acc[:, t], omv[:, 0:1], orstd[:, 0:1], ALU.subtract, ALU.mult)\
                            .then_inc(fo_ready, 1)
                    elif kind == "gate":
                        e, = args
                        dve.wait_ge(tanh_done, NE * c + e + 1)
                        nc.vector.scalar_tensor_tensor(gh[e % 2][:], th[e % 2][:], 1.0, bank(plan, step, u)[:], ALU.add, ALU.mult)\
                            .then_inc(work_dve, 1)
                    elif kind == "up":
                        e, = args
                        dve.wait_ge(work_full, filled(u, plan, step))
                        dve.wait_ge(work_dve, freed(u, plan, ("gate", args)))
                        if e >= 2 or u is not None:
                            dve.wait_ge(work_full, filled(u, plan, ("down", (e - 2, 1))) if e >= 2 else wbase(u))
                        nc.vector.tensor_tensor(hT[e % 2][:], gh[e % 2][:], bank(plan, step, u)[:], ALU.mult)\
                            .then_inc(work_dve, 1)
                    elif kind == "down":
                        e, h = args
                        dve.wait_ge(work_full, filled(u, plan, step))
                        if e == 0:
                            dve.wait_ge(ff_stored, 1 + 16 * c)
                        else:
                            dve.wait_ge(work_dve, freed(u, plan, ("down", (e - 1, h))))
                        for n in range(2):
                            t = 2 * h + n
                            src = bank(plan, step, u)[:, n * C:(n + 1) * C]
                            g = 0.5 if e >= S.E1 else coef[:, bass.ds(GT * c + t, 1), e:e + 1].rearrange("p a b -> p (a b)")
                            if e == 0:
                                last = nc.vector.tensor_scalar(acc[:, t], src, g, None, ALU.mult)
                            else:
                                last = nc.vector.scalar_tensor_tensor(acc[:, t], src, g, acc[:, t], ALU.mult, ALU.add)
                            if n == 0:
                                last.then_inc(tick, 1)
                        last.then_inc(work_dve, 1)
                if plan is first:
                    assert links.steps == base_first, links.steps
                if plan is full:
                    assert links.steps == per_full, (links.steps, per_full)

            slots(dve, body)

        @block.tensor
        def _(pe):
            pe.sem_inc(value_done, PROBS)
            def body(plan, u, parity):
                c = (1 + u) if u is not None else 0
                nxt = 1 - parity
                ahead = c
                last = None
                for step in plan.pe:
                    kind, args = step
                    if kind == "score":
                        g, kt, j, m = args
                        q0 = max(0, kt - GT * g) * P
                        if m == 0:
                            pe.wait_ge(work_dve, emptied(u, "dve"))
                        pe.wait_ge(exp_done, NM * u + m + 1)
                        dst = score_b[m % SCORE_BANKS]
                        keys = KZ[parity][:, j, kt * P:(kt + 1) * P]
                        last = nc.tensor.matmul(dst[:, q0:TOK], keys,
                                                QT[parity][:, 0 if stack else j, g * TOK + q0:(g + 1) * TOK],
                                                start=True, stop=kt < GT * g)
                        if kt >= GT * g:
                            last = nc.tensor.matmul(dst[:, q0:q0 + P], keep["identb"][:], keep["mask_kq"][:],
                                                    start=False, stop=True)
                        last.then_inc(score_full, 1)
                    elif kind == "value":
                        g, kt, j, m = args
                        q0 = max(0, kt - GT * g) * P
                        if kt == 0 and j == 0:
                            pe.wait_ge(sums_taken, S.GB * u + g + 1)
                        pe.wait_ge(exp_done, SCORE_BANKS + NM * u + m + 1)
                        last = nc.tensor.matmul(sums_b[SLOT * j:SLOT * (j + 1), q0:TOK],
                                                V[parity][:, kt, SLOT * j:SLOT * (j + 1)],
                                                probs[m % PROBS][:, q0:TOK],
                                                start=kt == 0, stop=kt == GT * (g + 1) - 1)
                        last.then_inc(value_done, 1)
                    elif kind == "peak":
                        g, t, j, ch, k = args
                        w = TOK if ch < g else (t + 1) * P
                        if k == 0:
                            pe.wait_ge(pairs_in, 16 * PAIRS * (ahead + 1))
                        pe.wait_ge(peak_taken, NX * ahead + k + 1)
                        dst = max_b[k % MAX_BANKS]
                        qt = (g * GT + t) * P
                        last = nc.tensor.matmul(dst[:, 0:w], QT[nxt][:, 0 if stack else j, qt:qt + P],
                                                KZ[nxt][:, j, ch * TOK:ch * TOK + w], start=True, stop=ch < g)
                        if ch == g:
                            last = nc.tensor.matmul(dst[:, w - P:w], keep["identb"][:], keep["mask_qk"][:],
                                                    start=False, stop=True)
                        last.then_inc(peak_full, 1)
                    elif kind == "turn_q":
                        g, h = args
                        pe.wait_ge(shift_ready, S.GB * ahead + g + 1)
                        wait_work_free(pe, u, plan, step)
                        dst = bank(plan, step, u)[:].bitcast(BF16)
                        for jj in range(1 if stack else 2):
                            for t in range(GT):
                                rows = QA[:, g * GT + t, (2 * h + jj) * P:(2 * h + jj + 1) * P]
                                last = nc.tensor.transpose(dst[:, jj * TOK + t * P:jj * TOK + (t + 1) * P], rows,
                                                           keep["identb"][:])
                        last.then_inc(work_full, 1)
                    elif kind == "turn_out":
                        g, = args
                        pe.wait_ge(sums_taken, S.GB * u + g + 2)
                        wait_work_free(pe, u, plan, step)
                        for t in range(GT):
                            last = nc.tensor.transpose(bank(plan, step, u)[:, t * P:(t + 1) * P],
                                                       sumsT[:, t * P:(t + 1) * P], keep["ident"][:])
                        last.then_inc(work_full, 1)
                    elif kind == "hidden":
                        n, = args
                        t, e = divmod(n, S.E0)
                        if n == 0:
                            if u is None:
                                pe.wait_ge(w_in, 16 * WLOADS)
                            pe.wait_ge(group_in[nxt], 8 * u + 8 * parity + 16 if u is not None else 16)
                        wait_work_free(pe, u, plan, step)
                        tok = slice(t * P, (t + 1) * P)
                        for k in range(KC):
                            last = nc.tensor.matmul(bank(plan, step, u)[:], XT[nxt][:, k, tok], w1[:, k, e, :],
                                                    start=k == 0, stop=k == KC - 1)
                        last.then_inc(work_full, 1)
                    elif kind == "turn_hidden":
                        n, = args
                        pe.wait_ge(work_dve, freed(u, plan, ("hidden", args)))
                        wait_work_free(pe, u, plan, step)
                        for k in range(S.F0 // P):
                            last = nc.tensor.transpose(bank(plan, step, u)[:, k * P:(k + 1) * P],
                                                       hn[n % 2][:, k * P:(k + 1) * P], keep["ident"][:])
                        last.then_inc(work_full, 1)
                    elif kind == "out":
                        n, = args
                        e = n % S.E0
                        pe.wait_ge(work_act, freed(u, plan, ("turn_hidden", args), "act"))
                        wait_work_free(pe, u, plan, step)
                        for k in range(S.F0 // P):
                            last = nc.tensor.matmul(bank(plan, step, u)[:, 0:C], hT[n % 2][:, k], w2[:, e, k, :],
                                                    start=k == 0, stop=k == S.F0 // P - 1)
                        last.then_inc(work_full, 1)
                    elif kind in ("gate", "up"):
                        e, = args
                        w = wg if kind == "gate" else wu
                        if e == 0 and kind == "gate":
                            if u is None:
                                pe.wait_ge(w_in, 16 * WLOADS)
                            pe.wait_ge(group_in[nxt], 8 * u + 8 * parity + 16 if u is not None else 16)
                        wait_work_free(pe, u, plan, step)
                        cols = slice(e * P, (e + 1) * P)
                        for k in range(KC):
                            last = nc.tensor.matmul(bank(plan, step, u)[:], w[:, k, cols], XT[nxt][:, k],
                                                    start=k == 0, stop=k == KC - 1)
                        last.then_inc(work_full, 1)
                    elif kind == "down":
                        e, h = args
                        if h == 0:
                            pe.wait_ge(work_dve, freed(u, plan, ("up", (e,))))
                        wait_work_free(pe, u, plan, step)
                        for n in range(2):
                            t = 2 * h + n
                            tok = slice(t * P, (t + 1) * P)
                            last = nc.tensor.matmul(bank(plan, step, u)[:, n * C:(n + 1) * C], hT[e % 2][:, tok], wd[:, e, :],
                                                    start=True, stop=True)
                        last.then_inc(work_full, 1)
                pe.drain().then_inc(slot_done, 1)

            slots(pe, body)


def stage_layer0(nc, a, S, keep, d):
    stage_layer(nc, a, S, keep, d, 0)


def stage_layer1(nc, a, S, keep, d):
    stage_layer(nc, a, S, keep, d, 1)


def stage_mid(nc, a, S, keep, d):
    H, HD, KC, C, E = S.H, S.HD, S.KC, S.C, S.E1
    HT = GT * H
    NQ = 2 * C
    SCALE = HD ** -0.5
    with ExitStack() as ctx:
        pool = Pools(nc, ctx, "mid")
        sb, psum, sem = pool.sb, pool.psum, pool.sem
        wnat = sb("wnat", [P, (NQ + C) // P, C])
        wqk = sb("wqk", [P, KC, NQ])
        wk2r = sb("wk2r", [P, KC, C + E])
        wo = sb("wo", [P, KC, C])
        bias = sb("bias", [P, NQ + C])
        half = sb("half", [P, GT])
        yg = sb("yg", [P, GT, C])
        yT = sb("yT", [P, KC, GT, P])
        xg = sb("xg", [P, GT, C])
        fg = sb("fg", [P, GT, C])
        x1 = sb("x1", [P, GT, C])
        stat, mv, ve, rstd = sb("stat", [P, GT, 6]), sb("mv", [P, GT, 2]), sb("ve", [P, GT]), sb("rstd", [P, GT])
        xn = sb("xn", [P, GT, C])
        xnT = sb("xnT", [P, KC, GT, P])
        va = sb("va", [P, GT, H, SLOT])
        qk = sb("qk", [P, 2, GT, C])
        k2 = sb("k2", [P, GT, C])
        qal = sb("qal", [P, GT, C])
        kal = sb("kal", [P, GT, C])
        part = [sb(f"part{n}", [P, 2, HT, HD], BF16) for n in range(3)]
        QA = sb("QA", [P, HT, P], BF16)
        KA = sb("KA", [P, HT, P], BF16)
        QT = sb("QT", [P, H, TOK], BF16)
        KT = sb("KT", [P, H, TOK], BF16)
        rl = sb("rl", [P, S.TILES, E])
        big = [sb(f"big{n}", [P, S.TILES, E]) for n in range(4)]
        big.insert(1, rl)
        row = [sb(f"row{n}", [P, S.TILES]) for n in range(3)]
        pT = [psum(f"pT{t}") for t in range(GT)]
        pP = [psum(f"pP{t}") for t in range(GT)]

        w_in, loaded, seen, set_up = sem("w_in"), sem("loaded"), sem("seen"), sem("set_up")
        w_turned, w_taken = sem("w_turned"), sem("w_taken")
        yT_psum, yT_ready, wo_done = sem("yT_psum"), sem("yT_ready"), sem("wo_done")
        x1_ready, var_ready, rstd_ready = sem("x1_ready"), sem("var_ready"), sem("rstd_ready")
        xn_ready, xnT_psum, xnT_ready, va_ready = sem("xn_ready"), sem("xnT_psum"), sem("xnT_ready"), sem("va_ready")
        proj_done, qk_taken, k2_ready, kal_ready = sem("proj_done"), sem("qk_taken"), sem("k2_ready"), sem("kal_ready")
        qal_ready, parts_ready, qa_ready, ka_ready = sem("qal_ready"), sem("parts_ready"), sem("qa_ready"), sem("ka_ready")
        turned, q_taken, k_taken = sem("turned"), sem("q_taken"), sem("k_taken")
        chain, tick = sem("chain"), sem("tick")
        rows_stored, attn_stored, turned_stored = sem("rows_stored"), sem("attn_stored"), sem("turned_stored")
        gate_exp, logits = sem("gate_exp"), sem("logits")

        LOADS = S.HG + 2
        ROWS, ATTN, TURNED = 4, 3, 2 * S.HG
        NW = (NQ + C) // P

        block = ctx.enter_context(nc.Block())

        @block.sync
        def _(sp):
            xt = a["L0_attn_x"].rearrange("b t c -> (b t) c").rearrange("(n p) c -> p n c", p=P)

            def load(g):
                tiles = bass.ds(g * GT, GT)
                for hg in range(S.HG):
                    w = C // S.HG
                    sp.dma_start(yg[:, :, hg * w:(hg + 1) * w], d["y0"][hg][:, tiles, :]).then_inc(loaded, 16)
                sp.dma_start(xg[:], xt[:, tiles, :]).then_inc(loaded, 16)
                sp.dma_start(fg[:], d["ff0"][:, tiles, :]).then_inc(loaded, 16)

            sp.sem_inc(rows_stored, 1)
            sp.sem_inc(attn_stored, 1)
            sp.sem_inc(turned_stored, 1)
            load(0)
            load_experts1(sp, a, keep)

            def store_turned(it):
                tok = bass.ds(it * TOK, TOK)
                sp.wait_ge(q_taken, 1 + 8 * it + 8)
                apart(sp, tick)
                for hg in range(S.HG):
                    sp.dma_start(d["qT1"][hg][:, :, tok], QT[:, 4 * hg:4 * hg + 4, :]).then_inc(turned_stored, 16)
                sp.wait_ge(k_taken, 1 + 8 * it + 8)
                apart(sp, tick)
                for hg in range(S.HG):
                    sp.dma_start(d["kT1"][hg][:, :, tok], KT[:, 4 * hg:4 * hg + 4, :]).then_inc(turned_stored, 16)

            def group(it, first, last):
                tiles, tok = bass.ds(it * GT, GT), bass.ds(it * TOK, TOK)
                sp.wait_ge(seen, it + 1)
                apart(sp, tick)
                if not last:
                    load(it + 1)
                sp.dma_start(d["x1"][:, tiles, :], x1[:]).then_inc(rows_stored, 16)
                sp.wait_ge(xn_ready, it * GT + GT)
                apart(sp, tick)
                sp.dma_start(d["xn1"][0:S.TILES * P, :].rearrange("(n p) c -> p n c", p=P)[:, tiles, :], xn[:])\
                    .then_inc(rows_stored, 16)
                sp.wait_ge(va_ready, it + 1)
                apart(sp, tick)
                sp.dma_start(d["va1"][:, tiles, :], va[:].rearrange("p t h n -> p t (h n)")).then_inc(rows_stored, 16)
                sp.wait_ge(xnT_ready, it * GT + GT)
                apart(sp, tick)
                sp.dma_start(d["xnT1"].rearrange("k p t -> p k t")[:, :, tok], xnT[:].rearrange("p k t j -> p k (t j)"))\
                    .then_inc(rows_stored, 16)
                if not first:
                    store_turned(it - 1)
                sp.wait_ge(qal_ready, it + 1)
                apart(sp, tick)
                sp.dma_start(d["qal"][:, tiles, :], qal[:]).then_inc(attn_stored, 16)
                sp.wait_ge(kal_ready, it + 1)
                apart(sp, tick)
                sp.dma_start(d["kal"][:, tiles, :], kal[:]).then_inc(attn_stored, 16)
                sp.wait_ge(qa_ready, it + 1)
                apart(sp, tick)
                sp.dma_start(d["qa1"][:, tiles, :], QA[:].rearrange("p (t h) n -> p t (h n)", t=GT)).then_inc(attn_stored, 16)

            group(0, True, False)
            with sp.Fori(1, S.G - 1) as it:
                group(it, False, False)
            group(S.G - 1, False, True)
            store_turned(S.G - 1)
            sp.dma_start(d["xn1"][S.TILES * P:S.TILES * P + 1, :], xn[0:1, 0, :]).then_inc(rows_stored, 16)
            sp.wait_ge(rows_stored, 1 + 16 * (ROWS * S.G + 1))
            sp.wait_ge(attn_stored, 1 + 16 * ATTN * S.G)
            sp.wait_ge(turned_stored, 1 + 16 * TURNED * S.G)

        @block.gpsimd
        def _(pool_e):
            def load(out, src):
                pool_e.dma_start(out, src).then_inc(w_in, 16)

            load(wnat[:, 0:NQ // P, :], a["L1_attn_w_attn"].rearrange("(n p) c -> p n c", p=P))
            load(wnat[:, NQ // P:, :], a["L1_attn_w_k2"].rearrange("(n p) c -> p n c", p=P))
            load(wk2r[:, :, C:], a["L1_ffn_router"].rearrange("(k p) e -> p k e", p=P))
            load(wo[:], a["L0_attn_wo"].rearrange("(k p) c -> p k c", p=P))
            load(bias[:, 0:NQ], a["L1_attn_b_attn"].partition_broadcast(P))
            load(bias[:, NQ:], a["L1_attn_b_k2"].partition_broadcast(P))
            nc.gpsimd.memset(half[:], -0.5).then_inc(set_up, 1)
            nc.gpsimd.memset(va[:], 0.0).then_inc(set_up, 1)
            nc.gpsimd.memset(KA[:], 0.0).then_inc(set_up, 1)
            pool_e.wait_ge(set_up, 4)
            nc.gpsimd.memset(va[:, :, :, HD:HD + 1], 1.0).then_inc(set_up, 1)
            nc.gpsimd.memset(KA[:, :, 6 * HD:6 * HD + 2], 1.0).then_inc(set_up, 1)
            with pool_e.Fori(0, S.G) as it:
                pool_e.wait_ge(var_ready, it + 1)
                nc.gpsimd.tensor_tensor(rstd[:], ve[:], half[:], ALU.pow).then_inc(rstd_ready, 1)

        STEPS = GT * 2 + 8

        @block.vector
        def _(dve):
            dve.sem_inc(qk_taken, 1)
            dve.sem_inc(k_taken, 1)
            nc.vector.memset(QA[:], 0.0).then_inc(set_up, 1)
            dve.wait_ge(w_in, 16 * 6)
            dve.wait_ge(set_up, 6)

            def take_k(it):
                dve.wait_ge(turned_stored, 1 + 16 * TURNED * it)
                for n in range(8):
                    dve.wait_ge(turned, 16 * it + 2 * n + 2)
                    nc.vector.tensor_copy(KT[:, 2 * n:2 * n + 2, :],
                                          pT[(2 * n + 1) % 4][:].bitcast(BF16).rearrange("p (g j) -> p g j", g=2))\
                        .then_inc(k_taken, 1)

            def group(it, first):
                c = Chain(dve, chain, it * STEPS)
                dve.wait_ge(loaded, 16 * LOADS * (it + 1))
                dve.wait_ge(rows_stored, 1 + 16 * ROWS * it)
                c.link(nc.vector.tensor_tensor(x1[:], xg[:], fg[:], ALU.add))
                for t in range(GT):
                    dve.wait_ge(wo_done, GT * it + t + 1)
                    nc.vector.tensor_tensor(x1[:, t], pP[t][:, 0:C], x1[:, t], ALU.add).then_inc(x1_ready, 1)
                dve.wait_ge(x1_ready, GT * it + GT)
                dve.sem_inc(seen, 1)
                for t in range(GT):
                    c.step(nc.vector.bn_stats(stat[:, t, :], x1[:, t]))
                c.settle()
                apart(dve, tick)
                for t in range(GT):
                    c.step(nc.vector.bn_aggr(mv[:, t, :], stat[:, t, :]))
                c.settle()
                nc.vector.tensor_scalar(ve[:], mv[:, :, 1], EPS_LN, None, ALU.add).then_inc(var_ready, 1)
                dve.wait_ge(rstd_ready, it + 1)
                for t in range(GT):
                    nc.vector.tensor_scalar(xn[:, t, :], x1[:, t], mv[:, t, 0:1], rstd[:, t:t + 1],
                                            ALU.subtract, ALU.mult).then_inc(xn_ready, 1)
                if not first:
                    take_k(it - 1)
                dve.wait_ge(attn_stored, 1 + 16 * ATTN * it)
                for t in range(GT):
                    dve.wait_ge(proj_done, GT * it + t + 1)
                    c_qk = nc.vector.tensor_tensor(qk[:, :, t, :], pP[t][:].rearrange("p (s n) -> p s n", s=2),
                                                   bias[:, 0:NQ].rearrange("p (s n) -> p s n", s=2), ALU.add)
                    c_qk.then_inc(tick, 1)
                    nc.vector.tensor_tensor(k2[:, t, :], pT[t][:, 0:C], bias[:, NQ:], ALU.add).then_inc(k2_ready, 1)
                    nc.vector.tensor_copy(rl[:, bass.ds(it * GT + t, 1), :].rearrange("p a c -> p (a c)"),
                                          pT[t][:, C:C + E]).then_inc(qk_taken, 1)
                dve.wait_ge(qk_taken, 1 + GT * it + GT)
                c.link(nc.vector.tensor_scalar(qk[:, 0], qk[:, 0], SCALE, None, ALU.mult))
                nc.vector.scalar_tensor_tensor(qal[:], qk[:, 0], 0.02, qk[:, 0], ALU.mult, ALU.min).then_inc(qal_ready, 1)
                q = qk[:].rearrange("p s t (h e) -> p s (t h) e", e=HD)
                c.link(nc.vector.tensor_copy(part[0][:], q))
                dve.wait_ge(qal_ready, it + 1)
                c.link(nc.vector.tensor_tensor(q, q, part[0][:], ALU.subtract))
                c.link(nc.vector.tensor_copy(part[1][:], q))
                c.link(nc.vector.tensor_tensor(q, q, part[1][:], ALU.subtract))
                nc.vector.tensor_copy(part[2][:], q).then_inc(parts_ready, 1)
                dve.wait_ge(parts_ready, it + 1)
                if not first:
                    dve.wait_ge(turned, 16 * it)
                kslot = KA[:, :, 0:6 * HD].rearrange("p n (s e) -> p n s e", e=HD)
                c.step(nc.vector.tensor_copy(kslot[:, :, 0:6:3, :], part[0][:, 1].unsqueeze(2).broadcast_to([P, HT, 2, HD])))
                c.step(nc.vector.tensor_copy(kslot[:, :, 1:5:3, :], part[1][:, 1].unsqueeze(2).broadcast_to([P, HT, 2, HD])))
                nc.vector.tensor_copy(kslot[:, :, 5, :], part[0][:, 1]).then_inc(tick, 1)
                c.settle()
                nc.vector.tensor_copy(kslot[:, :, 2, :], part[2][:, 1]).then_inc(ka_ready, 1)
                assert c.steps == STEPS, c.steps

            group(0, True)
            with dve.Fori(1, S.G) as it:
                group(it, False)
            take_k(S.G - 1)
            c = Chain(dve, chain, S.G * STEPS)
            top_two(nc, dve, c, S.TILES, E, big, row, gate_exp, logits, keep["gate1"], False)

        @block.scalar
        def _(act):
            act.sem_inc(q_taken, 1)
            for n in range(NW):
                act.wait_ge(w_turned, n + 1)
                dst = wqk[:, :, n * P:(n + 1) * P] if n < NQ // P else wk2r[:, :, (n - NQ // P) * P:(n - NQ // P + 1) * P]
                nc.scalar.copy(dst, pT[n % GT][:, 0:C].rearrange("p (k j) -> p k j", k=KC)).then_inc(w_taken, 1)
            act.wait_ge(set_up, 6)

            def take_q(it):
                act.wait_ge(turned_stored, 1 + 16 * TURNED * it)
                for n in range(8):
                    act.wait_ge(turned, 16 * it + 2 * n + 1)
                    nc.scalar.copy(QT[:, 2 * n:2 * n + 2, :],
                                   pT[(2 * n) % 4][:].bitcast(BF16).rearrange("p (g j) -> p g j", g=2)).then_inc(q_taken, 1)

            def take_y(it):
                for t in range(GT):
                    act.wait_ge(yT_psum, GT * it + t + 1)
                    nc.scalar.copy(yT[:, :, t, :], pT[t][:, 0:C].rearrange("p (k j) -> p k j", k=KC)).then_inc(yT_ready, 1)

            def group(it, first, last):
                if not first:
                    take_q(it - 1)
                act.wait_ge(rows_stored, 1 + 16 * ROWS * it)
                for t in range(GT):
                    act.wait_ge(xnT_psum, GT * it + t + 1)
                    nc.scalar.copy(xnT[:, :, t, :], pT[t][:, 0:C].rearrange("p (k j) -> p k j", k=KC)).then_inc(xnT_ready, 1)
                nc.scalar.copy(va[:, :, :, 0:HD], xn[:].rearrange("p t (h e) -> p t h e", e=HD)).then_inc(va_ready, 1)
                act.wait_ge(k2_ready, GT * it + GT)
                act.wait_ge(attn_stored, 1 + 16 * ATTN * it)
                nc.scalar.activation(kal[:], k2[:], ACT.Sigmoid, scale=0.02 * SCALE).then_inc(kal_ready, 1)
                if not last:
                    take_y(it + 1)
                act.wait_ge(parts_ready, it + 1)
                if not first:
                    act.wait_ge(turned, 16 * it)
                qslot = QA[:, :, 0:6 * HD].rearrange("p n (s e) -> p n s e", e=HD)
                for lo, hi, n in ((0, 3, 0), (3, 5, 1)):
                    nc.scalar.copy(qslot[:, :, lo:hi, :], part[n][:, 0].unsqueeze(2).broadcast_to([P, HT, hi - lo, HD]))\
                        .then_inc(tick, 1)
                nc.scalar.copy(qslot[:, :, 5, :], part[2][:, 0]).then_inc(qa_ready, 1)

            take_y(0)
            group(0, True, False)
            with act.Fori(1, S.G - 1) as it:
                group(it, False, False)
            group(S.G - 1, False, True)
            take_q(S.G - 1)
            act.wait_ge(logits, 1)
            nc.scalar.activation(big[3][:], big[2][:], ACT.Exp).then_inc(gate_exp, 1)

        @block.tensor
        def _(pe):
            pe.wait_ge(w_in, 16 * 6)
            for n in range(NW):
                if n >= GT:
                    pe.wait_ge(w_taken, n - GT + 1)
                for k in range(KC):
                    last = nc.tensor.transpose(pT[n % GT][:, k * P:(k + 1) * P], wnat[:, n, k * P:(k + 1) * P],
                                               keep["ident"][:])
                last.then_inc(w_turned, 1)
            pe.wait_ge(w_taken, NW)

            def mix(it):
                pe.wait_ge(loaded, 16 * LOADS * (it + 1))
                pe.wait_ge(qk_taken, 1 + GT * it)
                for t in range(GT):
                    for k in range(KC):
                        last = nc.tensor.transpose(pT[t][:, k * P:(k + 1) * P], yg[:, t, k * P:(k + 1) * P], keep["ident"][:])
                    last.then_inc(yT_psum, 1)
                for t in range(GT):
                    pe.wait_ge(yT_ready, GT * it + t + 1)
                    for k in range(KC):
                        last = nc.tensor.matmul(pP[t][:, 0:C], yT[:, k, t, :], wo[:, k, :], start=(k == 0), stop=(k == KC - 1))
                    last.then_inc(wo_done, 1)

            def turn(it):
                pe.wait_ge(qa_ready, it + 1)
                pe.wait_ge(ka_ready, it + 1)
                for n in range(8):
                    for m, src in enumerate((QA, KA)):
                        if n >= 2:
                            pe.wait_ge(q_taken if m == 0 else k_taken, 1 + 8 * it + n - 1)
                        bank = pT[(2 * n + m) % 4][:].bitcast(BF16)
                        for j in range(2):
                            for t in range(GT):
                                last = nc.tensor.transpose(bank[:, j * TOK + t * P:j * TOK + (t + 1) * P],
                                                           src[:, t * H + 2 * n + j, :], keep["identb"][:])
                        last.then_inc(turned, 1)

            def project(it):
                pe.wait_ge(q_taken, 1 + 8 * it)
                pe.wait_ge(k_taken, 1 + 8 * it)
                for t in range(GT):
                    pe.wait_ge(xn_ready, GT * it + t + 1)
                    for k in range(KC):
                        last = nc.tensor.transpose(pT[t][:, k * P:(k + 1) * P], xn[:, t, k * P:(k + 1) * P], keep["ident"][:])
                    last.then_inc(xnT_psum, 1)
                for t in range(GT):
                    pe.wait_ge(xnT_ready, GT * it + t + 1)
                    for k in range(KC):
                        nc.tensor.matmul(pP[t][:], xnT[:, k, t, :], wqk[:, k, :], start=(k == 0), stop=(k == KC - 1))
                    for k in range(KC):
                        last = nc.tensor.matmul(pT[t][:, 0:C + E], xnT[:, k, t, :], wk2r[:, k, :],
                                                start=(k == 0), stop=(k == KC - 1))
                    last.then_inc(proj_done, 1)

            mix(0)
            project(0)
            with pe.Fori(1, S.G) as it:
                mix(it)
                turn(it - 1)
                project(it)
            turn(S.G - 1)


def stage_final(nc, a, S, keep, d):
    H, HD, KC, C = S.H, S.HD, S.KC, S.C
    HH = P // HD
    NB = H // 4
    UNROLL = 4
    LOADS = 6
    LAST = S.TILES - 1
    with ExitStack() as ctx:
        pool = Pools(nc, ctx, "final")
        sb, psum, sem = pool.sb, pool.psum, pool.sem

        def two(name, shape):
            return [sb(f"{name}{n}", shape) for n in range(2)]

        def four(name):
            return [sb(f"{name}{n}", [P, C]) for n in range(UNROLL)]

        wnat = sb("wnat", [P, KC, C])
        wT = sb("wT", [P, KC, C])
        bias2 = sb("bias2", [P, C])
        heads = sb("heads", [P, KC, HH])
        causal = sb("causal", [P, P])
        carry = sb("carry", [P, S.TILES])
        state = sb("state", [P, KC, HH, HD])
        grown = sb("grown", [P, KC, HH, HD])
        q_in, k_in, y_in, xs_in, x_in, f_in = (four("q_in"), four("k_in"), four("y_in"), four("xs_in"),
                                               four("x_in"), four("f_in"))
        qT, kT = two("qT", [P, KC, P]), two("kT", [P, KC, P])
        qz = two("qz", [P, KC, HH, P])
        at = two("at", [P, H, P])
        e = two("e", [P, H // 2, 2, 2 * HD])
        yT = two("yT", [P, KC, P])
        rest = two("rest", [P, C])
        o = two("o", [P, C])
        turn_b, out_b, state_b, proj_b = psum("turn_b"), psum("out_b"), psum("state_b"), psum("proj_b")
        prod_b = [psum(f"prod_b{n}") for n in range(NB)]

        w_in, set_up, bias_ready = sem("w_in"), sem("set_up"), sem("bias_ready")
        w_turned, w_taken, tick = sem("w_turned"), sem("w_taken"), sem("tick")
        loaded = [sem(f"loaded{n}") for n in range(UNROLL)]
        stored = [sem(f"stored{n}") for n in range(2)]
        turned, turned_taken, qz_ready = sem("turned"), sem("turned_taken"), sem("qz_ready")
        prod_full, prod_taken, e_ready = sem("prod_full"), sem("prod_taken"), sem("e_ready")
        out_full = sem("out_full")
        state_full, grown_ready, state_ready = sem("state_full"), sem("grown_ready"), sem("state_ready")
        yT_ready, proj_full, o_ready = sem("yT_ready"), sem("proj_full"), sem("o_ready")
        sum_ready, rest_ready = sem("sum_ready"), sem("rest_ready")


        def tile(i, k):
            return UNROLL * i + k, k % 2, (UNROLL // 2) * i + k // 2

        block = ctx.enter_context(nc.Block())

        @block.sync
        def _(sp):
            out_rows = d["out"].rearrange("b t c -> (b t) c")

            def load(i, k):
                n, m = UNROLL * i + k, k % UNROLL
                one = bass.ds(n, 1)
                for buf, name in ((q_in, "qal"), (k_in, "kal"), (x_in, "x1"), (f_in, "ff1")):
                    sp.dma_start(buf[m][:], d[name][:, one, :].rearrange("p a c -> p (a c)")).then_inc(loaded[m], 16)
                sp.dma_start(y_in[m][:].rearrange("p (g c) -> p g c", g=S.HG),
                             d["y1"][:, :, one, :].rearrange("g p a c -> p g (a c)")).then_inc(loaded[m], 16)
                sp.dma_start(xs_in[m][:], d["xn1"][bass.ds(n * P + 1, P), :]).then_inc(loaded[m], 16)

            def refill(i, k):
                n, _, _ = tile(i, k)
                sp.wait_ge(rest_ready, n + 1)
                apart(sp, tick)
                sp.wait_ge(out_full, 2 + n + 1)
                apart(sp, tick)
                load(i, k + UNROLL)

            def store(i, k):
                n, par, _ = tile(i, k)
                sp.wait_ge(o_ready, 2 + n + 1)
                apart(sp, tick)
                sp.dma_start(out_rows[bass.ds(n * P, P), :], o[par][:]).then_inc(stored[par], 16)

            for par in range(2):
                sp.sem_inc(stored[par], 1)
            for k in range(UNROLL):
                load(0, k)
            with sp.Fori(0, S.TILES // UNROLL - 1) as i:
                for k in range(UNROLL):
                    refill(i, k)
                    store(i, k)
            for k in range(S.TILES - UNROLL, S.TILES):
                store(0, k)
            for par in range(2):
                sp.wait_ge(stored[par], 1 + 16 * (S.TILES // 2))

        @block.gpsimd
        def _(pool_e):
            pool_e.dma_start(wnat[:], a["L1_attn_w_proj"].rearrange("(n p) c -> p n c", p=P)).then_inc(w_in, 16)
            pool_e.dma_start(bias2[:], a["L1_attn_b_proj"].partition_broadcast(P)).then_inc(w_in, 16)
            nc.gpsimd.memset(causal[:], 1.0).then_inc(set_up, 1)
            nc.gpsimd.memset(heads[:], 1.0).then_inc(set_up, 1)
            nc.gpsimd.memset(carry[:], 1.0).then_inc(set_up, 1)
            nc.gpsimd.memset(state[:], 0.0).then_inc(set_up, 1)
            for par in range(2):
                nc.gpsimd.memset(e[par][:], 0.0).then_inc(set_up, 1)
            pool_e.wait_ge(set_up, 6)
            nc.gpsimd.affine_select(out=causal[:], in_=causal[:], compare_op=ALU.is_gt, fill=0.0, base=0,
                                    pattern=[[1, P]], channel_multiplier=-1).then_inc(set_up, 1)
            nc.gpsimd.affine_select(out=heads[:], in_=heads[:], compare_op=ALU.is_ge, fill=0.0, base=0,
                                    pattern=[[0, KC], [-HD, HH]], channel_multiplier=1).then_inc(set_up, 1)
            pool_e.wait_ge(set_up, 8)
            nc.gpsimd.affine_select(out=heads[:], in_=heads[:], compare_op=ALU.is_ge, fill=0.0, base=HD - 1,
                                    pattern=[[0, KC], [HD, HH]], channel_multiplier=-1).then_inc(set_up, 1)
            for b in range(S.B):
                end = (b + 1) * S.TB - 1
                nc.gpsimd.memset(carry[:, end:end + 1], 0.0).then_inc(set_up, 1)
            pool_e.wait_ge(w_in, 32)
            nc.gpsimd.tensor_tensor(bias2[:], bias2[:], bias2[:], ALU.add).then_inc(bias_ready, 1)
            pool_e.wait_ge(bias_ready, 1)
            pool_e.wait_ge(set_up, 9 + S.B)

            with pool_e.Fori(0, S.TILES // UNROLL) as i:
                for k in range(UNROLL):
                    n, par, _ = tile(i, k)
                    pool_e.wait_ge(turned_taken, 2 + 2 * n + 2)
                    pool_e.wait_ge(prod_full, NB * n + NB)
                    for f in range(KC):
                        nc.gpsimd.tensor_tensor(qz[par][:, f], qT[par][:, f].unsqueeze(1).broadcast_to([P, HH, P]),
                                                heads[:, f].unsqueeze(2).broadcast_to([P, HH, P]), ALU.mult)\
                            .then_inc(qz_ready, 1)
                    pool_e.wait_ge(loaded[k], 16 * LOADS * (i + 1))
                    nc.gpsimd.tensor_tensor(x_in[k][:], x_in[k][:], f_in[k][:], ALU.add).then_inc(sum_ready, 1)
                    pool_e.wait_ge(sum_ready, n + 1)
                    pool_e.wait_ge(o_ready, n + 1)
                    nc.gpsimd.tensor_tensor(rest[par][:], x_in[k][:], bias2[:], ALU.add).then_inc(rest_ready, 1)

        @block.vector
        def _(dve):
            dve.sem_inc(prod_taken, NB)
            dve.sem_inc(grown_ready, 1)
            dve.sem_inc(state_ready, 1)
            dve.sem_inc(o_ready, 2)
            dve.wait_ge(set_up, 9 + S.B)

            def errors(i, k):
                n, par, _ = tile(i, k)
                m = k % UNROLL
                dve.wait_ge(loaded[m], 16 * LOADS * (i + k // UNROLL + 1))
                dve.wait_ge(out_full, n + 1)
                for odd in range(2):
                    xs, y = (rows[m][:].rearrange("p (h two c) -> p h two c", two=2, c=HD)[:, :, odd, :]
                             for rows in (xs_in, y_in))
                    nc.vector.tensor_tensor(e[par][:, :, odd, odd * HD:(odd + 1) * HD], xs, y, ALU.subtract)\
                        .then_inc(e_ready, 1)

            def mask(i, k):
                n, par, _ = tile(i, k)
                dve.wait_ge(out_full, n + 1)
                for b in range(NB):
                    dve.wait_ge(prod_full, 2 * NB + NB * n + b + 1)
                    nc.vector.tensor_tensor(at[par][:, 4 * b:4 * b + 4, :], prod_b[b][:].rearrange("p (h t) -> p h t", h=4),
                                            causal[:].unsqueeze(1).broadcast_to([P, 4, P]), ALU.mult)\
                        .then_inc(prod_taken, 1)

            def grow(i, k):
                n, par, _ = tile(i, k)
                dve.wait_ge(state_full, n + 1)
                dve.wait_ge(state_ready, 1 + n)
                nc.vector.tensor_tensor(grown[:].rearrange("p f h c -> p (f h c)"), state_b[:, 0:C],
                                        state[:].rearrange("p f h c -> p (f h c)"), ALU.add).then_inc(grown_ready, 1)
                dve.wait_ge(grown_ready, 1 + n + 1)
                dve.wait_ge(out_full, 2 + n + 1)
                nc.vector.scalar_tensor_tensor(state[:].rearrange("p f h c -> p (f h) c"),
                                               grown[:].rearrange("p f h c -> p (f h) c"), carry[:, bass.ds(n, 1)],
                                               heads[:].rearrange("p f h -> p (f h)").unsqueeze(2)
                                               .broadcast_to([P, H, HD]),
                                               ALU.mult, ALU.mult).then_inc(state_ready, 1)

            def finish(i, k):
                n, par, before = tile(i, k)
                dve.wait_ge(proj_full, 2 + n + 1)
                dve.wait_ge(rest_ready, n + 1)
                dve.wait_ge(stored[par], 1 + 16 * before)
                nc.vector.tensor_tensor(o[par][:], proj_b[:, 0:C], rest[par][:], ALU.add).then_inc(o_ready, 1)

            def step(i, k):
                errors(i, k + 1)
                grow(i, k)
                mask(i, k + 1)
                finish(i, k - 1)

            errors(0, 0)
            mask(0, 0)
            errors(0, 1)
            grow(0, 0)
            mask(0, 1)
            with dve.Fori(0, (S.TILES - UNROLL) // UNROLL) as i:
                for k in range(1, UNROLL + 1):
                    step(i, k)
            for n in range(S.TILES - UNROLL + 1, LAST):
                step(0, n)
            finish(0, LAST - 1)
            finish(0, LAST)

        @block.scalar
        def _(act):
            act.sem_inc(turned_taken, 2)
            act.sem_inc(yT_ready, 1)
            act.wait_ge(w_turned, 1)
            nc.scalar.copy(wT[:], prod_b[0][:].rearrange("p (k n) -> p k n", k=KC)).then_inc(w_taken, 1)

            def turn(i, k):
                n, par, _ = tile(i, k)
                act.wait_ge(turned, n + 1)
                act.wait_ge(out_full, n + 1)
                nc.scalar.copy(qT[par][:], turn_b[:, 0:C].rearrange("p (f t) -> p f t", f=KC)).then_inc(turned_taken, 1)
                nc.scalar.copy(kT[par][:], turn_b[:, C:2 * C].rearrange("p (f t) -> p f t", f=KC)).then_inc(turned_taken, 1)

            def take_y(i, k):
                n, par, _ = tile(i, k)
                act.wait_ge(out_full, 2 + n + 1)
                act.wait_ge(proj_full, n + 1)
                nc.scalar.copy(yT[par][:], out_b[:, 0:C].rearrange("p (f t) -> p f t", f=KC)).then_inc(yT_ready, 1)

            turn(0, 0)
            turn(0, 1)
            take_y(0, 0)
            turn(0, 2)
            with act.Fori(0, (S.TILES - UNROLL) // UNROLL) as i:
                for k in range(1, UNROLL + 1):
                    take_y(i, k)
                    turn(i, k + 2)
            take_y(0, LAST - 2)
            turn(0, LAST)
            take_y(0, LAST - 1)
            take_y(0, LAST)

        @block.tensor
        def _(pe):
            pe.sem_inc(out_full, 2)
            pe.sem_inc(prod_full, 2 * NB)
            pe.sem_inc(proj_full, 2)
            pe.wait_ge(w_in, 32)
            for k in range(KC):
                for m in range(KC):
                    last = nc.tensor.transpose(prod_b[0][:, k * C + m * P:k * C + (m + 1) * P],
                                               wnat[:, m, k * P:(k + 1) * P], keep["ident"][:])
            last.then_inc(w_turned, 1)
            pe.wait_ge(w_taken, 1)

            def turn(i, k):
                n, par, _ = tile(i, k)
                m = k % UNROLL
                pe.wait_ge(loaded[m], 16 * LOADS * (i + k // UNROLL + 1))
                pe.wait_ge(turned_taken, 2 + 2 * n)
                for s, rows in enumerate((q_in[m], k_in[m])):
                    for f in range(KC):
                        last = nc.tensor.transpose(turn_b[:, s * C + f * P:s * C + (f + 1) * P],
                                                   rows[:, f * P:(f + 1) * P], keep["ident"][:])
                last.then_inc(turned, 1)

            def products(i, k):
                n, par, _ = tile(i, k)
                for b in range(NB):
                    f, h = divmod(4 * b, HH)
                    if h == 0:
                        pe.wait_ge(qz_ready, 2 * n + f + 1)
                    pe.wait_ge(prod_taken, NB * n + b + 1)
                    nc.tensor.matmul(prod_b[b][:], kT[par][:, f], qz[par][:, f, h:h + 4, :],
                                     start=True, stop=True).then_inc(prod_full, 1)

            def values(i, k):
                n, par, _ = tile(i, k)
                m = k % UNROLL
                pe.wait_ge(e_ready, 2 * n + 2)
                pe.wait_ge(grown_ready, 1 + n)
                for f in range(KC):
                    rows = e[par][:, f * HH // 2:(f + 1) * HH // 2].rearrange("p h two c -> p h (two c)")
                    rows = rows.rearrange("p h (a c) -> p h a c", c=HD)[:, :, 0:4:3, :]
                    last = nc.tensor.matmul(state_b[:, f * P:(f + 1) * P], k_in[m][:, f * P:(f + 1) * P], rows,
                                            start=True, stop=True)
                last.then_inc(state_full, 1)
                pe.wait_ge(yT_ready, 1 + n)
                pe.wait_ge(state_ready, 1 + n)
                for f in range(KC):
                    cols = slice(f * P, (f + 1) * P)
                    nc.tensor.matmul(out_b[:, cols], y_in[m][:, cols], keep["ident"][:], start=True, stop=False)
                    nc.tensor.matmul(out_b[:, cols], state[:, f], qT[par][:, f], start=False, stop=False)
                    if f == 0:
                        pe.wait_ge(prod_taken, NB + NB * n + NB)
                    for odd in range(2):
                        for j in range(HH // 2):
                            h = f * HH + 2 * j + odd
                            last = nc.tensor.matmul(out_b[2 * HD * j:2 * HD * (j + 1), cols],
                                                    e[par][:, h // 2, odd, :], at[par][:, h, :],
                                                    start=False, stop=odd == 1)
                last.then_inc(out_full, 1)

            def project(i, k):
                n, par, _ = tile(i, k)
                pe.wait_ge(yT_ready, 1 + n + 1)
                pe.wait_ge(o_ready, 2 + n)
                for f in range(KC):
                    last = nc.tensor.matmul(proj_b[:, 0:C], yT[par][:, f], wT[:, f], start=(f == 0), stop=(f == KC - 1))
                last.then_inc(proj_full, 1)

            turn(0, 0)
            turn(0, 1)
            products(0, 0)
            values(0, 0)
            turn(0, 2)
            products(0, 1)
            with pe.Fori(0, (S.TILES - UNROLL) // UNROLL) as i:
                for k in range(1, UNROLL + 1):
                    values(i, k)
                    project(i, k - 1)
                    turn(i, k + 2)
                    products(i, k + 1)
            for n in range(LAST - 2, LAST + 1):
                values(0, n)
                project(0, n - 1)
                if n + 2 <= LAST:
                    turn(0, n + 2)
                if n + 1 <= LAST:
                    products(0, n + 1)
            project(0, LAST)


STAGES = [[stage_prep0, stage_layer0], [stage_mid, stage_layer1], [stage_final]]


def build(nc, a, out):
    S = Shapes(a)
    nc.disable_value_cache = True
    HG, NT, TK = S.HG, S.TILES, S.TILES * P
    d = {
        "xnT0": scratch(nc, "xnT0", (S.KC, P, TK), F32),
        "va0": scratch(nc, "va0", (P, NT, S.H * SLOT), F32),
        "qa0": scratch(nc, "qa0", (P, NT, S.H * SLOT), BF16),
        "qT0": scratch(nc, "qT0", (HG, P, TK), BF16),
        "kT0": scratch(nc, "kT0", (HG, P, TK), BF16),
        "y0": scratch(nc, "y0", (HG, P, NT, 4 * S.HD), F32),
        "ff0": scratch(nc, "ff0", (P, NT, S.C), F32),
        "x1": scratch(nc, "x1", (P, NT, S.C), F32),
        "xnT1": scratch(nc, "xnT1", (S.KC, P, TK), F32),
        "va1": scratch(nc, "va1", (P, NT, S.H * SLOT), F32),
        "qa1": scratch(nc, "qa1", (P, NT, S.H * P), BF16),
        "qT1": scratch(nc, "qT1", (HG, P, 4, TK), BF16),
        "kT1": scratch(nc, "kT1", (HG, P, 4, TK), BF16),
        "y1": scratch(nc, "y1", (HG, P, NT, 4 * S.HD), F32),
        "ff1": scratch(nc, "ff1", (P, NT, S.C), F32),
        "qal": scratch(nc, "qal", (P, NT, S.C), F32),
        "kal": scratch(nc, "kal", (P, NT, S.C), F32),
        "xn1": scratch(nc, "xn1", (TK + 1, S.C), F32),
    }
    with ExitStack() as ctx:
        def sb(name, shape, dt=F32):
            return ctx.enter_context(nc.sbuf_tensor(name, shape, dt))
        keep = {
            "ident": sb("ident", [P, P]), "identb": sb("identb", [P, P], BF16),
            "mask_qk": sb("mask_qk", [P, P], BF16), "mask_kq": sb("mask_kq", [P, P], BF16),
            "gate0": sb("gate0", [P, NT, S.E0]), "gate1": sb("gate1", [P, NT, S.E1]),
        }
        d["out"] = out
        for layer, stages in enumerate(STAGES):
            with ExitStack() as weights_ctx:
                def weights(name, shape):
                    keep[name] = weights_ctx.enter_context(nc.sbuf_tensor(name, shape, F32))

                if layer == 0:
                    weights("w1", [P, S.KC, S.E0, S.F0])
                    weights("w2", [P, S.E0, S.F0 // P, S.C])
                    weights("ln", [P, 2, S.E0, S.F0 // P])
                    weights("ong", [P, 2, S.C])
                elif layer == 1:
                    weights("wg", [P, S.KC, (S.E1 + S.KC) * P])
                    weights("wu", [P, S.KC, (S.E1 + S.KC) * P])
                    weights("wd", [P, S.E1 + S.KC, S.C])
                keep[f"w_in{layer}"] = weights_ctx.enter_context(nc.semaphore(f"w_in{layer}"))
                for stage in stages:
                    stage(nc, a, S, keep, d)


def kernel(**inputs):
    import numpy as _np
    import concourse.bacc as _bacc
    from concourse import mybir as _mybir
    from concourse.bass_utils import run_bass_kernel_spmd as _run

    nc = _bacc.Bacc("TRN2", target_bir_lowering=False, num_devices=1)
    arrays, args = {}, {}
    for name, value in inputs.items():
        v = _np.ascontiguousarray(value)
        arrays[f"in_{name}"] = v
        args[name] = nc.dram_tensor(f"in_{name}", v.shape, _mybir.dt.from_np(v.dtype), kind="ExternalInput").ap()
    shape = inputs["L0_attn_x"].shape
    out = nc.dram_tensor("out_0", shape, F32, kind="ExternalOutput").ap()
    build(nc, args, out)
    r = _run(nc, [arrays], core_ids=[0])
    return r.results[0]["out_0"]
```
